# Optimizing a Trainium2 kernel written in Bass

```python
import numpy as np
import jax
import jax.numpy as jnp

def _softmax(x, axis=-1):
    return jax.nn.softmax(x, axis=axis)

def _gelu(x):
    return jax.nn.gelu(x, approximate=True)

def _silu(x):
    return jax.nn.silu(x)

def _sigmoid(x):
    return jax.nn.sigmoid(x)

def _layernorm(x, axis=-1, eps=1e-05):
    m = jnp.mean(x, axis=axis, keepdims=True)
    v = jnp.var(x, axis=axis, keepdims=True)
    return (x - m) / jnp.sqrt(v + eps)

def _scatter_add(tgt, idx, src, axis=0):
    return tgt.at[idx].add(src)

def _segment_sum(src, seg, n):
    return jax.ops.segment_sum(src, seg, n)
kernel_name = 'mk_decoder_preln_d1_seqx_r4_c10cc1'

def setup_inputs(seed: int=0):
    np.random.seed(seed)
    _w = jnp.asarray

    def _rec_inputs():
        import jax
        import jax.numpy as jnp
        _rk = jax.random.key(seed)
        x = -0.0003929 + 0.9999 * jax.random.normal(jax.random.fold_in(_rk, 1), (2, 512, 1024), jnp.float32)
        _lenS = 512 - jax.random.randint(jax.random.fold_in(_rk, 7), (2,), 0, max(1, 512 // 4) + 1, jnp.int32)
        _lenS2 = 1024 - jax.random.randint(jax.random.fold_in(_rk, 8), (2,), 0, max(1, 1024 // 4) + 1, jnp.int32)
        pos_BxS = jnp.broadcast_to(jnp.arange(512, dtype=jnp.int32), (2, 512))
        _ctx_1024P = jax.random.normal(jax.random.fold_in(_rk, 12), (2, 16, 256), jnp.float32)
        _ctx_1024c = jax.random.dirichlet(jax.random.fold_in(_rk, 512), 0.3 * jnp.ones((16,), jnp.float32), (2, 1024))
        _ctx_1024t = jnp.einsum('bsk,bkd->bsd', _ctx_1024c, _ctx_1024P)
        _ctx_1024t = _ctx_1024t * jax.lax.rsqrt(jnp.mean(jnp.square(_ctx_1024t)) + 1e-12) * 0.953939
        ctx_1024 = 6.77073e-06 + 0.0199965 * (_ctx_1024t + 0.3 * jax.random.normal(jax.random.fold_in(_rk, 612), (2, 1024, 256), jnp.float32))
        return (x, pos_BxS, ctx_1024)
    x, pos_BxS, ctx_1024 = _rec_inputs()

    def _L0_attn_setup():
        import jax, jax.numpy as jnp
        import numpy as np
        HIDDEN = 1024
        N_HEADS = 32
        N_KV_HEADS = 8
        HEAD_DIM = HIDDEN // N_HEADS
        N_REP = N_HEADS // N_KV_HEADS
        KV_DIM = N_KV_HEADS * HEAD_DIM

        def _kaiming_uniform(key, out_f, in_f):
            bound = 1.0 / np.sqrt(in_f)
            return jax.random.uniform(key, (out_f, in_f), jnp.float32, -bound, bound)

        def bitnet_linear(x, weight, scale_param):
            s = jnp.maximum(jnp.mean(jnp.abs(weight), axis=1), 1e-08)
            binary_w = jnp.sign(weight / s[:, None])
            y = jnp.einsum('bsi,oi->bso', x, binary_w)
            y = y * (s * scale_param)[None, None, :]
            return jnp.nan_to_num(y, nan=0.0, posinf=1000000.0, neginf=-1000000.0)
        key = jax.random.key(seed)
        ks = jax.random.split(key, 5)
        return {'hidden_states': jax.random.normal(ks[0], (1, 512, HIDDEN), jnp.float32), 'q_weight': _kaiming_uniform(ks[1], HIDDEN, HIDDEN), 'q_scale': jnp.ones((HIDDEN,), jnp.float32), 'k_weight': _kaiming_uniform(ks[2], KV_DIM, HIDDEN), 'k_scale': jnp.ones((KV_DIM,), jnp.float32), 'v_weight': _kaiming_uniform(ks[3], KV_DIM, HIDDEN), 'v_scale': jnp.ones((KV_DIM,), jnp.float32), 'o_weight': _kaiming_uniform(ks[4], HIDDEN, HIDDEN), 'o_scale': jnp.ones((HIDDEN,), jnp.float32)}
    _L0_attn_all = _L0_attn_setup()
    _L0_attn_in = {k: v for k, v in _L0_attn_all.items() if k in ('q_weight', 'q_scale', 'k_weight', 'k_scale', 'v_weight', 'v_scale', 'o_weight', 'o_scale')}
    del _L0_attn_all

    def _L0_xattn_setup():
        import jax, jax.numpy as jnp
        import numpy as np
        H = 256
        C = 4
        RH = 16
        HS = H // RH
        DR = 8
        M = 1024
        NH = 16
        HD = H // NH
        A_SIZE = (C - 1) * RH
        B_SIZE = C * RH
        EPS = 1e-05
        SSM_EPS = 1e-05

        def rat_read(res, W, gamma, beta, num_outputs):
            b, l, _ = res.shape
            x = res.reshape(b, l, H, C)
            y = jnp.einsum('blhc,hoc->bloh', x, W)
            mu = y.mean(-1, keepdims=True)
            var = y.var(-1, keepdims=True)
            yn = (y - mu) * jax.lax.rsqrt(var + EPS)
            yn = yn * gamma.reshape(num_outputs, H) + beta.reshape(num_outputs, H)
            return yn.reshape(b, l, num_outputs * H)

        def rope(x, pos):
            half = HD // 2
            inv = 1.0 / 10000.0 ** (jnp.arange(half, dtype=jnp.float32) / half)
            ang = pos.astype(jnp.float32)[..., None] * inv
            cos = jnp.cos(ang)[:, :, None, :]
            sin = jnp.sin(ang)[:, :, None, :]
            x1, x2 = (x[..., :half], x[..., half:])
            return jnp.concatenate([x1 * cos - x2 * sin, x2 * cos + x1 * sin], axis=-1)

        def attention(qkv_in, qkv_w, pos):
            b, l, _ = qkv_in.shape
            q, k, v = jnp.split(qkv_in, 3, axis=-1)
            q = jnp.einsum('bli,oi->blo', q, qkv_w[0]).reshape(b, l, NH, HD)
            k = jnp.einsum('bli,oi->blo', k, qkv_w[1]).reshape(b, l, NH, HD)
            v = jnp.einsum('bli,oi->blo', v, qkv_w[2]).reshape(b, l, NH, HD)
            q = rope(q, pos)
            k = rope(k, pos)
            scores = jnp.einsum('bqhd,bkhd->bhqk', q, k) / np.sqrt(HD).astype(np.float32)
            mask = jnp.tril(jnp.ones((l, l), dtype=bool))
            scores = jnp.where(mask, scores, jnp.float32(-1e+30))
            p = jax.nn.softmax(scores, axis=-1)
            o = jnp.einsum('bhqk,bkhd->bqhd', p, v)
            return o.reshape(b, l, H)

        def rat_write(res, y, wod_w, wab_w, wab_b, du_w, du_b):
            b, l, _ = res.shape
            o_d = y @ wod_w.T
            A_B = y @ wab_w.T + wab_b
            out = o_d[..., :H]
            delta_low = o_d[..., H:]
            A_logit = A_B[..., :A_SIZE]
            B_proj = A_B[..., A_SIZE:2 * A_SIZE]
            B_skip = A_B[..., 2 * A_SIZE:]
            delta = jax.nn.softplus(delta_low @ du_w.T + du_b)
            hs = res.reshape(b, l, HS, RH, C)
            out = out.reshape(b, l, HS, RH, 1)
            delta = delta.reshape(b, l, HS, RH, 1)
            A_logit = A_logit.reshape(b, l, 1, RH, C - 1)
            B_proj = B_proj.reshape(b, l, 1, RH, C - 1)
            B_skip = B_skip.reshape(b, l, 1, RH, 1)
            A_neg = -jax.nn.softplus(A_logit)
            A_bar = jnp.exp(delta * A_neg)
            B_bar = (A_bar - 1.0) / (A_neg - SSM_EPS) * B_proj
            B_bar_skip = delta * B_skip
            A_full = jnp.concatenate([A_bar, jnp.ones_like(A_bar[..., :1])], axis=-1)
            B_full = jnp.concatenate([B_bar, B_bar_skip], axis=-1)
            return (hs * A_full + out * B_full).reshape(b, l, H * C)

        def layer_forward(hidden_states, position_ids, attn_read_w, attn_read_g, attn_read_b, qkv_w, attn_wod_w, attn_wab_w, attn_wab_b, attn_du_w, attn_du_b, mlp_read_w, mlp_read_g, mlp_read_b, mlp_in_w, mlp_wod_w, mlp_wab_w, mlp_wab_b, mlp_du_w, mlp_du_b):
            qkv_in = rat_read(hidden_states, attn_read_w, attn_read_g, attn_read_b, 3)
            attn_out = attention(qkv_in, qkv_w, position_ids)
            hidden_states = rat_write(hidden_states, attn_out, attn_wod_w, attn_wab_w, attn_wab_b, attn_du_w, attn_du_b)
            mlp_in = rat_read(hidden_states, mlp_read_w, mlp_read_g, mlp_read_b, 2)
            g_in, u_in = (mlp_in[..., :H], mlp_in[..., H:])
            gate = jnp.einsum('bli,oi->blo', g_in, mlp_in_w[0])
            up = jnp.einsum('bli,oi->blo', u_in, mlp_in_w[1])
            mlp_out = jax.nn.silu(gate) * up
            hidden_states = rat_write(hidden_states, mlp_out, mlp_wod_w, mlp_wab_w, mlp_wab_b, mlp_du_w, mlp_du_b)
            return hidden_states
        key = jax.random.key(seed)
        ks = jax.random.split(key, 20)
        B, L = (2, 512)
        s = 0.02
        return {'hidden_states': jax.random.normal(ks[0], (B, L, H * C), jnp.float32), 'position_ids': jnp.tile(jnp.arange(L, dtype=jnp.int64), (B, 1)), 'attn_read_w': jax.random.normal(ks[1], (H, 3, C), jnp.float32) / np.sqrt(C).astype(np.float32), 'attn_read_g': jnp.ones((3 * H,), jnp.float32), 'attn_read_b': jnp.zeros((3 * H,), jnp.float32), 'qkv_w': jax.random.normal(ks[2], (3, H, H), jnp.float32) * s, 'attn_wod_w': jax.random.normal(ks[3], (H + DR, H), jnp.float32) * s, 'attn_wab_w': jax.random.normal(ks[4], (A_SIZE + B_SIZE, H), jnp.float32) * s, 'attn_wab_b': jax.random.normal(ks[5], (A_SIZE + B_SIZE,), jnp.float32) * s, 'attn_du_w': jax.random.normal(ks[6], (H, DR), jnp.float32) * s, 'attn_du_b': jax.random.normal(ks[7], (H,), jnp.float32) * s, 'mlp_read_w': jax.random.normal(ks[8], (H, 2, C), jnp.float32) / np.sqrt(C).astype(np.float32), 'mlp_read_g': jnp.ones((2 * H,), jnp.float32), 'mlp_read_b': jnp.zeros((2 * H,), jnp.float32), 'mlp_in_w': jax.random.normal(ks[9], (2, M, H), jnp.float32) * s, 'mlp_wod_w': jax.random.normal(ks[10], (H + DR, M), jnp.float32) * s, 'mlp_wab_w': jax.random.normal(ks[11], (A_SIZE + B_SIZE, M), jnp.float32) * s, 'mlp_wab_b': jax.random.normal(ks[12], (A_SIZE + B_SIZE,), jnp.float32) * s, 'mlp_du_w': jax.random.normal(ks[13], (H, DR), jnp.float32) * s, 'mlp_du_b': jax.random.normal(ks[14], (H,), jnp.float32) * s}
    _L0_xattn_all = _L0_xattn_setup()
    _L0_xattn_in = {k: v for k, v in _L0_xattn_all.items() if k in ('attn_read_w', 'attn_read_g', 'attn_read_b', 'qkv_w', 'attn_wod_w', 'attn_wab_w', 'attn_wab_b', 'attn_du_w', 'attn_du_b', 'mlp_read_w', 'mlp_read_g', 'mlp_read_b', 'mlp_wod_w', 'mlp_wab_w', 'mlp_wab_b', 'mlp_du_w', 'mlp_du_b')}
    del _L0_xattn_all

    def _L0_ffn_setup():
        import jax, jax.numpy as jnp
        import numpy as np
        B, T, D_IN, D_OUT = (8, 512, 1024, 1024)
        N_LORAS, RANK = (16, 32)
        SCALING = 1.0
        key = jax.random.key(seed)
        ks = jax.random.split(key, 8)
        std = 1.0 / D_IN ** 0.5
        x = jax.random.normal(ks[0], (B, T, D_IN), dtype=jnp.float32)
        idx = jax.random.randint(ks[1], (B,), 0, N_LORAS)
        gate = jax.nn.one_hot(idx, N_LORAS, dtype=jnp.float32)
        kernel = jax.random.normal(ks[2], (D_IN, D_OUT), dtype=jnp.float32) * std
        bias = jnp.zeros((D_OUT,), dtype=jnp.float32)
        lora_A = jax.random.normal(ks[3], (N_LORAS, RANK, D_IN), dtype=jnp.float32) * std
        lora_B = jax.random.normal(ks[4], (N_LORAS, D_OUT, RANK), dtype=jnp.float32) * 0.01
        lora_A_shared = jax.random.normal(ks[5], (RANK, D_IN), dtype=jnp.float32) * std
        lora_B_shared = jax.random.normal(ks[6], (D_OUT, RANK), dtype=jnp.float32) * 0.01
        return {'x': x, 'gate': gate, 'kernel': kernel, 'bias': bias, 'lora_A': lora_A, 'lora_B': lora_B, 'lora_A_shared': lora_A_shared, 'lora_B_shared': lora_B_shared}
    _L0_ffn_all = _L0_ffn_setup()
    _L0_ffn_in = {k: v for k, v in _L0_ffn_all.items() if k in ('gate', 'kernel', 'bias', 'lora_A', 'lora_B', 'lora_A_shared', 'lora_B_shared')}
    del _L0_ffn_all
    return {'x': x, 'pos_BxS': pos_BxS, 'ctx_1024': ctx_1024, 'L0_attn_q_weight': _L0_attn_in['q_weight'], 'L0_attn_q_scale': _L0_attn_in['q_scale'], 'L0_attn_k_weight': _L0_attn_in['k_weight'], 'L0_attn_k_scale': _L0_attn_in['k_scale'], 'L0_attn_v_weight': _L0_attn_in['v_weight'], 'L0_attn_v_scale': _L0_attn_in['v_scale'], 'L0_attn_o_weight': _L0_attn_in['o_weight'], 'L0_attn_o_scale': _L0_attn_in['o_scale'], 'L0_xattn_attn_read_w': _L0_xattn_in['attn_read_w'], 'L0_xattn_attn_read_g': _L0_xattn_in['attn_read_g'], 'L0_xattn_attn_read_b': _L0_xattn_in['attn_read_b'], 'L0_xattn_qkv_w': _L0_xattn_in['qkv_w'], 'L0_xattn_attn_wod_w': _L0_xattn_in['attn_wod_w'], 'L0_xattn_attn_wab_w': _L0_xattn_in['attn_wab_w'], 'L0_xattn_attn_wab_b': _L0_xattn_in['attn_wab_b'], 'L0_xattn_attn_du_w': _L0_xattn_in['attn_du_w'], 'L0_xattn_attn_du_b': _L0_xattn_in['attn_du_b'], 'L0_xattn_mlp_read_w': _L0_xattn_in['mlp_read_w'], 'L0_xattn_mlp_read_g': _L0_xattn_in['mlp_read_g'], 'L0_xattn_mlp_read_b': _L0_xattn_in['mlp_read_b'], 'L0_xattn_mlp_wod_w': _L0_xattn_in['mlp_wod_w'], 'L0_xattn_mlp_wab_w': _L0_xattn_in['mlp_wab_w'], 'L0_xattn_mlp_wab_b': _L0_xattn_in['mlp_wab_b'], 'L0_xattn_mlp_du_w': _L0_xattn_in['mlp_du_w'], 'L0_xattn_mlp_du_b': _L0_xattn_in['mlp_du_b'], 'L0_ffn_gate': _L0_ffn_in['gate'], 'L0_ffn_kernel': _L0_ffn_in['kernel'], 'L0_ffn_bias': _L0_ffn_in['bias'], 'L0_ffn_lora_A': _L0_ffn_in['lora_A'], 'L0_ffn_lora_B': _L0_ffn_in['lora_B'], 'L0_ffn_lora_A_shared': _L0_ffn_in['lora_A_shared'], 'L0_ffn_lora_B_shared': _L0_ffn_in['lora_B_shared']}

def reference(x, pos_BxS, ctx_1024, L0_attn_q_weight, L0_attn_q_scale, L0_attn_k_weight, L0_attn_k_scale, L0_attn_v_weight, L0_attn_v_scale, L0_attn_o_weight, L0_attn_o_scale, L0_xattn_attn_read_w, L0_xattn_attn_read_g, L0_xattn_attn_read_b, L0_xattn_qkv_w, L0_xattn_attn_wod_w, L0_xattn_attn_wab_w, L0_xattn_attn_wab_b, L0_xattn_attn_du_w, L0_xattn_attn_du_b, L0_xattn_mlp_read_w, L0_xattn_mlp_read_g, L0_xattn_mlp_read_b, L0_xattn_mlp_wod_w, L0_xattn_mlp_wab_w, L0_xattn_mlp_wab_b, L0_xattn_mlp_du_w, L0_xattn_mlp_du_b, L0_ffn_gate, L0_ffn_kernel, L0_ffn_bias, L0_ffn_lora_A, L0_ffn_lora_B, L0_ffn_lora_A_shared, L0_ffn_lora_B_shared):
    import jax
    import jax.numpy as jnp

    def _L0_attn_ref(hidden_states, q_weight, q_scale, k_weight, k_scale, v_weight, v_scale, o_weight, o_scale):
        import jax, jax.numpy as jnp
        import numpy as np
        HIDDEN = 1024
        N_HEADS = 32
        N_KV_HEADS = 8
        HEAD_DIM = HIDDEN // N_HEADS
        N_REP = N_HEADS // N_KV_HEADS
        KV_DIM = N_KV_HEADS * HEAD_DIM

        def _kaiming_uniform(key, out_f, in_f):
            bound = 1.0 / np.sqrt(in_f)
            return jax.random.uniform(key, (out_f, in_f), jnp.float32, -bound, bound)

        def bitnet_linear(x, weight, scale_param):
            s = jnp.maximum(jnp.mean(jnp.abs(weight), axis=1), 1e-08)
            binary_w = jnp.sign(weight / s[:, None])
            y = jnp.einsum('bsi,oi->bso', x, binary_w)
            y = y * (s * scale_param)[None, None, :]
            return jnp.nan_to_num(y, nan=0.0, posinf=1000000.0, neginf=-1000000.0)
        b, s, _ = hidden_states.shape
        q = bitnet_linear(hidden_states, q_weight, q_scale)
        k = bitnet_linear(hidden_states, k_weight, k_scale)
        v = bitnet_linear(hidden_states, v_weight, v_scale)
        q = q.reshape(b, s, N_HEADS, HEAD_DIM).transpose(0, 2, 1, 3)
        k = k.reshape(b, s, N_KV_HEADS, HEAD_DIM).transpose(0, 2, 1, 3)
        v = v.reshape(b, s, N_KV_HEADS, HEAD_DIM).transpose(0, 2, 1, 3)
        k = jnp.repeat(k, N_REP, axis=1)
        v = jnp.repeat(v, N_REP, axis=1)
        scores = jnp.einsum('bhqd,bhkd->bhqk', q, k) / np.sqrt(HEAD_DIM)
        attn = jax.nn.softmax(scores, axis=-1)
        out = jnp.einsum('bhqk,bhkd->bhqd', attn, v)
        out = out.transpose(0, 2, 1, 3).reshape(b, s, HIDDEN)
        return bitnet_linear(out, o_weight, o_scale)

    def _L0_xattn_ref(hidden_states, position_ids, attn_read_w, attn_read_g, attn_read_b, qkv_w, attn_wod_w, attn_wab_w, attn_wab_b, attn_du_w, attn_du_b, mlp_read_w, mlp_read_g, mlp_read_b, mlp_in_w, mlp_wod_w, mlp_wab_w, mlp_wab_b, mlp_du_w, mlp_du_b):
        import jax, jax.numpy as jnp
        import numpy as np
        H = 256
        C = 4
        RH = 16
        HS = H // RH
        DR = 8
        M = 1024
        NH = 16
        HD = H // NH
        A_SIZE = (C - 1) * RH
        B_SIZE = C * RH
        EPS = 1e-05
        SSM_EPS = 1e-05

        def rat_read(res, W, gamma, beta, num_outputs):
            b, l, _ = res.shape
            x = res.reshape(b, l, H, C)
            y = jnp.einsum('blhc,hoc->bloh', x, W)
            mu = y.mean(-1, keepdims=True)
            var = y.var(-1, keepdims=True)
            yn = (y - mu) * jax.lax.rsqrt(var + EPS)
            yn = yn * gamma.reshape(num_outputs, H) + beta.reshape(num_outputs, H)
            return yn.reshape(b, l, num_outputs * H)

        def rope(x, pos):
            half = HD // 2
            inv = 1.0 / 10000.0 ** (jnp.arange(half, dtype=jnp.float32) / half)
            ang = pos.astype(jnp.float32)[..., None] * inv
            cos = jnp.cos(ang)[:, :, None, :]
            sin = jnp.sin(ang)[:, :, None, :]
            x1, x2 = (x[..., :half], x[..., half:])
            return jnp.concatenate([x1 * cos - x2 * sin, x2 * cos + x1 * sin], axis=-1)

        def attention(qkv_in, qkv_w, pos):
            b, l, _ = qkv_in.shape
            q, k, v = jnp.split(qkv_in, 3, axis=-1)
            q = jnp.einsum('bli,oi->blo', q, qkv_w[0]).reshape(b, l, NH, HD)
            k = jnp.einsum('bli,oi->blo', k, qkv_w[1]).reshape(b, l, NH, HD)
            v = jnp.einsum('bli,oi->blo', v, qkv_w[2]).reshape(b, l, NH, HD)
            q = rope(q, pos)
            k = rope(k, pos)
            scores = jnp.einsum('bqhd,bkhd->bhqk', q, k) / np.sqrt(HD).astype(np.float32)
            mask = jnp.tril(jnp.ones((l, l), dtype=bool))
            scores = jnp.where(mask, scores, jnp.float32(-1e+30))
            p = jax.nn.softmax(scores, axis=-1)
            o = jnp.einsum('bhqk,bkhd->bqhd', p, v)
            return o.reshape(b, l, H)

        def rat_write(res, y, wod_w, wab_w, wab_b, du_w, du_b):
            b, l, _ = res.shape
            o_d = y @ wod_w.T
            A_B = y @ wab_w.T + wab_b
            out = o_d[..., :H]
            delta_low = o_d[..., H:]
            A_logit = A_B[..., :A_SIZE]
            B_proj = A_B[..., A_SIZE:2 * A_SIZE]
            B_skip = A_B[..., 2 * A_SIZE:]
            delta = jax.nn.softplus(delta_low @ du_w.T + du_b)
            hs = res.reshape(b, l, HS, RH, C)
            out = out.reshape(b, l, HS, RH, 1)
            delta = delta.reshape(b, l, HS, RH, 1)
            A_logit = A_logit.reshape(b, l, 1, RH, C - 1)
            B_proj = B_proj.reshape(b, l, 1, RH, C - 1)
            B_skip = B_skip.reshape(b, l, 1, RH, 1)
            A_neg = -jax.nn.softplus(A_logit)
            A_bar = jnp.exp(delta * A_neg)
            B_bar = (A_bar - 1.0) / (A_neg - SSM_EPS) * B_proj
            B_bar_skip = delta * B_skip
            A_full = jnp.concatenate([A_bar, jnp.ones_like(A_bar[..., :1])], axis=-1)
            B_full = jnp.concatenate([B_bar, B_bar_skip], axis=-1)
            return (hs * A_full + out * B_full).reshape(b, l, H * C)

        def layer_forward(hidden_states, position_ids, attn_read_w, attn_read_g, attn_read_b, qkv_w, attn_wod_w, attn_wab_w, attn_wab_b, attn_du_w, attn_du_b, mlp_read_w, mlp_read_g, mlp_read_b, mlp_in_w, mlp_wod_w, mlp_wab_w, mlp_wab_b, mlp_du_w, mlp_du_b):
            qkv_in = rat_read(hidden_states, attn_read_w, attn_read_g, attn_read_b, 3)
            attn_out = attention(qkv_in, qkv_w, position_ids)
            hidden_states = rat_write(hidden_states, attn_out, attn_wod_w, attn_wab_w, attn_wab_b, attn_du_w, attn_du_b)
            mlp_in = rat_read(hidden_states, mlp_read_w, mlp_read_g, mlp_read_b, 2)
            g_in, u_in = (mlp_in[..., :H], mlp_in[..., H:])
            gate = jnp.einsum('bli,oi->blo', g_in, mlp_in_w[0])
            up = jnp.einsum('bli,oi->blo', u_in, mlp_in_w[1])
            mlp_out = jax.nn.silu(gate) * up
            hidden_states = rat_write(hidden_states, mlp_out, mlp_wod_w, mlp_wab_w, mlp_wab_b, mlp_du_w, mlp_du_b)
            return hidden_states
        return layer_forward(hidden_states, position_ids, attn_read_w, attn_read_g, attn_read_b, qkv_w, attn_wod_w, attn_wab_w, attn_wab_b, attn_du_w, attn_du_b, mlp_read_w, mlp_read_g, mlp_read_b, mlp_in_w, mlp_wod_w, mlp_wab_w, mlp_wab_b, mlp_du_w, mlp_du_b)

    def _L0_ffn_ref(x, gate, kernel, bias, lora_A, lora_B, lora_A_shared, lora_B_shared):
        import jax, jax.numpy as jnp
        import numpy as np
        B, T, D_IN, D_OUT = (8, 512, 1024, 1024)
        N_LORAS, RANK = (16, 32)
        SCALING = 1.0
        base_out = jnp.matmul(x, kernel) + bias
        b = gate.shape[0]
        x_flat = x.reshape(b, -1, x.shape[-1])
        A_eff = jnp.einsum('bn,nri->bri', gate, lora_A)
        B_eff = jnp.einsum('bn,nor->bor', gate, lora_B)
        Ax = jnp.einsum('bri,bti->btr', A_eff, x_flat)
        delta_flat = jnp.einsum('bor,btr->bto', B_eff, Ax)
        Ax_s = jnp.einsum('ri,bti->btr', lora_A_shared, x_flat)
        delta_flat = delta_flat + jnp.einsum('or,btr->bto', lora_B_shared, Ax_s)
        delta = delta_flat.reshape(x.shape[:-1] + (kernel.shape[-1],))
        return base_out + (SCALING * delta).astype(base_out.dtype)
    x = x + _L0_attn_ref(_layernorm(x, axis=-1), L0_attn_q_weight, L0_attn_q_scale, L0_attn_k_weight, L0_attn_k_scale, L0_attn_v_weight, L0_attn_v_scale, L0_attn_o_weight, L0_attn_o_scale)
    x = x + _L0_xattn_ref(_layernorm(x, axis=-1), pos_BxS, L0_xattn_attn_read_w, L0_xattn_attn_read_g, L0_xattn_attn_read_b, L0_xattn_qkv_w, L0_xattn_attn_wod_w, L0_xattn_attn_wab_w, L0_xattn_attn_wab_b, L0_xattn_attn_du_w, L0_xattn_attn_du_b, L0_xattn_mlp_read_w, L0_xattn_mlp_read_g, L0_xattn_mlp_read_b, ctx_1024, L0_xattn_mlp_wod_w, L0_xattn_mlp_wab_w, L0_xattn_mlp_wab_b, L0_xattn_mlp_du_w, L0_xattn_mlp_du_b)
    x = x + _L0_ffn_ref(_layernorm(x, axis=-1), L0_ffn_gate, L0_ffn_kernel, L0_ffn_bias, L0_ffn_lora_A, L0_ffn_lora_B, L0_ffn_lora_A_shared, L0_ffn_lora_B_shared)
    return x

_drawn_inputs = setup_inputs


def setup_inputs(seed=0):
    import zlib

    import numpy as np

    out = dict(_drawn_inputs(seed))
    spreads = {'L0_attn_q_scale': (1.0, 0.2),
     'L0_attn_k_scale': (1.0, 0.2),
     'L0_attn_v_scale': (1.0, 0.2),
     'L0_attn_o_scale': (1.0, 0.2),
     'L0_xattn_attn_read_g': (1.0, 0.2),
     'L0_xattn_attn_read_b': (0.0, 0.1),
     'L0_xattn_mlp_read_g': (1.0, 0.2),
     'L0_xattn_mlp_read_b': (0.0, 0.1),
     'L0_ffn_bias': (0.0, 0.1)}
    factors = {}
    for name, (base, spread) in spreads.items():
        noise = np.random.default_rng([zlib.crc32(name.encode()), seed]).standard_normal(out[name].shape)
        drawn = base * np.exp(spread * noise) if base else spread * noise
        out[name] = jnp.asarray(drawn.astype(out[name].dtype))
    for name, factor in factors.items():
        out[name] = (out[name] * factor).astype(out[name].dtype)
    return out
```

```python
from contextlib import ExitStack

import numpy as np

import concourse.bass as bass
from concourse import mybir

F32 = mybir.dt.float32
F32R = mybir.dt.float32r
F16 = mybir.dt.float16
BF16 = mybir.dt.bfloat16
I32 = mybir.dt.int32
ALU = mybir.AluOpType
ACT = mybir.ActivationFunctionType
AX_X = mybir.AxisListType.X
ds = bass.ds

P = 128
B, S, D = 2, 512, 1024
T = B * S
NT = T // P
KC = D // P
QT = S // P
LN_EPS = 1e-5

A_HD, A_KV = 32, 8
A_REP = D // A_HD // A_KV
KVD = A_KV * A_HD
QKV = D + 2 * KVD
A_SCALE = float(1.0 / np.sqrt(A_HD))
A_MAX = 3 * A_HD
A_ROWS = A_MAX + 2
V_GAIN = 64.0

H, C, RH = 256, 4, 16
HS, DR, M = H // RH, 8, 1024
X_NH = 16
X_HD = H // X_NH
HALF = X_HD // 2
HC = P // C
NQ = 4
X_QUADS = X_NH // NQ
X_MAX = 4 * X_HD
X_SCALE = float(1.0 / np.sqrt(X_HD))
N_A = (C - 1) * RH
N_AB = 2 * N_A + RH
N_Z = H + N_A
N_W = H + N_AB + DR
SSM_EPS = 1e-5

N_LORA, RANK = 16, 32
R8 = P // N_LORA
R4 = RANK // R8
R2 = 2 * RANK

MAGIC = 1.5 * 2.0 ** 23
TWO_PI = 2 * np.pi
TP1 = 6.28125
TP2 = float(np.float32(np.float16(TWO_PI - TP1)))
TP3 = float(TWO_PI - TP1 - TP2)
ROPE_INV = (np.float32(1) / np.power(np.float32(10000), np.arange(HALF, dtype=np.float32) / np.float32(HALF))).astype(np.float32)

COLS = {}
_at = 0
for _n, _w in (("q_scale", KC), ("k_scale", KVD // P), ("g1", 6), ("b1", 6), ("g2", 4), ("b2", 4)):
    COLS[_n] = (_at, _at + _w)
    _at += _w
N_COLS = _at
ROWS = {}
_at = 0
for _n, _w in (("wab1", N_AB), ("wab2", N_AB), ("du1", H), ("du2", H), ("bias", D)):
    ROWS[_n] = (_at, _at + _w)
    _at += _w
N_ROWS = _at
N_SCALES = KVD + D


def build_program(nc, d, out):
    ctx = ExitStack()
    with ctx:
        def sb(name, shape, dt=F32):
            return ctx.enter_context(nc.sbuf_tensor(name, shape, dt))

        def sem(name):
            return ctx.enter_context(nc.semaphore(name))

        def scratch(name, shape):
            return nc.dram_tensor(name, shape, F32).ap()

        psum = ctx.enter_context(nc.psum_tensor("psum", [P, 8, 512], F32))

        cols = sb("cols", [P, N_COLS])
        rows = sb("rows", [P, N_ROWS])
        ident = sb("ident", [P, P])
        ident_bf = sb("ident_bf", [P, P], BF16)
        mask_qk = sb("mask_qk", [P, P], BF16)
        mask_kq = sb("mask_kq", [P, P], BF16)
        ones32 = sb("ones32", [P, A_HD])
        minus_half = sb("minus_half", [P, 4])
        c_q = sb("c_q", [P, KC])
        c_k = sb("c_k", [P, KVD // P])
        c_o = sb("c_o", [P, D])
        pos_i = sb("pos_i", [P, NT], I32)
        pos_f = sb("pos_f", [P, NT])
        trig = sb("trig", [P, 3, NT, HALF])

        region_x = sb("region_x", [P, KC * T])
        region_a = sb("region_a", [P, KC * T])
        region_w = sb("region_w", [P, QKV + D + QKV + D + KC * QKV // 2])
        region_p = sb("region_p", [P, 2 * 4 * 512])
        region_s = sb("region_s", [P, KC * D // 2])
        xnT_hi = region_x[:, 0:KC * T // 2].bitcast(F16).rearrange("p (c t) -> p c t", c=KC)
        xnT_lo = region_x[:, KC * T // 2:].bitcast(F16).rearrange("p (c t) -> p c t", c=KC)
        x1 = region_x[:, :].rearrange("p (t n) -> p t n", t=NT)
        attT_hi = region_a[:, 0:KC * T // 2].bitcast(F16).rearrange("p (c t) -> p c t", c=KC)
        attT_lo = region_a[:, KC * T // 2:].bitcast(F16).rearrange("p (c t) -> p c t", c=KC)
        kern = region_a[:, :].rearrange("p (c n) -> p c n", c=KC)
        _o = 0
        w_in_qkv = region_w[:, 0:QKV]
        w_in_o = region_w[:, QKV:QKV + D]
        _o = QKV + D
        w_abs = region_w[:, _o:_o + QKV + D]
        _o += QKV + D
        sign_qkv = region_w[:, _o:].bitcast(F16).rearrange("p (c n) -> p c n", c=KC)
        sign_o = region_s[:, :].bitcast(F16).rearrange("p (c n) -> p c n", c=KC)
        prob = region_p[:, :].rearrange("p (b j n) -> p b j n", b=2, j=4)
        x_in = region_p[:, 0:2 * D].rearrange("p (u n) -> p u n", u=2)
        _o = 2 * D
        scale_rows = region_p[:, _o:_o + N_SCALES]
        _o += N_SCALES
        mean_w = region_p[:, _o:_o + P]
        _o += P
        c_v = region_p[:, _o:_o + KVD]
        _o += KVD
        ang = region_p[:, _o:_o + NT * HALF].rearrange("p (t f) -> p t f", f=HALF)
        _o += NT * HALF
        trig_n, trig_r = (region_p[:, _o + n * 2 * NT * HALF:_o + (n + 1) * 2 * NT * HALF].rearrange("p (k t f) -> p k t f", k=2, f=HALF)
                          for n in range(2))

        q_op = [sb(f"q_op{u}", [P, A_REP, S], F32R) for u in range(2)]
        kr = sb("kr", [P, 2 * NQ * S], F32R)
        k_op = [kr[:, u * S:(u + 1) * S] for u in range(2)]
        hi_st = sb("hi_st", [P, S], F32R)
        lo_st = sb("lo_st", [P, S], F32R)
        m_hi = sb("m_hi", [16, P], F32R)
        m_lo = sb("m_lo", [16, P], F32R)
        kx_op = [kr[:, u * NQ * S:(u + 1) * NQ * S].rearrange("p (j n) -> p j n", j=NQ) for u in range(2)]

        st = sb("st", [P, 2, 2, 6])
        mv = sb("mv", [P, 2, 2])
        ve = sb("ve", [P, 2, 1])
        rstd = sb("rstd", [P, 2, 1])

        v_all = sb("v_all", [P, NT, KVD])
        v_g = sb("v_g", [P, 2, QT, A_HD])
        m_neg = sb("m_neg", [P, 2, 16])
        o_sb, den_sb, att = (w_in_qkv[:, n * S:(n + 1) * S] for n in range(3))

        v_x = region_w[:, 3 * S:3 * S + NT * 2 * H].rearrange("p (t n) -> p t n", t=NT)
        _o = 3 * S + NT * 2 * H
        ctx_w = region_w[:, _o:_o + 4 * M].rearrange("p (w k n) -> p w k n", w=2, k=2)
        _o += 4 * M
        wqkv = region_w[:, _o:_o + 6 * H].rearrange("p (s n) -> p s n", s=6)
        lora_bt = region_w[:, _o:_o + D]
        lora_at = region_w[:, _o + D:_o + D + KC * R2].rearrange("p (c r) -> p c r", c=KC)
        y0 = region_p[:, 2 * D:3 * D]
        h_st = region_p[:, 3 * D:4 * D]
        hT = v_all[:].rearrange("p t n -> p (t n)")[:, 0:D].rearrange("p (c n) -> p c n", c=KC)
        v_q = v_all[:].rearrange("p t n -> p (t n)")[:, 0:2 * QT * P].rearrange("p (b k n) -> p b k n", b=B, k=QT)
        write1 = region_s[:, 0:2 * N_W].rearrange("p (k n) -> p k n", k=2)
        write2 = region_s[:, 2 * N_W:10 * N_W].rearrange("p (k n) -> p k n", k=KC)
        v_rest = v_all[:].rearrange("p t n -> p (t n)")[:, D:2 * D]
        read1 = v_rest[:, 0:KC * 3 * HC].rearrange("p (c n) -> p c n", c=KC)
        read2 = v_rest[:, 0:KC * 2 * HC].rearrange("p (c n) -> p c n", c=KC)
        du = [v_rest[0:DR, KC * 2 * HC + n * H:KC * 2 * HC + (n + 1) * H] for n in range(2)]
        yn = sb("yn", [P, 3 * H])
        ynT = sb("ynT", [P, 6, P])
        rot = yn[:, 0:2 * H]
        rope_a = yn[:, 2 * H:3 * H]
        mvs = sb("mvs", [P, 2 * NT])
        ves = sb("ves", [P, 1])
        rstds = sb("rstds", [P, NT])
        st3 = sb("st3", [P, 3, 2, 6])
        mv3 = sb("mv3", [P, 3, 2])
        ve3 = sb("ve3", [P, 3])
        rs3 = sb("rs3", [P, 3])
        _w = [region_p[:, n * D:(n + 1) * D] for n in range(4)] + [region_w[:, 3 * S + n * D:3 * S + (n + 1) * D] for n in range(4)]
        h_in, h_mid, h_out, tanh_b, mlpT_f, out_t, abar, bbar = _w
        mlpT = mlpT_f.rearrange("p (f n) -> p f n", f=KC)
        h_a = region_w[:, 0:3 * H]
        z_b, e_b = region_w[:, 3 * H:3 * H + N_Z], region_w[:, 3 * H + N_Z:3 * H + 2 * N_Z]
        b_skip = abar[:, 3 * H:4 * H]
        sp_b = sb("sp_b", [P, N_Z])
        ab_b, r_b, rc_b = bbar[:, 3 * H:3 * H + 64], bbar[:, 3 * H + 64:3 * H + 64 + N_A], bbar[:, 3 * H + 128:3 * H + 128 + N_A]
        yT = v_g[:].rearrange("p b t e -> p (b t e)").rearrange("p (k n) -> p k n", k=2)
        low = sb("low", [DR, P])
        ax = bbar[:, 3 * H + 192:3 * H + 192 + R2]
        axT = region_w[0:R2, 3 * H + 2 * N_Z:3 * H + 2 * N_Z + P]
        lora_in = region_a[:, :].rearrange("p (s n) -> p s n", s=2 * R4)
        gate_b = region_w[:, 0:R4 * NT * RANK].rearrange("p (k n) -> p k n", k=R4)
        gate_a = region_w[:, R4 * NT * RANK:R4 * NT * RANK + NT * R8]
        a_eff = region_p[:, 0:KC * NT * RANK].rearrange("p (b c r) -> p b c r", b=NT, c=KC)
        b_eff = region_p[:, 2 * D:4 * D].rearrange("p (m n) -> p m n", m=2)

        def wait_apart(eng, semaphore, value):
            value = eng.to_reg(value)
            eng.wait_ge(s_const, 64)
            eng.wait_ge(semaphore, value)

        a_scr = scratch("a_scr", [NT, P, KC * RANK])
        b_scr = scratch("b_scr", [NT * RANK, D])
        k_scr = scratch("k_scr", [2, B, KVD, S])
        qk_scr = scratch("qk_scr", [2, 2, H, T])
        y_scr = scratch("y_scr", [H, T])

        s_const = sem("const_loaded")
        block = ctx.enter_context(nc.Block())

        x_slot = [sem(f"x_slot{u}_loaded") for u in range(2)]
        w_qkv_loaded, w_o_loaded = sem("w_qkv_loaded"), sem("w_o_loaded")
        sign_q_done, sign_o_done = sem("sign_q_done"), sem("sign_o_done")
        abs_taken, abs_done = sem("abs_taken"), sem("abs_done")
        made = sem("constants_made")
        ln_step, ln_rstd = sem("ln_step"), sem("ln_rstd")
        xn_ready = sem("xn_ready")
        xT_done, xT_hi, xT_free = sem("xT_done"), sem("xT_hi"), sem("xT_free")
        means_done, c_ready = sem("weight_means_done"), sem("scales_ready")
        k_mm, k_hi_ready, k_lo_ready , k_stored = sem("k_mm"), sem("k_hi_ready"), sem("k_lo_ready"), sem("k_stored")
        v_mm, v_ready = sem("v_mm"), sem("v_ready")
        ang_step, trig_done = sem("ang_step"), sem("trig_done")
        q_mm, q_hi_ready, q_lo_ready = sem("q_mm"), sem("q_hi_ready"), sem("q_lo_ready")
        q_stacked = [sem(f"q_stacked{u}") for u in range(2)]
        k_loaded = [sem(f"k_loaded{u}") for u in range(2)]
        m_loaded = [sem(f"m_loaded{u}") for u in range(2)]
        s_mm, s_max = sem("s_mm"), sem("s_max")
        mT_done, m_hi_ready, m_lo_ready = sem("mT_done"), sem("m_hi_ready"), sem("m_lo_ready")
        st_mm, p_ready, pv_done = sem("st_mm"), sem("p_ready"), sem("pv_done")
        vg_ready = sem("vg_ready")
        o_copied, den_rec, att_ready, att_hi_ready, att_lo_ready = sem("o_copied"), sem("den_rec"), sem("att_ready"), sem("att_hi_ready"), sem("att_lo_ready")
        lora_loaded, lora_mm, lora_ready, lora_stored = sem("lora_loaded"), sem("lora_mm"), sem("lora_ready"), sem("lora_stored")
        xw_loaded = sem("xw_loaded")
        x_again = [sem(f"x_again{u}") for u in range(2)]
        op_mm, y0_ready, x1_ready = sem("op_mm"), sem("y0_ready"), sem("x1_ready")
        l_step, l_rstd, h_ready = sem("l_step"), sem("l_rstd"), sem("h_ready")
        hT_mm, hT_ready, y_mm = sem("hT_mm"), sem("hT_ready"), sem("y_mm")
        y_step, y_rstd, yn_ready = sem("y_step"), sem("y_rstd"), sem("yn_ready")
        ynT_mm, ynT_ready, qkv_mm = sem("ynT_mm"), sem("ynT_ready"), sem("qkv_mm")
        rope_step, vx_ready, rT_mm, r_hi, r_lo, qk_stored = (sem(n) for n in (
            "rope_step", "vx_ready", "rT_mm", "r_hi", "r_lo", "qk_stored"))
        vx_zero, k_ones = sem("vx_zero"), sem("k_ones")
        xq_loaded = [sem(f"xq_loaded{u}") for u in range(2)]
        xm_loaded = [sem(f"xm_loaded{u}") for u in range(2)]
        xs_mm, xs_max, xmT_done, xm_hi, xm_lo = sem("xs_mm"), sem("xs_max"), sem("xmT_done"), sem("xm_hi"), sem("xm_lo")
        xst_mm, xp_ready, xpv_done, xv_ready = sem("xst_mm"), sem("xp_ready"), sem("xpv_done"), sem("xv_ready")
        xo_copied, xden_rec, xatt_ready, y_stored = sem("xo_copied"), sem("xden_rec"), sem("xatt_ready"), sem("y_stored")
        w2_loaded, kern_loaded, yT_loaded, lo_loaded = sem("w2_loaded"), sem("kern_loaded"), sem("yT_loaded"), sem("lo_loaded")
        h2_ready = sem("h2_ready")
        W = {n: sem(n) for n in (
            "w_mm", "low_ready", "du_mm", "z_ready", "az_ready", "e_ready", "l_ready", "sp_ready", "r_step",
            "da_ready", "abar_ready", "ha_ready", "b_step", "hn_ready")}
        h2T_mm, h2T_ready, y2_mm = sem("h2T_mm"), sem("h2T_ready"), sem("y2_mm")
        y2_step, y2_rstd, y2n_ready = sem("y2_step"), sem("y2_rstd"), sem("y2n_ready")
        y2T_mm, y2T_ready, gu_mm, tanh_ready, g_ready, mlp_ready = (sem(n) for n in (
            "y2T_mm", "y2T_ready", "gu_mm", "tanh_ready", "g_ready", "mlp_ready"))
        x2_ready, f_step, f_rstd, xf_ready = (sem(n) for n in ("x2_ready", "f_step", "f_rstd", "xf_ready"))
        fT_mm, fT_ready, ax_mm, ax_ready, axT_mm, axT_ready, f_mm, o_step, out_ready, out_stored = (sem(n) for n in (
            "fT_mm", "fT_ready", "ax_mm", "ax_ready", "axT_mm", "axT_ready", "f_mm", "o_step", "out_ready", "out_stored"))
        xatt_free = sem("a_finished")
        XI = X_QUADS * B
        NI = A_KV * B

        @block.sync
        def _(sp):
            sp.dma_start(cols[:], d["cols"]).then_inc(s_const, 16)
            sp.dma_start(rows[:], d["rows"]).then_inc(s_const, 16)
            sp.dma_start(scale_rows, d["scale_rows"]).then_inc(s_const, 16)
            sp.dma_start(pos_i[:], d["pos"]).then_inc(s_const, 16)
            sp.sem_inc(xT_done, 2)
            sp.sem_inc(sign_q_done, 1)
            sp.sem_inc(sign_o_done, 1)
            with sp.Fori(0, NT // 2) as it:
                for u in range(2):
                    i = it * 2 + u
                    sp.wait_ge(xT_done, i + 1)
                    sp.dma_start(x_in[:, u, :], d["x"][ds(i * P, P), :]).then_inc(x_slot[u], 16)
                    sp.wait_ge(abs_done, 2 * i + 1)
                    sp.dma_start(w_in_qkv, d["wT"][ds(i * P, P), 0:QKV]).then_inc(w_qkv_loaded, 16)
                    sp.wait_ge(abs_done, 2 * i + 2)
                    sp.dma_start(w_in_o, d["wT"][ds(i * P, P), QKV:QKV + D]).then_inc(w_o_loaded, 16)
            for n in range(4):
                b, m = n // 2, n % 2
                sp.wait_ge(k_hi_ready, n + 1)
                sp.wait_ge(k_lo_ready, n + 1)
                for part in range(2):
                    sp.dma_start(k_scr[part, b, m * P:(m + 1) * P, :], (hi_st, lo_st)[part][:].bitcast(F32)).then_inc(k_stored, 16)
            sp.wait_ge(k_stored, 2 * 16 * 4)
            sp.wait_ge(made, 16)
            sp.wait_ge(abs_done, 2 * NT + 2)
            sp.wait_ge(xT_done, NT + 2)
            for r in range(R4):
                sp.dma_start(lora_in[:, r, :], d["lora_a"][r]).then_inc(lora_loaded, 16)
                sp.dma_start(lora_in[:, R4 + r, :], d["lora_b"][r]).then_inc(lora_loaded, 16)
            sp.dma_start(gate_a, d["gate_a"]).then_inc(lora_loaded, 16)
            sp.dma_start(gate_b, d["gate_b"]).then_inc(lora_loaded, 16)
            sp.wait_ge(lora_ready, R4 + 4)
            for b in range(NT):
                sp.dma_start(a_scr[b], a_eff[:, b].rearrange("p c r -> p (c r)")).then_inc(lora_stored, 16)
            for m in range(2):
                sp.dma_start(b_scr[m * P:(m + 1) * P, :], b_eff[:, m, :]).then_inc(lora_stored, 16)

            sp.sem_inc(st_mm, 32)

            def stack_q(g, b):
                i = g * 2 + b
                sp.wait_ge(st_mm, 16 * i + 16)
                for part in range(3):
                    sp.dma_start(k_op[b][part * A_HD:(part + 1) * A_HD, :].bitcast(F32),
                                 k_scr[part % 2, b, ds(g * A_HD, A_HD), :]).then_inc(k_loaded[b], 16)
                sp.wait_ge(q_hi_ready, i + 1)
                sp.wait_ge(q_lo_ready, i + 1)
                for part in range(3):
                    src = (hi_st, hi_st, lo_st)[part]
                    for j in range(A_REP):
                        sp.dma_start(q_op[b][part * A_HD:(part + 1) * A_HD, j, :].bitcast(F32),
                                     src[j * A_HD:(j + 1) * A_HD, :].bitcast(F32)).then_inc(q_stacked[b], 16)

            def stack_m(g, b):
                i = g * 2 + b
                sp.wait_ge(m_hi_ready, i + 1)
                sp.wait_ge(m_lo_ready, i + 1)
                for r, src in ((A_MAX, m_hi), (A_MAX + 1, m_lo)):
                    sp.dma_start(q_op[b][r:r + 1].rearrange("o j n -> o (j n)").bitcast(F32), src[:].bitcast(F32)).then_inc(m_loaded[b], 16)

            stack_q(0, 0)
            stack_q(0, 1)
            stack_m(0, 0)
            with sp.Fori(0, A_KV - 1) as g:
                stack_q(g + 1, 0)
                stack_m(g, 1)
                stack_q(g + 1, 1)
                stack_m(g + 1, 0)
            stack_m(A_KV - 1, 1)

            sp.wait_ge(xatt_free, 1)
            sp.dma_start(read1, d["read1"]).then_inc(xw_loaded, 16)
            sp.dma_start(wqkv, d["wqkv"].rearrange("p o k n -> p (o k) n")).then_inc(xw_loaded, 16)
            sp.dma_start(ctx_w, d["ctx"]).then_inc(xw_loaded, 16)

            def load_x(i, u):
                sp.dma_start(x_in[:, u, :], d["x"][ds(i * P, P), :] if not isinstance(i, int) else d["x"][i * P:(i + 1) * P, :]).then_inc(x_again[u], 16)

            def store_qk(i):
                sp.wait_ge(r_hi, i + 1)
                sp.wait_ge(r_lo, i + 2)
                for part in range(2):
                    sp.dma_start(qk_scr[part].rearrange("q (m p) t -> p (q m) t", p=P)[:, :, ds(i * P, P)],
                                 (hi_st, lo_st)[part][:].rearrange("p (s t) -> p s t", s=4).bitcast(F32)).then_inc(qk_stored, 16)

            load_x(0, 0)
            load_x(1, 1)
            with sp.Fori(0, NT // 2 - 1) as it:
                for u in range(2):
                    i = it * 2 + u
                    sp.wait_ge(x1_ready, i + 1)
                    load_x(i + 2, u)
                    store_qk(i)
            store_qk(NT - 2)
            store_qk(NT - 1)
            sp.wait_ge(qk_stored, 2 * 16 * NT + 32)
            sp.wait_ge(k_ones, 2)
            sp.sem_inc(xst_mm, 32)

            def load_quad(qd, b):
                i = qd * 2 + b
                sp.wait_ge(xst_mm, 16 * i + 16)
                for side, dst, parts in ((0, q_op[b], (0, 0, 1, 1)), (1, kx_op[b], (0, 1, 0, 1))):
                    for r, part in enumerate(parts):
                        sp.dma_start(dst[r * X_HD:(r + 1) * X_HD].bitcast(F32),
                                     qk_scr[part, side, ds(qd * NQ * X_HD, NQ * X_HD), b * S:(b + 1) * S].rearrange("(j d) n -> d j n", j=NQ)
                                     ).then_inc(xq_loaded[b], 16)

            def load_max(qd, b):
                i = qd * 2 + b
                sp.wait_ge(xm_hi, i + 1)
                sp.wait_ge(xm_lo, i + 1)
                for r, src in ((X_MAX, m_hi), (X_MAX + 1, m_lo)):
                    sp.dma_start(q_op[b][r:r + 1].rearrange("o j n -> o (j n)").bitcast(F32), src[:].bitcast(F32)).then_inc(xm_loaded[b], 16)

            def store_y(qd, b):
                i = qd * 2 + b
                sp.wait_ge(xatt_ready, i + 1)
                for j in range(NQ):
                    sp.dma_start(y_scr[ds(qd * NQ * X_HD + j * X_HD, X_HD), b * S:(b + 1) * S], att[j * 32:j * 32 + X_HD, :]).then_inc(y_stored, 16)

            load_quad(0, 0)
            load_quad(0, 1)
            load_max(0, 0)
            with sp.Fori(0, X_QUADS - 1) as qd:
                load_max(qd, 1)
                load_quad(qd + 1, 0)
                store_y(qd, 0)
                load_max(qd + 1, 0)
                load_quad(qd + 1, 1)
                store_y(qd, 1)
            load_max(X_QUADS - 1, 1)
            store_y(X_QUADS - 1, 0)
            store_y(X_QUADS - 1, 1)
            sp.wait_ge(y_stored, 16 * NQ * XI + 16)
            sp.wait_ge(lora_stored, 16 * (NT + 2))
            sp.dma_start(write1, d["write1"]).then_inc(w2_loaded, 16)
            sp.dma_start(write2, d["write2"]).then_inc(w2_loaded, 16)
            sp.dma_start(read2, d["read2"]).then_inc(w2_loaded, 16)
            for n in range(2):
                sp.dma_start(du[n], d[f"du{n + 1}"]).then_inc(w2_loaded, 16)
            sp.dma_start(kern, d["kern"]).then_inc(kern_loaded, 16)
            sp.dma_start(lora_at[:, :, RANK:], d["lora_as"]).then_inc(kern_loaded, 16)
            sp.dma_start(lora_bt[RANK:R2, :], d["lora_bs"]).then_inc(kern_loaded, 16)
            sp.sem_inc(f_mm, 1)
            sp.sem_inc(W["w_mm"], 2)
            with sp.Fori(0, NT) as i:
                sp.wait_ge(W["w_mm"], 2 * i + 1)
                sp.dma_start(yT, y_scr.rearrange("(k p) t -> p k t", p=P)[:, :, ds(i * P, P)]).then_inc(yT_loaded, 16)
                sp.wait_ge(f_mm, i + 1)
                sp.dma_start(lora_at[:, :, 0:RANK], a_scr[ds(i, 1)].rearrange("o p (c r) -> (o p) c r", c=KC)).then_inc(lo_loaded, 16)
                sp.dma_start(lora_bt[0:RANK, :], b_scr[ds(i * RANK, RANK), :]).then_inc(lo_loaded, 16)
                sp.wait_ge(out_ready, i + 1)
                sp.dma_start(out[ds(i * P, P), :], out_t).then_inc(out_stored, 16)
            sp.wait_ge(out_stored, 16 * NT + 16)

        @block.gpsimd
        def _(pool):
            pool.memset(ident[:], 0.0).then_inc(made, 1)
            pool.memset(ident_bf[:], 0.0).then_inc(made, 1)
            pool.memset(mask_qk[:], 0.0).then_inc(made, 1)
            pool.memset(mask_kq[:], 0.0).then_inc(made, 1)
            pool.memset(mean_w, 1.0 / D).then_inc(made, 1)
            pool.memset(ones32[:], 1.0).then_inc(made, 1)
            pool.memset(minus_half[:], -0.5).then_inc(made, 1)
            pool.wait_ge(made, 4)
            for t in (ident, ident_bf):
                pool.affine_select(out=t[:], in_=t[:], compare_op=ALU.not_equal, fill=1.0, base=0,
                                   pattern=[[-1, P]], channel_multiplier=1).then_inc(made, 1)
            pool.affine_select(out=mask_qk[:], in_=mask_qk[:], compare_op=ALU.is_ge, fill=-1e30, base=0,
                               pattern=[[-1, P]], channel_multiplier=1).then_inc(made, 1)
            pool.affine_select(out=mask_kq[:], in_=mask_kq[:], compare_op=ALU.is_ge, fill=-1e30, base=0,
                               pattern=[[1, P]], channel_multiplier=-1).then_inc(made, 1)
            for u in range(2):
                pool.memset(q_op[u][:].bitcast(F32), 0.0).then_inc(made, 1)
            pool.memset(kr[:].bitcast(F32), 0.0).then_inc(made, 1)
            pool.wait_ge(made, 14)
            for u in range(2):
                pool.memset(k_op[u][A_MAX:A_ROWS, :].bitcast(F32), 1.0).then_inc(made, 1)
            pool.wait_ge(made, 16)
            with pool.Fori(0, NT // 2) as it:
                for u in range(2):
                    i = it * 2 + u
                    pool.wait_ge(ln_step, 4 * i + 4)
                    pool.tensor_tensor(rstd[:, u, :], ve[:, u, :], minus_half[:, 0:1], ALU.pow).then_inc(ln_rstd, 1)

            def values(g, b):
                i = g * 2 + b
                pool.wait_ge(pv_done, 4 * i + 4)
                pool.tensor_copy(v_g[:, b], v_all[:, b * QT:(b + 1) * QT, ds(g * A_HD, A_HD)]).then_inc(vg_ready, 1)

            def normalise(g, b):
                i = g * 2 + b
                pool.wait_ge(den_rec, i + 1)
                pool.wait_ge(att_lo_ready, i + 1)
                pool.tensor_tensor(att, o_sb, den_sb, ALU.mult).then_inc(att_ready, 1)
                pool.wait_ge(att_hi_ready, i + 1)
                hi = attT_hi[:, ds(g, 1), b * S:(b + 1) * S]
                lo = attT_lo[:, ds(g, 1), b * S:(b + 1) * S]
                pool.tensor_tensor(lo, att.unsqueeze(1), hi, ALU.subtract).then_inc(att_lo_ready, 1)

            pool.sem_inc(att_lo_ready, 1)
            pool.wait_ge(v_ready, NT + 2)
            values(0, 0)
            values(0, 1)
            with pool.Fori(0, A_KV - 1) as g:
                normalise(g, 0)
                values(g + 1, 0)
                normalise(g, 1)
                values(g + 1, 1)
            normalise(A_KV - 1, 0)
            normalise(A_KV - 1, 1)
            pool.wait_ge(att_lo_ready, NI + 1)
            pool.wait_ge(pv_done, 8 + QT * NI)
            pool.sem_inc(xatt_free, 1)
            pool.memset(v_x, 0.0).then_inc(vx_zero, 1)
            with pool.Fori(0, NT) as i:
                pool.wait_ge(l_step, 5 * i + 5)
                pool.tensor_tensor(rstds[:, ds(i, 1)], ves[:], minus_half[:, 0:1], ALU.pow).then_inc(l_rstd, 1)
                pool.wait_ge(y_step, 10 * i + 10)
                pool.tensor_tensor(rs3[:], ve3[:], minus_half[:, 0:3], ALU.pow).then_inc(y_rstd, 1)
            pool.wait_ge(y_rstd, NT)
            pool.memset(kr[X_MAX:P, :].bitcast(F32), 0.0).then_inc(k_ones, 1)
            pool.wait_ge(k_ones, 1)
            pool.memset(kr[X_MAX:X_MAX + 2, :].bitcast(F32), 1.0).then_inc(k_ones, 1)

            def x_values(qd, b):
                i = qd * 2 + b
                pool.wait_ge(xpv_done, 4 * i + 4)
                pool.tensor_copy(v_q[:, b], v_x[:, b * QT:(b + 1) * QT, ds(qd * NQ * 32, NQ * 32)]).then_inc(xv_ready, 1)

            def x_normalise(qd, b):
                i = qd * 2 + b
                pool.wait_ge(xden_rec, i + 1)
                pool.wait_ge(y_stored, 16 * NQ * i + 16)
                pool.tensor_tensor(att, o_sb, den_sb, ALU.mult).then_inc(xatt_ready, 1)

            pool.wait_ge(k_ones, 2)
            pool.wait_ge(vx_ready, NT + 1)
            pool.wait_ge(qkv_mm, NT)
            pool.sem_inc(y_stored, 16)
            x_values(0, 0)
            x_values(0, 1)
            with pool.Fori(0, X_QUADS - 1) as qd:
                x_normalise(qd, 0)
                x_values(qd + 1, 0)
                x_normalise(qd, 1)
                x_values(qd + 1, 1)
            x_normalise(X_QUADS - 1, 0)
            x_normalise(X_QUADS - 1, 1)

            def write(k, i, h):
                n = 2 * i + k
                h3 = h.rearrange("p (s r c) -> p s r c", s=HS, r=RH)
                a3 = abar[:, 0:3 * H].rearrange("p (s r c) -> p s r c", s=HS, r=RH)
                pool.wait_ge(W["sp_ready"], n + 1)
                pool.tensor_tensor(a3, sp_b[:, 0:H].rearrange("p (s r) -> p s r", s=HS).unsqueeze(3).broadcast_to([P, HS, RH, C - 1]),
                                   sp_b[:, H:].rearrange("p (r c) -> p r c", r=RH).unsqueeze(1).broadcast_to([P, HS, RH, C - 1]),
                                   ALU.mult).then_inc(W["da_ready"], 1)
                pool.wait_ge(W["abar_ready"], n + 1)
                pool.tensor_tensor(h_a.rearrange("p (s r c) -> p s r c", s=HS, r=RH), h3[:, :, :, 0:C - 1], a3,
                                   ALU.mult).then_inc(W["ha_ready"], 1)

            with pool.Fori(0, NT) as i:
                write(0, i, h_in)
                pool.wait_ge(y2_step, 5 * i + 5)
                pool.tensor_tensor(rs3[:, 0:2], ve3[:, 0:2], minus_half[:, 0:2], ALU.pow).then_inc(y2_rstd, 1)
                write(1, i, h_mid)
                pool.wait_ge(f_step, 4 * i + 4)
                pool.tensor_tensor(rstd[:, 0, :], ves[:], minus_half[:, 0:1], ALU.pow).then_inc(f_rstd, 1)

        @block.scalar
        def _(act):
            with act.Fori(0, NT // 2) as it:
                for u in range(2):
                    i = it * 2 + u
                    act.wait_ge(w_qkv_loaded, 16 * (i + 1))
                    act.activation(sign_qkv[:, ds(i, 1), :], w_in_qkv.unsqueeze(1), ACT.Sign).then_inc(sign_q_done, 1)
                    act.wait_ge(w_o_loaded, 16 * (i + 1))
                    act.activation(sign_o[:, ds(i, 1), :], w_in_o.unsqueeze(1), ACT.Sign).then_inc(sign_o_done, 1)
                    act.wait_ge(xT_done, i + 3)
                    for h in range(2):
                        act.activation(xnT_hi[:, 4 * h:4 * h + 4, ds(i * P, P)],
                                       psum[:, 2 * u + h, :].rearrange("p (c n) -> p c n", c=4), ACT.Copy).then_inc(xT_hi, 1)
            for n in range(4):
                b, m = n // 2, n % 2
                act.wait_ge(k_mm, n + 1)
                act.wait_ge(c_ready, 4)
                if n:
                    act.wait_ge(k_stored, 32 * n)
                act.activation(hi_st[:], psum[:, n, :], ACT.Identity, scale=c_k[:, m:m + 1]).then_inc(k_hi_ready, 1)
            act.wait_ge(trig_done, 1)
            for k in range(2):
                act.activation(trig[:, k], trig_r[:, k], ACT.Sin).then_inc(trig_done, 1)
            act.wait_ge(trig_done, 2)
            act.activation(trig[:, 2], trig[:, 0], ACT.Copy, scale=-1.0).then_inc(trig_done, 1)
            act.wait_ge(k_stored, 128)
            for r in range(R4):
                act.wait_ge(lora_mm, r + 1)
                act.activation(a_eff[:, :, :, r * R8:(r + 1) * R8],
                               psum[:, r, :].rearrange("p (c b r) -> p b c r", c=KC, b=NT), ACT.Copy).then_inc(lora_ready, 1)
            act.wait_ge(lora_stored, 16 * (NT + 2))
            act.sem_inc(pv_done, 8)

            def q_hi(g, b, first=False):
                i = g * 2 + b
                act.wait_ge(q_mm, i + 1)
                if not first:
                    wait_apart(act, q_stacked[1 - b], 16 * 3 * A_REP * (g + b))
                act.activation(hi_st[:], psum[:, 0, :], ACT.Identity, scale=c_q[:, ds(g, 1)]).then_inc(q_hi_ready, 1)

            def max_hi(g, b, first=False):
                i = g * 2 + b
                act.wait_ge(mT_done, i + 1)
                if not first:
                    act.wait_ge(m_loaded[1 - b], 32 * (g + b))
                act.activation(m_hi[:], psum[0:16, 1, 0:P], ACT.Copy).then_inc(m_hi_ready, 1)

            def exps(g, b, kts):
                i = g * 2 + b
                for kt in kts:
                    act.wait_ge(pv_done, 4 * i + kt + 7)
                    for j in range(A_REP):
                        n = 4 * kt + j
                        act.wait_ge(st_mm, 16 * i + n + 33)
                        act.activation(prob[:, kt % 2, j, :], psum[:, 4 + n % 2, :], ACT.Exp, scale=A_SCALE).then_inc(p_ready, 1)

            def copy_out(g, b, first=False):
                i = g * 2 + b
                act.wait_ge(pv_done, 4 * i + 12)
                if not first:
                    act.wait_ge(att_ready, i)
                act.activation(o_sb, psum[:, 6, :], ACT.Copy).then_inc(o_copied, 1)
                act.activation(den_sb, psum[:, 7, :], ACT.Copy).then_inc(o_copied, 1)

            def att_hi(g, b):
                i = g * 2 + b
                act.wait_ge(att_ready, i + 1)
                act.activation(attT_hi[:, ds(g, 1), b * S:(b + 1) * S], att.unsqueeze(1), ACT.Copy).then_inc(att_hi_ready, 1)

            def step(g, b, g1, b1, g2, first=False):
                exps(g, b, (0, 1))
                if g2 is not None:
                    q_hi(g2, b)
                exps(g, b, (2, 3))
                if not first:
                    att_hi(*((g, 0) if b else (g - 1, 1)))
                copy_out(g, b, first)
                if g1 is not None:
                    max_hi(g1, b1)

            q_hi(0, 0, True)
            q_hi(0, 1)
            max_hi(0, 0, True)
            step(0, 0, 0, 1, 1, True)
            step(0, 1, 1, 0, 1)
            with act.Fori(1, A_KV - 1) as g:
                step(g, 0, g, 1, g + 1)
                step(g, 1, g + 1, 0, g + 1)
            step(A_KV - 1, 0, A_KV - 1, 1, None)
            step(A_KV - 1, 1, None, None, None)
            att_hi(A_KV - 1, 1)
            act.wait_ge(vx_zero, 1)
            g0, b0 = COLS["g1"][0], COLS["b1"][0]
            act.sem_inc(qk_stored, 32)
            with act.Fori(0, NT) as i:
                act.wait_ge(hT_mm, i + 1)
                for h in range(2):
                    act.activation(hT[:, 4 * h:4 * h + 4, :], psum[:, 2 + h, :].rearrange("p (c n) -> p c n", c=4), ACT.Copy).then_inc(hT_ready, 1)
                act.wait_ge(ynT_mm, i + 1)
                for n in range(6):
                    act.activation(ynT[:, n, :], psum[:, 6 + n // 4, (n % 4) * P:(n % 4 + 1) * P], ACT.Identity,
                                   scale=cols[:, g0 + n:g0 + n + 1], bias=cols[:, b0 + n:b0 + n + 1]).then_inc(ynT_ready, 1)
                act.wait_ge(qkv_mm, i + 1)
                act.activation(v_x[:, ds(i, 1), :].rearrange("p o (h e) -> p (o h) e", e=32)[:, :, 0:X_HD],
                               psum[:, 3, 0:H].rearrange("p (h e) -> p h e", e=X_HD), ACT.Copy).then_inc(vx_ready, 1)
                act.wait_ge(rT_mm, i + 2)
                act.wait_ge(qk_stored, 32 * i + 32)
                act.activation(hi_st[:], psum[:, 4, :], ACT.Copy).then_inc(r_hi, 1)
            act.sem_inc(xpv_done, 8)

            def x_max_hi(qd, b, first=False):
                i = qd * 2 + b
                act.wait_ge(xmT_done, i + 1)
                if not first:
                    act.wait_ge(xm_loaded[1 - b], 32 * (qd + b))
                act.activation(m_hi[:], psum[0:16, 1, 0:P], ACT.Copy).then_inc(xm_hi, 1)

            def x_step(qd, b, q1, b1, first=False):
                i = qd * 2 + b
                for kt in range(QT):
                    act.wait_ge(xpv_done, 4 * i + kt + 7)
                    for j in range(NQ):
                        n = 4 * kt + j
                        act.wait_ge(xst_mm, 16 * i + n + 33)
                        act.activation(prob[:, kt % 2, j, 0:S - kt * P], psum[:, 4 + n % 2, 0:S - kt * P], ACT.Exp, scale=X_SCALE).then_inc(xp_ready, 1)
                act.wait_ge(xpv_done, 4 * i + 12)
                if not first:
                    act.wait_ge(xatt_ready, i)
                act.activation(o_sb, psum[:, 6, :], ACT.Copy).then_inc(xo_copied, 1)
                act.activation(den_sb, psum[:, 7, :], ACT.Copy).then_inc(xo_copied, 1)
                if q1 is not None:
                    x_max_hi(q1, b1)

            x_max_hi(0, 0, True)
            x_step(0, 0, 0, 1, True)
            x_step(0, 1, 1, 0)
            with act.Fori(1, X_QUADS - 1) as qd:
                x_step(qd, 0, qd, 1)
                x_step(qd, 1, qd + 1, 0)
            x_step(X_QUADS - 1, 0, X_QUADS - 1, 1)
            x_step(X_QUADS - 1, 1, None, None)

            def write(k, i):
                n = 2 * i + k
                act.wait_ge(W["w_mm"], n + 3)
                act.activation(low[:], psum[0:DR, 1, 0:P], ACT.Copy).then_inc(W["low_ready"], 1)
                act.wait_ge(W["az_ready"], n + 1)
                act.activation(e_b, e_b, ACT.Exp, scale=-1.0).then_inc(W["e_ready"], 1)
                act.wait_ge(W["e_ready"], n + 1)
                act.activation(e_b, e_b, ACT.Ln, bias=1.0).then_inc(W["l_ready"], 1)
                act.wait_ge(W["da_ready"], n + 1)
                act.activation(abar[:, 0:3 * H], abar[:, 0:3 * H], ACT.Exp, scale=-1.0).then_inc(W["abar_ready"], 1)

            g0, b0 = COLS["g2"][0], COLS["b2"][0]
            with act.Fori(0, NT) as i:
                write(0, i)
                act.wait_ge(h2T_mm, i + 1)
                for h in range(2):
                    act.activation(hT[:, 4 * h:4 * h + 4, :], psum[:, 2 + h, :].rearrange("p (c n) -> p c n", c=4), ACT.Copy).then_inc(h2T_ready, 1)
                act.wait_ge(y2T_mm, i + 1)
                for n in range(4):
                    act.activation(ynT[:, n, :], psum[:, 5, n * P:(n + 1) * P], ACT.Identity,
                                   scale=cols[:, g0 + n:g0 + n + 1], bias=cols[:, b0 + n:b0 + n + 1]).then_inc(y2T_ready, 1)
                act.wait_ge(gu_mm, i + 1)
                act.activation(tanh_b.rearrange("p (h n) -> p h n", h=2), psum[:, 6:8, :], ACT.Tanh, scale=0.5).then_inc(tanh_ready, 1)
                write(1, i)
                act.wait_ge(fT_mm, i + 1)
                for h in range(2):
                    act.activation(hT[:, 4 * h:4 * h + 4, :], psum[:, 2 + h, :].rearrange("p (c n) -> p c n", c=4), ACT.Copy).then_inc(fT_ready, 1)
                act.wait_ge(ax_mm, i + 1)
                act.activation(ax, psum[:, 5, 0:R2], ACT.Copy).then_inc(ax_ready, 1)
                act.wait_ge(axT_mm, i + 1)
                act.activation(axT, psum[0:R2, 5, 256:256 + P], ACT.Copy).then_inc(axT_ready, 1)

        @block.vector
        def _(dve):
            dve.memset(w_abs, 0.0).then_inc(abs_done, 2)
            dve.wait_ge(s_const, 64)
            dve.tensor_copy(pos_f[:], pos_i[:]).then_inc(ang_step, 1)
            dve.wait_ge(ang_step, 1)
            for f in range(HALF):
                dve.tensor_scalar(ang[:, :, f], pos_f[:], float(ROPE_INV[f]), None, ALU.mult).then_inc(ang_step, 1)
            dve.wait_ge(ang_step, 1 + HALF)
            n_step = 1 + HALF

            def link(ins):
                nonlocal n_step
                ins.then_inc(ang_step, 1)
                n_step += 1
                dve.wait_ge(ang_step, n_step)

            for k in range(2):
                n, r = trig_n[:, k], trig_r[:, k]
                link(dve.tensor_scalar(n, ang, float(1 / TWO_PI), 0.25 * k, ALU.mult, ALU.add))
                link(dve.tensor_scalar(n, n, MAGIC, None, ALU.add))
                link(dve.tensor_scalar(n, n, -MAGIC, None, ALU.add))
                link(dve.scalar_tensor_tensor(r, n, -TP1, ang, ALU.mult, ALU.add))
                link(dve.scalar_tensor_tensor(r, n, -TP2, r, ALU.mult, ALU.add))
                link(dve.scalar_tensor_tensor(r, n, -TP3, r, ALU.mult, ALU.add))
                link(dve.tensor_scalar(r, r, float(k * np.pi / 2), 3.1415925, ALU.add, ALU.min))
                link(dve.tensor_scalar(r, r, -3.1415925, None, ALU.max))
            dve.sem_inc(trig_done, 1)

            with dve.Fori(0, NT // 2) as it:
                for u in range(2):
                    i = it * 2 + u
                    dve.wait_ge(x_slot[u], 16 * (it + 1))
                    for h in range(2):
                        dve.bn_stats(st[:, u, h, :], x_in[:, u, h * 512:(h + 1) * 512]).then_inc(ln_step, 1)
                    wait_apart(dve, ln_step, 4 * i + 2)
                    dve.bn_aggr(mv[:, u, :], st[:, u]).then_inc(ln_step, 1)
                    dve.wait_ge(ln_step, 4 * i + 3)
                    dve.tensor_scalar(ve[:, u, :], mv[:, u, 1:2], LN_EPS, None, ALU.add).then_inc(ln_step, 1)
                    dve.wait_ge(ln_rstd, i + 1)
                    dve.tensor_scalar(x_in[:, u, :], x_in[:, u, :], mv[:, u, 0:1], rstd[:, u, 0:1],
                                      ALU.subtract, ALU.mult).then_inc(xn_ready, 1)
                    dve.wait_ge(sign_q_done, i + 2)
                    dve.tensor_scalar(w_in_qkv.bitcast(I32), w_in_qkv.bitcast(I32), 0x7FFFFFFF, None, ALU.bitwise_and).then_inc(abs_taken, 1)
                    dve.wait_ge(sign_o_done, i + 2)
                    dve.tensor_scalar(w_in_o.bitcast(I32), w_in_o.bitcast(I32), 0x7FFFFFFF, None, ALU.bitwise_and).then_inc(abs_taken, 1)
                    dve.wait_ge(abs_done, 2 * i + 2)
                    dve.wait_ge(abs_taken, 2 * i + 2)
                    dve.tensor_tensor(w_abs[:, 0:QKV], w_in_qkv, w_abs[:, 0:QKV], ALU.add).then_inc(abs_done, 1)
                    dve.tensor_tensor(w_abs[:, QKV:], w_in_o, w_abs[:, QKV:], ALU.add).then_inc(abs_done, 1)
                    for h in range(2):
                        dve.wait_ge(xT_hi, 2 * i + h + 1)
                        dve.tensor_tensor(xnT_lo[:, 4 * h:4 * h + 4, ds(i * P, P)],
                                          psum[:, 2 * u + h, :].rearrange("p (c n) -> p c n", c=4),
                                          xnT_hi[:, 4 * h:4 * h + 4, ds(i * P, P)], ALU.subtract).then_inc(xT_free, 1)
            dve.wait_ge(means_done, 1)
            for h in range(2):
                dve.scalar_tensor_tensor(c_o[:, h * 512:(h + 1) * 512], psum[:, 4 + h, :], 1e-8,
                                         scale_rows[:, KVD + h * 512:KVD + (h + 1) * 512], ALU.max, ALU.mult).then_inc(c_ready, 1)
            dve.scalar_tensor_tensor(c_v, psum[:, 6, 0:KVD], 1e-8, scale_rows[:, 0:KVD], ALU.max, ALU.mult).then_inc(c_ready, 1)
            dve.scalar_tensor_tensor(c_k[:], psum[:, 7, KC:KC + 2], 1e-8, cols[:, slice(*COLS["k_scale"])], ALU.max, ALU.mult).then_inc(c_ready, 1)
            dve.scalar_tensor_tensor(c_q[:], psum[:, 7, 0:KC], 1e-8, cols[:, slice(*COLS["q_scale"])], ALU.max, ALU.mult).then_inc(c_ready, 1)
            dve.wait_ge(c_ready, 5)
            for n in range(4):
                m = n % 2
                dve.wait_ge(k_hi_ready, n + 1)
                dve.scalar_tensor_tensor(lo_st[:], psum[:, n, :], c_k[:, m:m + 1], hi_st[:].bitcast(F32), ALU.mult, ALU.subtract).then_inc(k_lo_ready, 1)
            with dve.Fori(0, NT // 2) as it:
                for u in range(2):
                    i = it * 2 + u
                    dve.wait_ge(v_mm, i + 1)
                    dve.scalar_tensor_tensor(v_all[:, ds(i, 1), :], psum[:, 4 + u, 0:KVD].unsqueeze(1), V_GAIN, c_v.unsqueeze(1),
                                             ALU.mult, ALU.mult).then_inc(v_ready, 1)
            dve.wait_ge(trig_done, 4)
            for m in range(2):
                for h in range(2):
                    dve.wait_ge(lora_mm, R4 + 2 * m + h + 1)
                    dve.tensor_copy(b_eff[:, m, h * 512:(h + 1) * 512], psum[:, 4 + 2 * m + h, :]).then_inc(lora_ready, 1)

            def q_lo(g, b):
                i = g * 2 + b
                dve.wait_ge(q_hi_ready, i + 1)
                dve.scalar_tensor_tensor(lo_st[:], psum[:, 0, :], c_q[:, ds(g, 1)], hi_st[:].bitcast(F32), ALU.mult, ALU.subtract).then_inc(q_lo_ready, 1)

            def maxima(g, b):
                i = g * 2 + b
                for n in range(16):
                    dve.wait_ge(s_mm, 16 * i + n + 1)
                    dve.tensor_reduce(m_neg[:, b, n:n + 1], psum[:, 2 + n % 2, :], AX_X, ALU.max, negate=True).then_inc(s_max, 1)

            def max_lo(g, b):
                i = g * 2 + b
                dve.wait_ge(m_hi_ready, i + 1)
                dve.tensor_tensor(m_lo[:], psum[0:16, 1, 0:P], m_hi[:].bitcast(F32), ALU.subtract).then_inc(m_lo_ready, 1)

            def invert(g, b):
                i = g * 2 + b
                dve.wait_ge(o_copied, 2 * i + 2)
                dve.reciprocal(den_sb, den_sb).then_inc(den_rec, 1)

            def step(g, b, g1, b1, g2, first=False):
                if g1 is not None:
                    maxima(g1, b1)
                if not first:
                    invert(*((g, 0) if b else (g - 1, 1)))
                if g2 is not None:
                    q_lo(g2, b)
                if g1 is not None:
                    max_lo(g1, b1)

            q_lo(0, 0)
            q_lo(0, 1)
            maxima(0, 0)
            max_lo(0, 0)
            step(0, 0, 0, 1, 1, True)
            step(0, 1, 1, 0, 1)
            with dve.Fori(1, A_KV - 1) as g:
                step(g, 0, g, 1, g + 1)
                step(g, 1, g + 1, 0, g + 1)
            step(A_KV - 1, 0, A_KV - 1, 1, None)
            step(A_KV - 1, 1, None, None, None)
            invert(A_KV - 1, 1)

            dve.wait_ge(trig_done, 4)
            def residual(i, u, use, h_done):
                for h in range(2):
                    dve.wait_ge(op_mm, 2 * i + h + 1)
                    if h == 0 and h_done is not None:
                        dve.wait_ge(hT_mm, h_done)
                    dve.scalar_tensor_tensor(y0[:, h * 512:(h + 1) * 512], psum[:, h, :], 1.0 / V_GAIN, c_o[:, h * 512:(h + 1) * 512],
                                             ALU.mult, ALU.mult).then_inc(y0_ready, 1)
                dve.wait_ge(y0_ready, 2 * i + 4)
                dve.wait_ge(x_again[u], 16 * use)
                dve.tensor_tensor(x1[:, ds(i, 1), :], y0.unsqueeze(1), x_in[:, u:u + 1, :], ALU.add).then_inc(x1_ready, 1)
                wait_apart(dve, x1_ready, i + 1)
                for h in range(2):
                    dve.bn_stats(st[:, 0, h, :], x1[:, ds(i, 1), h * 512:(h + 1) * 512]).then_inc(l_step, 1)
                wait_apart(dve, l_step, 5 * i + 2)
                dve.bn_aggr(mv[:, 0, :], st[:, 0]).then_inc(l_step, 1)
                dve.wait_ge(l_step, 5 * i + 3)
                dve.tensor_copy(mvs[:, ds(2 * i, 2)], mv[:, 0, :]).then_inc(l_step, 1)
                dve.tensor_scalar(ves[:], mv[:, 0, 1:2], LN_EPS, None, ALU.add).then_inc(l_step, 1)
                dve.wait_ge(l_rstd, i + 1)
                dve.tensor_scalar(h_st, x1[:, ds(i, 1), :].rearrange("p o n -> p (o n)"), mvs[:, ds(2 * i, 1)], rstds[:, ds(i, 1)],
                                  ALU.subtract, ALU.mult).then_inc(h_ready, 1)

            def read(i):
                dve.wait_ge(y_mm, i + 1)
                y = [psum[:, 4 + h, 0:4 * 3 * HC].rearrange("p (c o n) -> p c o n", c=4, o=3) for h in range(2)]
                for o in range(3):
                    for h in range(2):
                        dve.bn_stats(st3[:, o, h, :], y[h][:, :, o, :]).then_inc(y_step, 1)
                wait_apart(dve, y_step, 10 * i + 6)
                for o in range(3):
                    dve.bn_aggr(mv3[:, o, :], st3[:, o]).then_inc(y_step, 1)
                dve.wait_ge(y_step, 10 * i + 9)
                dve.tensor_scalar(ve3[:], mv3[:, :, 1], LN_EPS, None, ALU.add).then_inc(y_step, 1)
                dve.wait_ge(y_rstd, i + 1)
                dve.wait_ge(rT_mm, i + 1)
                for o in range(3):
                    for h in range(2):
                        dve.tensor_scalar(yn[:, o * H + h * P:o * H + (h + 1) * P].rearrange("p (c n) -> p c n", c=4), y[h][:, :, o, :],
                                          mv3[:, o, 0:1], rs3[:, o:o + 1], ALU.subtract, ALU.mult).then_inc(yn_ready, 1)

            def rope(i):
                dve.wait_ge(qkv_mm, i + 1)
                qk = psum[:, 2, :].rearrange("p (h e f) -> p h e f", e=2, f=HALF)
                to = rot.rearrange("p (h e f) -> p h e f", e=2, f=HALF)
                other = rope_a.rearrange("p (h f) -> p h f", f=HALF)

                def angle(k):
                    return trig[:, k, ds(i, 1), :].broadcast_to([P, 2 * X_NH, HALF])

                for e in range(2):
                    dve.tensor_tensor(to[:, :, e, :], qk[:, :, e, :], angle(1), ALU.mult).then_inc(rope_step, 1)
                for e in range(2):
                    dve.tensor_tensor(other, qk[:, :, 1 - e, :], angle(0 if e else 2), ALU.mult).then_inc(rope_step, 1)
                    dve.wait_ge(rope_step, 6 * i + 9 + 2 * e)
                    dve.tensor_tensor(to[:, :, e, :], to[:, :, e, :], other, ALU.add).then_inc(rope_step, 1)
                    dve.wait_ge(rope_step, 6 * i + 10 + 2 * e)

            def split(i):
                dve.wait_ge(r_hi, i + 1)
                dve.tensor_tensor(lo_st[:], psum[:, 4, :], hi_st[:].bitcast(F32), ALU.subtract).then_inc(r_lo, 1)

            dve.sem_inc(rT_mm, 1)
            dve.sem_inc(y0_ready, 2)
            residual(0, 0, 1, None)
            with dve.Fori(0, NT // 2 - 1) as it:
                for u in range(2):
                    i = it * 2 + u
                    read(i)
                    rope(i)
                    split(i)
                    residual(i + 1, 1 - u, it + 1 + u, i + 1)
            read(NT - 2)
            rope(NT - 2)
            split(NT - 2)
            residual(NT - 1, 1, NT // 2, NT - 1)
            read(NT - 1)
            rope(NT - 1)
            split(NT - 1)

            def x_maxima(qd, b):
                i = qd * 2 + b
                for n in range(16):
                    dve.wait_ge(xs_mm, 16 * i + n + 1)
                    dve.tensor_reduce(m_neg[:, b, n:n + 1], psum[:, 2 + n % 2, 0:(n % QT + 1) * P], AX_X, ALU.max, negate=True).then_inc(xs_max, 1)

            def x_max_lo(qd, b):
                i = qd * 2 + b
                dve.wait_ge(xm_hi, i + 1)
                dve.tensor_tensor(m_lo[:], psum[0:16, 1, 0:P], m_hi[:].bitcast(F32), ALU.subtract).then_inc(xm_lo, 1)

            def x_invert(qd, b):
                i = qd * 2 + b
                dve.wait_ge(xo_copied, 2 * i + 4)
                dve.reciprocal(den_sb, den_sb).then_inc(xden_rec, 1)

            def x_step(qd, b, q1, b1, first=False):
                if q1 is not None:
                    x_maxima(q1, b1)
                if not first:
                    x_invert(*((qd, 0) if b else (qd - 1, 1)))
                if q1 is not None:
                    x_max_lo(q1, b1)

            x_maxima(0, 0)
            x_max_lo(0, 0)
            x_step(0, 0, 0, 1, True)
            x_step(0, 1, 1, 0)
            with dve.Fori(1, X_QUADS - 1) as qd:
                x_step(qd, 0, qd, 1)
                x_step(qd, 1, qd + 1, 0)
            x_step(X_QUADS - 1, 0, X_QUADS - 1, 1)
            x_step(X_QUADS - 1, 1, None, None)
            x_invert(X_QUADS - 1, 1)

            def write(k, i, h, to):
                n = 2 * i + k
                wab = rows[:, slice(*ROWS[f"wab{k + 1}"])]
                mid = [HS, RH, C - 1]
                h4 = h.rearrange("p (s r c) -> p s r c", s=HS, r=RH)
                to4 = to.rearrange("p (s r c) -> p s r c", s=HS, r=RH)
                o2 = psum[:, 0, 0:H].rearrange("p (s r) -> p s r", s=HS)
                bb3 = bbar[:, 0:3 * H].rearrange("p (s r c) -> p s r c", s=HS, r=RH)
                bs2 = b_skip.rearrange("p (s r) -> p s r", s=HS)
                dve.wait_ge(W["du_mm"], n + 1)
                dve.tensor_tensor(z_b[:, 0:H], psum[:, 1, H:2 * H], rows[:, slice(*ROWS[f"du{k + 1}"])], ALU.add).then_inc(W["z_ready"], 1)
                dve.tensor_tensor(z_b[:, H:], psum[:, 0, H:N_Z], wab[:, 0:N_A], ALU.add).then_inc(W["z_ready"], 1)
                dve.tensor_tensor(ab_b, psum[:, 0, N_Z:H + N_AB], wab[:, N_A:], ALU.add).then_inc(W["z_ready"], 1)
                dve.wait_ge(W["z_ready"], 3 * n + 3)
                dve.scalar_tensor_tensor(e_b, z_b, -1.0, z_b, ALU.mult, ALU.max).then_inc(W["az_ready"], 1)
                dve.wait_ge(W["l_ready"], n + 1)
                dve.scalar_tensor_tensor(sp_b[:], z_b, 0.0, e_b, ALU.max, ALU.add).then_inc(W["sp_ready"], 1)
                dve.wait_ge(W["sp_ready"], n + 1)
                dve.tensor_scalar(rc_b, sp_b[:, H:], SSM_EPS, None, ALU.add).then_inc(W["r_step"], 1)
                dve.wait_ge(W["r_step"], 3 * n + 1)
                dve.reciprocal(rc_b, rc_b).then_inc(W["r_step"], 1)
                dve.wait_ge(W["r_step"], 3 * n + 2)
                dve.scalar_tensor_tensor(r_b, ab_b[:, 0:N_A], -1.0, rc_b, ALU.mult, ALU.mult).then_inc(W["r_step"], 1)
                dve.tensor_tensor(bs2, sp_b[:, 0:H].rearrange("p (s r) -> p s r", s=HS),
                                  ab_b[:, N_A:].unsqueeze(1).broadcast_to([P, HS, RH]), ALU.mult).then_inc(W["b_step"], 1)
                dve.wait_ge(W["b_step"], 4 * n + 1)
                dve.tensor_tensor(bs2, bs2, o2, ALU.mult).then_inc(W["b_step"], 1)
                dve.wait_ge(W["b_step"], 4 * n + 2)
                dve.tensor_tensor(to4[:, :, :, C - 1], h4[:, :, :, C - 1], bs2, ALU.add).then_inc(W["hn_ready"], 1)
                dve.wait_ge(W["abar_ready"], n + 1)
                dve.wait_ge(W["r_step"], 3 * n + 3)
                dve.scalar_tensor_tensor(bbar[:, 0:3 * H].rearrange("p (s n) -> p s n", s=HS), abar[:, 0:3 * H].rearrange("p (s n) -> p s n", s=HS),
                                         -1.0, r_b.unsqueeze(1).broadcast_to([P, HS, N_A]), ALU.add, ALU.mult).then_inc(W["b_step"], 1)
                dve.wait_ge(W["b_step"], 4 * n + 3)
                dve.tensor_tensor(bb3, bb3, o2.unsqueeze(3).broadcast_to([P] + mid), ALU.mult).then_inc(W["b_step"], 1)
                dve.wait_ge(W["b_step"], 4 * n + 4)
                dve.wait_ge(W["ha_ready"], n + 1)
                dve.tensor_tensor(to4[:, :, :, 0:C - 1], h_a.rearrange("p (s r c) -> p s r c", s=HS, r=RH), bb3, ALU.add).then_inc(W["hn_ready"], 1)

            dve.sem_inc(out_stored, 16)
            with dve.Fori(0, NT) as i:
                x1_t = x1[:, ds(i, 1), :].rearrange("p o n -> p (o n)")
                dve.tensor_scalar(h_in, x1_t, mvs[:, ds(2 * i, 1)], rstds[:, ds(i, 1)], ALU.subtract, ALU.mult).then_inc(h2_ready, 1)
                dve.wait_ge(h2_ready, i + 1)
                write(0, i, h_in, h_mid)
                dve.wait_ge(y2_mm, i + 1)
                y = psum[:, 4, :].rearrange("p (c o n) -> p c o n", c=KC, o=2)
                for o in range(2):
                    dve.bn_stats(st3[:, o, 0, :], y[:, :, o, :]).then_inc(y2_step, 1)
                wait_apart(dve, y2_step, 5 * i + 2)
                for o in range(2):
                    dve.bn_aggr(mv3[:, o, :], st3[:, o, 0, :]).then_inc(y2_step, 1)
                dve.wait_ge(y2_step, 5 * i + 4)
                dve.tensor_scalar(ve3[:, 0:2], mv3[:, 0:2, 1], LN_EPS, None, ALU.add).then_inc(y2_step, 1)
                dve.wait_ge(y2_rstd, i + 1)
                for o in range(2):
                    dve.tensor_scalar(yn[:, o * H:(o + 1) * H].rearrange("p (c n) -> p c n", c=KC), y[:, :, o, :],
                                      mv3[:, o, 0:1], rs3[:, o:o + 1], ALU.subtract, ALU.mult).then_inc(y2n_ready, 1)
                dve.wait_ge(tanh_ready, i + 1)
                t2 = tanh_b.rearrange("p (h n) -> p h n", h=2)
                dve.scalar_tensor_tensor(t2, t2, 1.0, psum[:, 6:8, :], ALU.add, ALU.mult).then_inc(g_ready, 1)
                dve.wait_ge(g_ready, i + 1)
                dve.scalar_tensor_tensor(mlpT_f.rearrange("p (h n) -> p h n", h=2), t2, 0.5, psum[:, 2:4, :], ALU.mult, ALU.mult).then_inc(mlp_ready, 1)
                write(1, i, h_mid, h_out)
                dve.wait_ge(W["hn_ready"], 4 * i + 4)
                dve.tensor_tensor(x1_t, x1_t, h_out, ALU.add).then_inc(x2_ready, 1)
                wait_apart(dve, x2_ready, i + 1)
                for h in range(2):
                    dve.bn_stats(st[:, 0, h, :], x1[:, ds(i, 1), h * 512:(h + 1) * 512]).then_inc(f_step, 1)
                wait_apart(dve, f_step, 4 * i + 2)
                dve.bn_aggr(mv[:, 0, :], st[:, 0]).then_inc(f_step, 1)
                dve.wait_ge(f_step, 4 * i + 3)
                dve.tensor_scalar(ves[:], mv[:, 0, 1:2], LN_EPS, None, ALU.add).then_inc(f_step, 1)
                dve.wait_ge(f_rstd, i + 1)
                dve.tensor_scalar(h_out, x1_t, mv[:, 0, 0:1], rstd[:, 0, 0:1], ALU.subtract, ALU.mult).then_inc(xf_ready, 1)
                dve.wait_ge(f_mm, i + 2)
                dve.wait_ge(out_stored, 16 * i + 16)
                o3 = out_t.rearrange("p (h n) -> p h n", h=2)
                dve.tensor_tensor(o3, psum[:, 6:8, :], rows[:, slice(*ROWS["bias"])].rearrange("p (h n) -> p h n", h=2), ALU.add).then_inc(o_step, 1)
                dve.wait_ge(o_step, i + 1)
                dve.tensor_tensor(out_t, out_t, x1_t, ALU.add).then_inc(out_ready, 1)

        @block.tensor
        def _(pe):
            pe.sem_inc(xT_free, 4)
            pe.wait_ge(made, 11)
            with pe.Fori(0, NT // 2) as it:
                for u in range(2):
                    i = it * 2 + u
                    pe.wait_ge(xn_ready, i + 1)
                    pe.wait_ge(xT_free, 2 * i + 2)
                    for c in range(KC):
                        mm = pe.transpose(psum[:, 2 * u + c // 4, (c % 4) * P:(c % 4 + 1) * P], x_in[:, u, c * P:(c + 1) * P], ident[:])
                        if c == KC - 1:
                            mm.then_inc(xT_done, 1)
            pe.wait_ge(abs_done, 2 * NT + 2)
            for h in range(2):
                pe.matmul(psum[:, 4 + h, :], mean_w, w_abs[:, QKV + h * 512:QKV + (h + 1) * 512], start=True, stop=True)
            pe.matmul(psum[:, 6, 0:KVD], mean_w, w_abs[:, D + KVD:QKV], start=True, stop=True)
            for c in range(KC + 2):
                mm = pe.matmul(psum[:, 7, c:c + 1], w_abs[:, c * P:(c + 1) * P], mean_w[:, 0:1], start=True, stop=True)
            mm.then_inc(means_done, 1)
            pe.wait_ge(sign_q_done, NT + 1)
            pe.wait_ge(xT_free, 2 * NT + 4)

            def project(bank, width, weights, tokens, swap=False):
                for c in range(KC):
                    for part in range(2):
                        x = (xnT_hi, xnT_lo)[part]
                        w = weights(c)
                        mm = pe.matmul(psum[:, bank, 0:width], *((x[:, c, tokens], w) if swap else (w, x[:, c, tokens])),
                                       start=(c == 0 and part == 0), stop=(c == KC - 1 and part == 1))
                return mm

            for n in range(4):
                b, m = n // 2, n % 2
                project(n, S, lambda c: sign_qkv[:, c, D + m * P:D + (m + 1) * P], slice(b * S, (b + 1) * S)).then_inc(k_mm, 1)
            pe.wait_ge(c_ready, 5)
            pe.sem_inc(v_ready, 2)
            with pe.Fori(0, NT // 2) as it:
                for u in range(2):
                    i = it * 2 + u
                    pe.wait_ge(v_ready, i + 1)
                    project(4 + u, KVD, lambda c: sign_qkv[:, c, D + KVD:QKV], ds(i * P, P), swap=True).then_inc(v_mm, 1)
            pe.wait_ge(k_lo_ready, 4)
            pe.wait_ge(v_ready, NT + 2)
            pe.wait_ge(lora_loaded, 16 * (2 * R4 + 2))
            for r in range(R4):
                for c in range(KC):
                    mm = pe.matmul(psum[:, r, c * NT * R8:(c + 1) * NT * R8], lora_in[:, r, c * P:(c + 1) * P], gate_a, start=True, stop=True)
                mm.then_inc(lora_mm, 1)
            for m in range(2):
                for h in range(2):
                    for k in range(R4):
                        mm = pe.matmul(psum[:, 4 + 2 * m + h, :], gate_b[:, k, m * P:(m + 1) * P], lora_in[:, R4 + k, h * 512:(h + 1) * 512],
                                       start=(k == 0), stop=(k == R4 - 1))
                    mm.then_inc(lora_mm, 1)
            pe.wait_ge(lora_ready, R4 + 4)
            pe.wait_ge(v_ready, NT + 2)
            pe.sem_inc(s_max, 2)
            pe.sem_inc(p_ready, 2)

            def queries(g, b, first=False):
                i = g * 2 + b
                if not first:
                    pe.wait_ge(q_lo_ready, i)
                project(0, S, lambda c: sign_qkv[:, c, ds(g * P, P)], slice(b * S, (b + 1) * S)).then_inc(q_mm, 1)

            def scores(g, b):
                i = g * 2 + b
                pe.wait_ge(q_stacked[b], 16 * 3 * A_REP * (g + 1))
                pe.wait_ge(k_loaded[b], 48 * (g + 1))
                for j in range(A_REP):
                    for qt in range(QT):
                        n = j * QT + qt
                        pe.wait_ge(s_max, 16 * i + n + 1)
                        pe.matmul(psum[:, 2 + n % 2, :], q_op[b][0:A_MAX, j, qt * P:(qt + 1) * P], k_op[b][0:A_MAX, :],
                                  start=True, stop=True).then_inc(s_mm, 1)

            def turn_max(g, b, first=False):
                i = g * 2 + b
                pe.wait_ge(s_max, 16 * i + 18)
                if not first:
                    pe.wait_ge(m_lo_ready, i)
                pe.transpose(psum[0:16, 1, 0:P], m_neg[:, b, :], ident[:]).then_inc(mT_done, 1)

            def shifted(g, b, kt):
                i = g * 2 + b
                for j in range(A_REP):
                    n = 4 * kt + j
                    pe.wait_ge(p_ready, 16 * i + n + 1)
                    mm = pe.matmul(psum[:, 4 + n % 2, :], k_op[b][0:A_ROWS, kt * P:(kt + 1) * P], q_op[b][0:A_ROWS, j, :],
                                   start=True, stop=True).then_inc(st_mm, 1)

            def values(g, b, kt):
                i = g * 2 + b
                pe.wait_ge(p_ready, 16 * i + 4 * kt + 6)
                for j in range(A_REP):
                    pe.matmul(psum[j * 32:(j + 1) * 32, 6, :], v_g[:, b, kt, :], prob[:, kt % 2, j, :], start=(kt == 0), stop=(kt == QT - 1))
                for j in range(A_REP):
                    mm = pe.matmul(psum[j * 32:(j + 1) * 32, 7, :], ones32[:], prob[:, kt % 2, j, :], start=(kt == 0), stop=(kt == QT - 1))
                mm.then_inc(pv_done, 1)

            def step(g, b, g1, b1, g2, first=False):
                i = g * 2 + b
                if g1 is not None:
                    scores(g1, b1)
                pe.wait_ge(m_loaded[b], 32 * (g + 1))
                shifted(g, b, 0)
                shifted(g, b, 1)
                pe.wait_ge(vg_ready, i + 1)
                if not first:
                    pe.wait_ge(o_copied, 2 * i)
                values(g, b, 0)
                if g2 is not None:
                    queries(g2, b)
                shifted(g, b, 2)
                values(g, b, 1)
                shifted(g, b, 3)
                values(g, b, 2)
                values(g, b, 3)
                if g1 is not None:
                    turn_max(g1, b1)

            queries(0, 0, True)
            queries(0, 1)
            scores(0, 0)
            turn_max(0, 0, True)
            step(0, 0, 0, 1, 1, True)
            step(0, 1, 1, 0, 1)
            with pe.Fori(1, A_KV - 1) as g:
                step(g, 0, g, 1, g + 1)
                step(g, 1, g + 1, 0, g + 1)
            step(A_KV - 1, 0, A_KV - 1, 1, None)
            step(A_KV - 1, 1, None, None, None)

            pe.wait_ge(att_hi_ready, NI)
            pe.wait_ge(att_lo_ready, NI + 1)
            pe.wait_ge(xw_loaded, 16 * 3)

            def out_proj(i, h):
                pe.wait_ge(y0_ready, 2 * i + 2)
                for g in range(KC):
                    for part in range(2):
                        mm = pe.matmul(psum[:, h, :], (attT_hi, attT_lo)[part][:, g, ds(i * P, P)], sign_o[:, g, h * 512:(h + 1) * 512],
                                       start=(g == 0 and part == 0), stop=(g == KC - 1 and part == 1))
                mm.then_inc(op_mm, 1)

            def turn(bank, src, n, done):
                for c in range(n):
                    mm = pe.transpose(psum[:, bank + c // 4, (c % 4) * P:(c % 4 + 1) * P], src[:, c * P:(c + 1) * P], ident[:])
                mm.then_inc(done, 1)

            def x_tile(i, nxt):
                pe.wait_ge(h_ready, i + 1)
                pe.wait_ge(vx_ready, i + 1)
                pe.wait_ge(rope_step, 6 * i + 6)
                turn(2, h_st, KC, hT_mm)
                if nxt:
                    out_proj(i + 1, 0)
                pe.wait_ge(hT_ready, 2 * i + 2)
                pe.wait_ge(r_lo, i + 1)
                for c in range(KC):
                    mm = pe.matmul(psum[:, 4 + c // 4, (c % 4) * 3 * HC:(c % 4 + 1) * 3 * HC], hT[:, c, :], read1[:, c, :], start=True, stop=True)
                mm.then_inc(y_mm, 1)
                if nxt:
                    out_proj(i + 1, 1)
                pe.wait_ge(yn_ready, 6 * i + 6)
                turn(6, yn, 6, ynT_mm)
                pe.wait_ge(ynT_ready, 6 * i + 6)
                for o in range(3):
                    for k in range(2):
                        mm = pe.matmul(psum[:, 2 + o // 2, (o % 2) * H:(o % 2 + 1) * H], ynT[:, 2 * o + k, :], wqkv[:, 2 * o + k, :],
                                       start=(k == 0), stop=(k == 1))
                mm.then_inc(qkv_mm, 1)
                pe.wait_ge(rope_step, 6 * i + 12)
                turn(4, rot, 4, rT_mm)

            pe.sem_inc(vx_ready, 1)
            pe.sem_inc(rope_step, 6)
            pe.sem_inc(r_lo, 1)
            out_proj(0, 0)
            out_proj(0, 1)
            with pe.Fori(0, NT - 1) as i:
                x_tile(i, True)
            x_tile(NT - 1, False)

            pe.sem_inc(xs_max, 2)
            pe.sem_inc(xp_ready, 2)
            pe.sem_inc(xo_copied, 2)
            pe.wait_ge(r_lo, NT + 1)

            def x_scores(qd, b):
                i = qd * 2 + b
                pe.wait_ge(xq_loaded[b], 128 * (qd + 1))
                for j in range(NQ):
                    for qt in range(QT):
                        n = j * QT + qt
                        bank = psum[:, 2 + n % 2, :]
                        pe.wait_ge(xs_max, 16 * i + n + 1)
                        pe.matmul(bank[:, 0:(qt + 1) * P], q_op[b][0:X_MAX, j, qt * P:(qt + 1) * P], kx_op[b][0:X_MAX, j, 0:(qt + 1) * P],
                                  start=True, stop=True)
                        pe.matmul(bank[:, qt * P:(qt + 1) * P], ident_bf[:], mask_qk[:], start=False, stop=True, skip_group_check=True).then_inc(xs_mm, 1)

            def x_turn_max(qd, b, first=False):
                i = qd * 2 + b
                pe.wait_ge(xs_max, 16 * i + 18)
                if not first:
                    pe.wait_ge(xm_lo, i)
                pe.transpose(psum[0:16, 1, 0:P], m_neg[:, b, :], ident[:]).then_inc(xmT_done, 1)

            def x_shifted(qd, b, kt):
                i = qd * 2 + b
                for j in range(NQ):
                    n = 4 * kt + j
                    bank = psum[:, 4 + n % 2, :]
                    pe.wait_ge(xp_ready, 16 * i + n + 1)
                    pe.matmul(bank[:, 0:S - kt * P], kx_op[b][:, j, kt * P:(kt + 1) * P], q_op[b][:, j, kt * P:], start=True, stop=True)
                    pe.matmul(bank[:, 0:P], ident_bf[:], mask_kq[:], start=False, stop=True, skip_group_check=True).then_inc(xst_mm, 1)

            def x_values(qd, b, kt):
                i = qd * 2 + b
                pe.wait_ge(xp_ready, 16 * i + 4 * kt + 6)
                for bank in (6, 7):
                    for j in range(NQ):
                        w = v_q[:, b, kt, j * 32:(j + 1) * 32] if bank == 6 else ones32[:]
                        mm = pe.matmul(psum[j * 32:(j + 1) * 32, bank, kt * P:], w, prob[:, kt % 2, j, 0:S - kt * P],
                                       start=(kt == 0), stop=(kt == QT - 1), skip_group_check=True)
                mm.then_inc(xpv_done, 1)

            def x_step(qd, b, q1, b1):
                i = qd * 2 + b
                if q1 is not None:
                    x_scores(q1, b1)
                pe.wait_ge(xm_loaded[b], 32 * (qd + 1))
                x_shifted(qd, b, 0)
                x_shifted(qd, b, 1)
                pe.wait_ge(xv_ready, i + 1)
                pe.wait_ge(xo_copied, 2 * i + 2)
                for kt in range(QT):
                    x_values(qd, b, kt)
                    if kt + 2 < QT:
                        x_shifted(qd, b, kt + 2)
                if q1 is not None:
                    x_turn_max(q1, b1)

            x_scores(0, 0)
            x_turn_max(0, 0, True)
            x_step(0, 0, 0, 1)
            x_step(0, 1, 1, 0)
            with pe.Fori(1, X_QUADS - 1) as qd:
                x_step(qd, 0, qd, 1)
                x_step(qd, 1, qd + 1, 0)
            x_step(X_QUADS - 1, 0, X_QUADS - 1, 1)
            x_step(X_QUADS - 1, 1, None, None)

            def write(k, i, lhs, w, chunks):
                n = 2 * i + k
                for c in range(chunks):
                    pe.matmul(psum[:, 0, 0:H + N_AB], lhs[:, c, :], w[:, c, 0:H + N_AB], start=(c == 0), stop=(c == chunks - 1))
                for c in range(chunks):
                    mm = pe.matmul(psum[0:DR, 1, 0:P], w[:, c, H + N_AB:], lhs[:, c, :], start=(c == 0), stop=(c == chunks - 1))
                mm.then_inc(W["w_mm"], 1)
                pe.wait_ge(W["low_ready"], n + 1)
                pe.matmul(psum[:, 1, H:2 * H], low[:], du[k], start=True, stop=True).then_inc(W["du_mm"], 1)

            pe.wait_ge(xo_copied, 2 * XI + 2)
            pe.wait_ge(w2_loaded, 16 * 5)
            pe.wait_ge(kern_loaded, 48)
            with pe.Fori(0, NT) as i:
                pe.wait_ge(yT_loaded, 16 * i + 16)
                write(0, i, yT, write1, 2)
                pe.wait_ge(W["hn_ready"], 4 * i + 2)
                turn(2, h_mid, KC, h2T_mm)
                pe.wait_ge(h2T_ready, 2 * i + 2)
                for c in range(KC):
                    mm = pe.matmul(psum[:, 4, c * 2 * HC:(c + 1) * 2 * HC], hT[:, c, :], read2[:, c, :], start=True, stop=True)
                mm.then_inc(y2_mm, 1)
                pe.wait_ge(y2n_ready, 2 * i + 2)
                turn(5, yn, 4, y2T_mm)
                pe.wait_ge(y2T_ready, 4 * i + 4)
                for n, bank in ((0, 6), (1, 2)):
                    for f in range(KC):
                        for k in range(2):
                            mm = pe.matmul(psum[:, bank + f // 4, (f % 4) * P:(f % 4 + 1) * P], ctx_w[:, n, k, f * P:(f + 1) * P], ynT[:, 2 * n + k, :],
                                           start=(k == 0), stop=(k == 1))
                mm.then_inc(gu_mm, 1)
                pe.wait_ge(mlp_ready, i + 1)
                write(1, i, mlpT, write2, KC)
                pe.wait_ge(xf_ready, i + 1)
                turn(2, h_out, KC, fT_mm)
                pe.wait_ge(fT_ready, 2 * i + 2)
                pe.wait_ge(lo_loaded, 32 * i + 32)
                for c in range(KC):
                    mm = pe.matmul(psum[:, 5, 0:R2], hT[:, c, :], lora_at[:, c, :], start=(c == 0), stop=(c == KC - 1))
                mm.then_inc(ax_mm, 1)
                for h in range(2):
                    for c in range(KC):
                        pe.matmul(psum[:, 6 + h, :], hT[:, c, :], kern[:, c, h * 512:(h + 1) * 512], start=(c == 0), stop=False)
                wait_apart(pe, ax_ready, i + 1)
                pe.transpose(psum[0:R2, 5, 256:256 + P], ax, ident[:]).then_inc(axT_mm, 1)
                pe.wait_ge(axT_ready, i + 1)
                for h in range(2):
                    mm = pe.matmul(psum[:, 6 + h, :], axT, lora_bt[0:R2, h * 512:(h + 1) * 512], start=False, stop=True)
                mm.then_inc(f_mm, 1)


def kernel(**inputs):
    import concourse.bacc as bacc
    from concourse.bass_utils import run_bass_kernel_spmd

    nc = bacc.Bacc("TRN2", target_bir_lowering=False, num_devices=1)
    arrays = {"in_" + n: v for n, v in lay_out(inputs).items()}
    dram = {n[3:]: nc.dram_tensor(n, a.shape, mybir.dt.from_np(a.dtype), kind="ExternalInput").ap() for n, a in arrays.items()}
    out = nc.dram_tensor("out", (T, D), F32, kind="ExternalOutput").ap()
    build_program(nc, dram, out)
    r = run_bass_kernel_spmd(nc, [arrays], core_ids=[0])
    return r.results[0]["out"].reshape(B, S, D)


def lay_out(inputs):
    a = {n: np.asarray(v) for n, v in inputs.items()}
    x = "L0_xattn_"
    cat = np.concatenate
    columns = lambda v: v.reshape(-1, P).T
    lay = {}
    lay["x"] = a["x"].reshape(T, D)
    lay["pos"] = a["pos_BxS"].astype(np.int32).reshape(NT, P).T
    lay["wT"] = cat([a[f"L0_attn_{n}_weight"].T for n in "qkvo"], axis=1)
    lay["cols"] = cat([columns(a["L0_attn_q_scale"]), columns(a["L0_attn_k_scale"]),
                       columns(a[x + "attn_read_g"]), columns(a[x + "attn_read_b"]),
                       columns(a[x + "mlp_read_g"]), columns(a[x + "mlp_read_b"])], axis=1)
    lay["rows"] = np.broadcast_to(cat([a[x + "attn_wab_b"], a[x + "mlp_wab_b"],
                                       a[x + "attn_du_b"], a[x + "mlp_du_b"], a["L0_ffn_bias"]])[None], (P, N_ROWS))
    lay["scale_rows"] = np.broadcast_to(cat([a["L0_attn_v_scale"], a["L0_attn_o_scale"]])[None], (P, N_SCALES))
    for name, w in (("read1", a[x + "attn_read_w"]), ("read2", a[x + "mlp_read_w"])):
        n_out = w.shape[1]
        block = np.zeros((KC, HC, C, n_out, HC), np.float32)
        for h in range(HC):
            block[:, h, :, :, h] = w.reshape(KC, HC, n_out, C)[:, h].transpose(0, 2, 1)
        lay[name] = block.reshape(KC, P, n_out * HC).transpose(1, 0, 2)
    lay["wqkv"] = a[x + "qkv_w"].transpose(0, 2, 1).reshape(3, 2, P, H).transpose(2, 0, 1, 3)
    for n, name in ((1, "attn"), (2, "mlp")):
        wod, wab = a[x + name + "_wod_w"], a[x + name + "_wab_w"]
        wT = cat([wod[:H], wab, wod[H:]]).T
        lay[f"write{n}"] = wT.reshape(-1, P, N_W).transpose(1, 0, 2)
        lay[f"du{n}"] = a[x + name + "_du_w"].T
    lay["ctx"] = a["ctx_1024"].transpose(0, 2, 1).reshape(2, 2, P, M).transpose(2, 0, 1, 3)
    lay["kern"] = a["L0_ffn_kernel"].reshape(KC, P, D).transpose(1, 0, 2)
    lay["lora_a"] = a["L0_ffn_lora_A"].reshape(N_LORA, R4, R8, D).transpose(1, 0, 2, 3).reshape(R4, P, D)
    lay["lora_as"] = a["L0_ffn_lora_A_shared"].T.reshape(KC, P, RANK).transpose(1, 0, 2)
    lay["lora_b"] = a["L0_ffn_lora_B"].transpose(0, 2, 1).reshape(R4, P, D)
    lay["lora_bs"] = a["L0_ffn_lora_B_shared"].T
    gate = a["L0_ffn_gate"]
    gate_a = np.zeros((N_LORA, R8, NT, R8), np.float32)
    for r in range(R8):
        gate_a[:, r, :, r] = gate.T
    lay["gate_a"] = gate_a.reshape(P, NT * R8)
    gate_b = np.zeros((N_LORA, RANK, NT, RANK), np.float32)
    for r in range(RANK):
        gate_b[:, r, :, r] = gate.T
    lay["gate_b"] = gate_b.reshape(R4, P, NT * RANK).transpose(1, 0, 2)
    return {n: np.ascontiguousarray(v) for n, v in lay.items()}
```

```python
from contextlib import ExitStack

import numpy as np

import concourse.bass as bass
from concourse import mybir

F32 = mybir.dt.float32
F32R = mybir.dt.float32r
F16 = mybir.dt.float16
BF16 = mybir.dt.bfloat16
I32 = mybir.dt.int32
ALU = mybir.AluOpType
ACT = mybir.ActivationFunctionType
AX_X = mybir.AxisListType.X
ds = bass.ds

P = 128
B, S, D = 2, 512, 1024
T = B * S
NT = T // P
KC = D // P
QT = S // P
LN_EPS = 1e-5

A_HD, A_KV = 32, 8
A_REP = D // A_HD // A_KV
KVD = A_KV * A_HD
QKV = D + 2 * KVD
A_SCALE = float(1.0 / np.sqrt(A_HD))
A_MAX = 3 * A_HD
A_ROWS = A_MAX + 2
NI = A_KV * B
A_ROUNDS = (NI - 4) // 3
V_GAIN = 64.0

H, C, RH = 256, 4, 16
HS, DR, M = H // RH, 8, 1024
X_NH = 16
X_HD = H // X_NH
HALF = X_HD // 2
HC = P // C
NQ = 4
X_QUADS = X_NH // NQ
X_MAX = 4 * X_HD
X_SCALE = float(1.0 / np.sqrt(X_HD))
N_A = (C - 1) * RH
N_AB = 2 * N_A + RH
N_Z = H + N_A
N_W = H + N_AB + DR
SSM_EPS = 1e-5

N_LORA, RANK = 16, 32
R8 = P // N_LORA
R4 = RANK // R8
R2 = 2 * RANK

MAGIC = 1.5 * 2.0 ** 23
TWO_PI = 2 * np.pi
TP1 = 6.28125
TP2 = float(np.float32(np.float16(TWO_PI - TP1)))
TP3 = float(TWO_PI - TP1 - TP2)
ROPE_INV = (np.float32(1) / np.power(np.float32(10000), np.arange(HALF, dtype=np.float32) / np.float32(HALF))).astype(np.float32)

COLS = {}
_at = 0
for _n, _w in (("q_scale", KC), ("k_scale", KVD // P), ("g1", 6), ("b1", 6), ("g2", 4), ("b2", 4)):
    COLS[_n] = (_at, _at + _w)
    _at += _w
N_COLS = _at
ROWS = {}
_at = 0
for _n, _w in (("wab1", N_AB), ("wab2", N_AB), ("du1", H), ("du2", H), ("bias", D)):
    ROWS[_n] = (_at, _at + _w)
    _at += _w
N_ROWS = _at
N_SCALES = KVD + D


def build_program(nc, d, out):
    ctx = ExitStack()
    with ctx:
        def sb(name, shape, dt=F32):
            return ctx.enter_context(nc.sbuf_tensor(name, shape, dt))

        def sem(name):
            return ctx.enter_context(nc.semaphore(name))

        def scratch(name, shape):
            return nc.dram_tensor(name, shape, F32).ap()

        psum = ctx.enter_context(nc.psum_tensor("psum", [P, 8, 512], F32))

        cols = sb("cols", [P, N_COLS])
        rows = sb("rows", [P, N_ROWS])
        ident = sb("ident", [P, P])
        ident_bf = sb("ident_bf", [P, P], BF16)
        mask_qk = sb("mask_qk", [P, P], BF16)
        mask_kq = sb("mask_kq", [P, P], BF16)
        ones32 = sb("ones32", [P, A_HD])
        minus_half = sb("minus_half", [P, 4])
        c_q = sb("c_q", [P, KC])
        c_k = sb("c_k", [P, KVD // P])
        c_o = sb("c_o", [P, D])
        pos_i = sb("pos_i", [P, NT], I32)
        pos_f = sb("pos_f", [P, NT])
        trig = sb("trig", [P, 3, NT, HALF])

        region_x = sb("region_x", [P, KC * T])
        region_a = sb("region_a", [P, KC * T])
        region_w = sb("region_w", [P, QKV + D + QKV + D + KC * QKV // 2])
        region_p = sb("region_p", [P, 2 * 4 * 512])
        region_s = sb("region_s", [P, KC * D // 2])
        xnT_hi = region_x[:, 0:KC * T // 2].bitcast(F16).rearrange("p (c t) -> p c t", c=KC)
        xnT_lo = region_x[:, KC * T // 2:].bitcast(F16).rearrange("p (c t) -> p c t", c=KC)
        x1 = region_x[:, :].rearrange("p (t n) -> p t n", t=NT)
        attT_hi, attT_lo = (region_a[:, n * KC * T // 2:(n + 1) * KC * T // 2].bitcast(F16).rearrange("p (i s) -> p i s", s=S) for n in range(2))
        o_in_hi, o_in_lo = (x.rearrange("p (c b) s -> p c (b s)", b=B) for x in (attT_hi, attT_lo))
        kern = region_a[:, :].rearrange("p (c n) -> p c n", c=KC)
        w_in = [region_w[:, 0:QKV + D], region_a[:, 0:QKV + D]]
        _o = QKV + D
        w_abs = region_w[:, _o:_o + QKV + D]
        _o += QKV + D
        sign_qkv = region_w[:, _o:].bitcast(F16).rearrange("p (c n) -> p c n", c=KC)
        sign_o = region_s[:, :].bitcast(F16).rearrange("p (c n) -> p c n", c=KC)
        prob_a = region_x[:, :].rearrange("p (b j n) -> p b j n", b=4, j=4)
        prob = region_p[:, :].rearrange("p (b j n) -> p b j n", b=2, j=4)
        x_in = region_p[:, 0:2 * D].rearrange("p (u n) -> p u n", u=2)
        _o = 2 * D
        scale_rows = region_p[:, _o:_o + N_SCALES]
        _o += N_SCALES
        mean_w = region_p[:, _o:_o + P]
        _o += P
        c_v = region_p[:, _o:_o + KVD]
        _o += KVD
        ang = region_p[:, _o:_o + NT * HALF].rearrange("p (t f) -> p t f", f=HALF)
        _o += NT * HALF
        trig_n, trig_r = (region_p[:, _o + n * 2 * NT * HALF:_o + (n + 1) * 2 * NT * HALF].rearrange("p (k t f) -> p k t f", k=2, f=HALF)
                          for n in range(2))

        q_op = [sb(f"q_op{u}", [P, A_REP, S], F32R) for u in range(2)]
        kr = sb("kr", [P, 2 * NQ * S], F32R)
        k_op = [kr[:, u * S:(u + 1) * S] for u in range(3)]
        qa_op = [q_op[0], q_op[1], kr[:, 4 * S:].rearrange("p (j n) -> p j n", j=A_REP)]
        hi_st = sb("hi_st", [P, S], F32R)
        lo_st = sb("lo_st", [P, S], F32R)
        stage = [(hi_st[:], lo_st[:])] + [(kr[:, (2 + 2 * n) * S:(3 + 2 * n) * S], kr[:, (3 + 2 * n) * S:(4 + 2 * n) * S]) for n in range(3)]
        m_hi = sb("m_hi", [16, P], F32R)
        m_lo = sb("m_lo", [16, P], F32R)
        kx_op = [kr[:, u * NQ * S:(u + 1) * NQ * S].rearrange("p (j n) -> p j n", j=NQ) for u in range(2)]

        st = sb("st", [P, 2, 2, 6])
        mv = sb("mv", [P, 2, 2])
        ve = sb("ve", [P, 2, 1])
        rstd = sb("rstd", [P, 2, 1])

        v_all = sb("v_all", [P, NT, KVD])
        v_heads = v_all[:].rearrange("p a b -> p (a b)").rearrange("p (g t e) -> p g t e", g=A_KV, e=A_HD)
        v_steps = v_all[:].rearrange("p a b -> p (a b)").rearrange("p (i n) -> p i n", n=QT * A_HD)
        v_g = sb("v_g", [P, 3, QT, A_HD])
        m_neg = sb("m_neg", [P, 3, 16])
        o_sb, den_sb, att = (region_w[:, n * S:(n + 1) * S] for n in range(3))

        v_x = region_w[:, 3 * S:3 * S + NT * 2 * H].rearrange("p (t n) -> p t n", t=NT)
        _o = 3 * S + NT * 2 * H
        ctx_w = region_w[:, _o:_o + 4 * M].rearrange("p (w k n) -> p w k n", w=2, k=2)
        _o += 4 * M
        wqkv = region_w[:, _o:_o + 6 * H].rearrange("p (s n) -> p s n", s=6)
        lora_bt = region_w[:, _o:_o + D]
        lora_at = region_w[:, _o + D:_o + D + KC * R2].rearrange("p (c r) -> p c r", c=KC)
        y0 = region_p[:, 2 * D:3 * D]
        h_st = region_p[:, 3 * D:4 * D]
        hT = v_all[:].rearrange("p t n -> p (t n)")[:, 0:D].rearrange("p (c n) -> p c n", c=KC)
        v_q = v_all[:].rearrange("p t n -> p (t n)")[:, 0:2 * QT * P].rearrange("p (b k n) -> p b k n", b=B, k=QT)
        write1 = region_s[:, 0:2 * N_W].rearrange("p (k n) -> p k n", k=2)
        write2 = region_s[:, 2 * N_W:10 * N_W].rearrange("p (k n) -> p k n", k=KC)
        v_rest = v_all[:].rearrange("p t n -> p (t n)")[:, D:2 * D]
        read1 = v_rest[:, 0:KC * 3 * HC].rearrange("p (c n) -> p c n", c=KC)
        read2 = v_rest[:, 0:KC * 2 * HC].rearrange("p (c n) -> p c n", c=KC)
        du = [v_rest[0:DR, KC * 2 * HC + n * H:KC * 2 * HC + (n + 1) * H] for n in range(2)]
        yn = sb("yn", [P, 3 * H])
        ynT = sb("ynT", [P, 6, P])
        rot = yn[:, 0:2 * H]
        rope_a = yn[:, 2 * H:3 * H]
        mvs = sb("mvs", [P, 2 * NT])
        ves = sb("ves", [P, 1])
        rstds = sb("rstds", [P, NT])
        st3 = sb("st3", [P, 3, 2, 6])
        mv3 = sb("mv3", [P, 3, 2])
        ve3 = sb("ve3", [P, 3])
        rs3 = sb("rs3", [P, 3])
        _w = [region_p[:, n * D:(n + 1) * D] for n in range(4)] + [region_w[:, 3 * S + n * D:3 * S + (n + 1) * D] for n in range(4)]
        h_in, h_mid_0, h_mid_1, h_out, mlpT_f, out_t, abar, bbar = _w
        h_mid = [h_mid_0, h_mid_1]
        hT_f = c_o[:].rearrange("p (c n) -> p c n", c=KC)
        mlpT = mlpT_f.rearrange("p (f n) -> p f n", f=KC)
        h_a = region_w[:, 0:3 * H]
        z_b, e_b = region_w[:, 3 * H:3 * H + N_Z], region_w[:, 3 * H + N_Z:3 * H + 2 * N_Z]
        b_skip = abar[:, 3 * H:4 * H]
        sp_b = sb("sp_b", [P, N_Z])
        ab_b, r_b, rc_b = bbar[:, 3 * H:3 * H + 64], bbar[:, 3 * H + 64:3 * H + 64 + N_A], bbar[:, 3 * H + 128:3 * H + 128 + N_A]
        yT = v_g[:].rearrange("p b t e -> p (b t e)")[:, 0:2 * P].rearrange("p (k n) -> p k n", k=2)
        low = [region_s[0:DR, 10 * N_W + n * P:10 * N_W + (n + 1) * P] for n in range(2)]
        ax = bbar[:, 3 * H + 192:3 * H + 192 + R2]
        axT = region_w[0:R2, 3 * H + 2 * N_Z:3 * H + 2 * N_Z + P]
        lora_in = region_a[:, :].rearrange("p (s n) -> p s n", s=2 * R4)
        gate_b = region_w[:, 0:R4 * NT * RANK].rearrange("p (k n) -> p k n", k=R4)
        gate_a = region_w[:, R4 * NT * RANK:R4 * NT * RANK + NT * R8]
        a_eff = region_p[:, 0:KC * NT * RANK].rearrange("p (b c r) -> p b c r", b=NT, c=KC)
        b_eff = region_p[:, 2 * D:4 * D].rearrange("p (m n) -> p m n", m=2)

        def wait_apart(eng, *waits):
            waits = [(semaphore, eng.to_reg(value)) for semaphore, value in waits]
            eng.wait_ge(s_const, 64)
            for semaphore, value in waits:
                eng.wait_ge(semaphore, value)

        def run_rounds(eng, round_):
            round_(0, 0, True, False, False)
            round_(1, 1, True, True, False)
            with eng.Fori(1, NT // 2) as it:
                for u in range(2):
                    round_(it * 2 + u, u, True, True, True)
            round_(NT, 0, False, True, True)
            round_(NT + 1, 1, False, False, True)

        a_scr = scratch("a_scr", [NT, P, KC * RANK])
        b_scr = scratch("b_scr", [NT * RANK, D])
        k_scr = scratch("k_scr", [2, A_KV, B, A_HD, S])
        q_scr = scratch("q_scr", [2, A_KV, B, A_REP * A_HD, S])
        qk_scr = scratch("qk_scr", [2, 2, H, T])
        y_scr = scratch("y_scr", [H, T])

        s_const = sem("const_loaded")
        block = ctx.enter_context(nc.Block())

        x_slot = [sem(f"x_slot{u}_loaded") for u in range(2)]
        w_loaded = [sem(f"w_loaded{u}") for u in range(2)]
        signs_done, abs_taken, qkv_summed, o_summed = sem("signs_done"), sem("abs_taken"), sem("qkv_summed"), sem("o_summed")
        made = sem("constants_made")
        ln_step, ln_rstd = sem("ln_step"), sem("ln_rstd")
        xn_ready = sem("xn_ready")
        xT_done, xT_hi, xT_free = sem("xT_done"), sem("xT_hi"), sem("xT_free")
        means_done, c_ready = sem("weight_means_done"), sem("scales_ready")
        qk_mm, qk_hi, qk_lo = sem("qk_mm"), sem("qk_hi"), sem("qk_lo")
        staged_out = [sem(f"staged_out{u}") for u in range(4)]
        v_mm, v_ready = sem("v_mm"), sem("v_ready")
        ang_step, trig_done = sem("ang_step"), sem("trig_done")
        qk_loaded = [sem(f"qk_loaded{u}") for u in range(3)]
        m_loaded = [sem(f"m_loaded{u}") for u in range(3)]
        s_mm, s_max = sem("s_mm"), sem("s_max")
        mT_done, m_hi_ready, m_lo_ready = sem("mT_done"), sem("m_hi_ready"), sem("m_lo_ready")
        st_mm, p_ready, pv_done = sem("st_mm"), sem("p_ready"), sem("pv_done")
        vg_ready = sem("vg_ready")
        o_copied, den_rec, att_ready, att_hi_ready, att_lo_ready = sem("o_copied"), sem("den_rec"), sem("att_ready"), sem("att_hi_ready"), sem("att_lo_ready")
        lora_loaded, lora_mm, lora_ready, lora_stored = sem("lora_loaded"), sem("lora_mm"), sem("lora_ready"), sem("lora_stored")
        xw_loaded = sem("xw_loaded")
        x_again = [sem(f"x_again{u}") for u in range(2)]
        op_mm, y0_ready, x1_ready = sem("op_mm"), sem("y0_ready"), sem("x1_ready")
        l_step, l_rstd, h_ready = sem("l_step"), sem("l_rstd"), sem("h_ready")
        hT_mm, hT_ready, y_mm = sem("hT_mm"), sem("hT_ready"), sem("y_mm")
        y_step, y_rstd, yn_ready = sem("y_step"), sem("y_rstd"), sem("yn_ready")
        ynT_mm, ynT_ready, qkv_mm = sem("ynT_mm"), sem("ynT_ready"), sem("qkv_mm")
        rope_step, vx_ready, rT_mm, r_hi, r_lo, qk_stored = (sem(n) for n in (
            "rope_step", "vx_ready", "rT_mm", "r_hi", "r_lo", "qk_stored"))
        vx_zero, k_ones = sem("vx_zero"), sem("k_ones")
        xq_loaded = [sem(f"xq_loaded{u}") for u in range(2)]
        xm_loaded = [sem(f"xm_loaded{u}") for u in range(2)]
        xs_mm, xs_max, xmT_done, xm_hi, xm_lo = sem("xs_mm"), sem("xs_max"), sem("xmT_done"), sem("xm_hi"), sem("xm_lo")
        xst_mm, xp_ready, xpv_done, xv_ready = sem("xst_mm"), sem("xp_ready"), sem("xpv_done"), sem("xv_ready")
        xo_copied, xden_rec, xatt_ready, y_stored = sem("xo_copied"), sem("xden_rec"), sem("xatt_ready"), sem("y_stored")
        w2_loaded, kern_loaded, yT_loaded, lo_loaded = sem("w2_loaded"), sem("kern_loaded"), sem("yT_loaded"), sem("lo_loaded")
        h2_ready = sem("h2_ready")
        W = {n: [sem(f"{n}_{k}") for k in (1, 2)] for n in (
            "w_mm", "low_ready", "du_mm", "z_ready", "az_ready", "e_ready", "l_ready", "sp_ready", "r_step",
            "da_ready", "abar_ready", "ha_ready", "b_step", "hn_ready")}
        h2T_mm, h2T_ready, y2_mm = sem("h2T_mm"), sem("h2T_ready"), sem("y2_mm")
        y2_step, y2_rstd, y2n_ready = sem("y2_step"), sem("y2_rstd"), sem("y2n_ready")
        y2T_mm, y2T_ready, gu_mm, tanh_ready, g_ready, mlp_ready = (sem(n) for n in (
            "y2T_mm", "y2T_ready", "gu_mm", "tanh_ready", "g_ready", "mlp_ready"))
        x2_ready, f_step, f_rstd, xf_ready = (sem(n) for n in ("x2_ready", "f_step", "f_rstd", "xf_ready"))
        fT_mm, fT_ready, ax_mm, ax_ready, axT_mm, axT_ready, f_mm, o_step, out_ready, out_stored = (sem(n) for n in (
            "fT_mm", "fT_ready", "ax_mm", "ax_ready", "axT_mm", "axT_ready", "f_mm", "o_step", "out_ready", "out_stored"))
        xatt_free = sem("a_finished")
        XI = X_QUADS * B

        @block.sync
        def _(sp):
            sp.dma_start(cols[:], d["cols"]).then_inc(s_const, 16)
            sp.dma_start(rows[:], d["rows"]).then_inc(s_const, 16)
            sp.dma_start(scale_rows, d["scale_rows"]).then_inc(s_const, 16)
            sp.dma_start(pos_i[:], d["pos"]).then_inc(s_const, 16)
            sp.sem_inc(xT_done, 2)
            with sp.Fori(0, NT // 2) as it:
                for u in range(2):
                    i = it * 2 + u
                    sp.wait_ge(xT_done, i + 1)
                    sp.dma_start(x_in[:, u, :], d["x"][ds(i * P, P), :]).then_inc(x_slot[u], 16)
                    sp.wait_ge(qkv_summed, i + 1)
                    sp.wait_ge(o_summed, i + 1)
                    sp.dma_start(w_in[u], d["wT"][ds(i * P, P), :]).then_inc(w_loaded[u], 16)
            sp.wait_ge(qkv_summed, NT + 2)
            sp.wait_ge(o_summed, NT + 2)
            sp.wait_ge(xT_done, NT + 2)
            for r in range(R4):
                sp.dma_start(lora_in[:, r, :], d["lora_a"][r]).then_inc(lora_loaded, 16)
                sp.dma_start(lora_in[:, R4 + r, :], d["lora_b"][r]).then_inc(lora_loaded, 16)
            sp.dma_start(gate_a, d["gate_a"]).then_inc(lora_loaded, 16)
            sp.dma_start(gate_b, d["gate_b"]).then_inc(lora_loaded, 16)
            for n in range(4):
                b, m = n // 2, n % 2
                sp.wait_ge(qk_hi, n + 1)
                sp.wait_ge(qk_lo, n + 1)
                for part in range(2):
                    for h in range(4):
                        sp.dma_start(k_scr[part, 4 * m + h, b], stage[n][part][h * A_HD:(h + 1) * A_HD, :].bitcast(F32)).then_inc(staged_out[n], 16)
            sp.wait_ge(lora_ready, R4 + 4)
            for b in range(NT):
                sp.dma_start(a_scr[b], a_eff[:, b].rearrange("p c r -> p (c r)")).then_inc(lora_stored, 16)
            for m in range(2):
                sp.dma_start(b_scr[m * P:(m + 1) * P, :], b_eff[:, m, :]).then_inc(lora_stored, 16)
            q_rows = q_scr.rearrange("a g b n s -> a (g b) n s")
            with sp.Fori(0, NI // 4) as it:
                for u in range(4):
                    i = it * 4 + u
                    sp.wait_ge(qk_hi, i + 5)
                    sp.wait_ge(qk_lo, i + 5)
                    for part in range(2):
                        sp.dma_start(q_rows[part, ds(i, 1)].rearrange("o n s -> (o n) s"), stage[u][part].bitcast(F32)).then_inc(staged_out[u], 16)

            for u in range(4):
                sp.wait_ge(staged_out[u], 16 * 8 + 32 * NI // 4)
            sp.wait_ge(made, 16)
            sp.sem_inc(st_mm, 48)
            k_rows = k_scr.rearrange("a g b n s -> a (g b) n s")

            def load_qk(t, k):
                i, u = t * 3 + k, k % 3
                sp.wait_ge(st_mm, 16 * i + 16)
                for part in range(3):
                    sp.dma_start(k_op[u][part * A_HD:(part + 1) * A_HD, :].bitcast(F32),
                                 k_rows[part % 2, ds(i, 1)].rearrange("o n s -> (o n) s")).then_inc(qk_loaded[u], 16)
                    sp.dma_start(qa_op[u][part * A_HD:(part + 1) * A_HD].bitcast(F32),
                                 q_rows[part // 2, ds(i, 1)].rearrange("o (j e) s -> (o e) j s", j=A_REP)).then_inc(qk_loaded[u], 16)

            def load_max(t, k):
                i, u = t * 3 + k, k % 3
                sp.wait_ge(m_hi_ready, i + 1)
                sp.wait_ge(m_lo_ready, i + 1)
                for r, src in ((A_MAX, m_hi), (A_MAX + 1, m_lo)):
                    sp.dma_start(qa_op[u][r:r + 1].rearrange("o j n -> o (j n)").bitcast(F32), src[:].bitcast(F32)).then_inc(m_loaded[u], 16)

            for k in range(3):
                load_qk(0, k)
            load_max(0, 0)
            load_max(0, 1)
            with sp.Fori(0, A_ROUNDS) as t:
                for k in (1, 2, 3):
                    load_qk(t, k + 2)
                    load_max(t, k + 1)
            load_qk(0, NI - 1)
            load_max(0, NI - 2)
            load_max(0, NI - 1)

            sp.wait_ge(xatt_free, 1)
            sp.dma_start(read1, d["read1"]).then_inc(xw_loaded, 16)
            sp.dma_start(wqkv, d["wqkv"].rearrange("p o k n -> p (o k) n")).then_inc(xw_loaded, 16)
            sp.dma_start(ctx_w, d["ctx"]).then_inc(xw_loaded, 16)

            def load_x(i, u):
                sp.dma_start(x_in[:, u, :], d["x"][ds(i * P, P), :] if not isinstance(i, int) else d["x"][i * P:(i + 1) * P, :]).then_inc(x_again[u], 16)

            def store_qk(i):
                sp.wait_ge(r_hi, i + 1)
                sp.wait_ge(r_lo, i + 2)
                for part in range(2):
                    sp.dma_start(qk_scr[part].rearrange("q (m p) t -> p (q m) t", p=P)[:, :, ds(i * P, P)],
                                 (hi_st, lo_st)[part][:].rearrange("p (s t) -> p s t", s=4).bitcast(F32)).then_inc(qk_stored, 16)

            load_x(0, 0)
            load_x(1, 1)
            with sp.Fori(0, NT // 2 - 1) as it:
                for u in range(2):
                    i = it * 2 + u
                    sp.wait_ge(x1_ready, i + 1)
                    load_x(i + 2, u)
                    store_qk(i)
            store_qk(NT - 2)
            store_qk(NT - 1)
            sp.wait_ge(qk_stored, 2 * 16 * NT + 32)
            sp.wait_ge(k_ones, 2)
            sp.sem_inc(xst_mm, 32)

            def load_quad(qd, b):
                i = qd * 2 + b
                sp.wait_ge(xst_mm, 16 * i + 16)
                for side, dst, parts in ((0, q_op[b], (0, 0, 1, 1)), (1, kx_op[b], (0, 1, 0, 1))):
                    for r, part in enumerate(parts):
                        sp.dma_start(dst[r * X_HD:(r + 1) * X_HD].bitcast(F32),
                                     qk_scr[part, side, ds(qd * NQ * X_HD, NQ * X_HD), b * S:(b + 1) * S].rearrange("(j d) n -> d j n", j=NQ)
                                     ).then_inc(xq_loaded[b], 16)

            def load_max(qd, b):
                i = qd * 2 + b
                sp.wait_ge(xm_hi, i + 1)
                sp.wait_ge(xm_lo, i + 1)
                for r, src in ((X_MAX, m_hi), (X_MAX + 1, m_lo)):
                    sp.dma_start(q_op[b][r:r + 1].rearrange("o j n -> o (j n)").bitcast(F32), src[:].bitcast(F32)).then_inc(xm_loaded[b], 16)

            def store_y(qd, b):
                i = qd * 2 + b
                sp.wait_ge(xatt_ready, i + 1)
                for j in range(NQ):
                    sp.dma_start(y_scr[ds(qd * NQ * X_HD + j * X_HD, X_HD), b * S:(b + 1) * S], att[j * 32:j * 32 + X_HD, :]).then_inc(y_stored, 16)

            load_quad(0, 0)
            load_quad(0, 1)
            load_max(0, 0)
            with sp.Fori(0, X_QUADS - 1) as qd:
                load_max(qd, 1)
                load_quad(qd + 1, 0)
                store_y(qd, 0)
                load_max(qd + 1, 0)
                load_quad(qd + 1, 1)
                store_y(qd, 1)
            load_max(X_QUADS - 1, 1)
            store_y(X_QUADS - 1, 0)
            store_y(X_QUADS - 1, 1)
            sp.wait_ge(y_stored, 16 * NQ * XI + 16)
            sp.wait_ge(lora_stored, 16 * (NT + 2))
            sp.dma_start(write1, d["write1"]).then_inc(w2_loaded, 16)
            sp.dma_start(write2, d["write2"]).then_inc(w2_loaded, 16)
            sp.dma_start(read2, d["read2"]).then_inc(w2_loaded, 16)
            for n in range(2):
                sp.dma_start(du[n], d[f"du{n + 1}"]).then_inc(w2_loaded, 16)
            sp.dma_start(kern, d["kern"]).then_inc(kern_loaded, 16)
            sp.dma_start(lora_at[:, :, RANK:], d["lora_as"]).then_inc(kern_loaded, 16)
            sp.dma_start(lora_bt[RANK:R2, :], d["lora_bs"]).then_inc(kern_loaded, 16)
            def load_y(i):
                sp.wait_ge(W["w_mm"][0], i + 1)
                sp.dma_start(yT, y_scr.rearrange("(k p) t -> p k t", p=P)[:, :, ds(i * P, P)]).then_inc(yT_loaded, 16)

            def load_adapters(i):
                sp.wait_ge(f_mm, i + 1)
                sp.dma_start(lora_at[:, :, 0:RANK], a_scr[ds(i, 1)].rearrange("o p (c r) -> (o p) c r", c=KC)).then_inc(lo_loaded, 16)
                sp.dma_start(lora_bt[0:RANK, :], b_scr[ds(i * RANK, RANK), :]).then_inc(lo_loaded, 16)

            def store_out(i):
                sp.wait_ge(out_ready, i + 1)
                sp.dma_start(out[ds(i * P, P), :], out_t).then_inc(out_stored, 16)

            sp.sem_inc(f_mm, 1)
            sp.sem_inc(W["w_mm"][0], 1)
            for i in range(3):
                load_y(i)
            load_adapters(0)
            with sp.Fori(2, NT - 1) as i:
                load_y(i + 1)
                load_adapters(i - 1)
                store_out(i - 2)
            for i in (NT - 1, NT):
                load_adapters(i - 1)
                store_out(i - 2)
            store_out(NT - 1)
            sp.wait_ge(out_stored, 16 * NT + 16)

        @block.gpsimd
        def _(pool):
            pool.memset(w_abs[:, QKV:], 0.0).then_inc(o_summed, 2)
            pool.memset(ident[:], 0.0).then_inc(made, 1)
            pool.memset(ident_bf[:], 0.0).then_inc(made, 1)
            pool.memset(mask_qk[:], 0.0).then_inc(made, 1)
            pool.memset(mask_kq[:], 0.0).then_inc(made, 1)
            pool.memset(mean_w, 1.0 / D).then_inc(made, 1)
            pool.memset(ones32[:], 1.0).then_inc(made, 1)
            pool.memset(minus_half[:], -0.5).then_inc(made, 1)
            pool.wait_ge(made, 4)
            for t in (ident, ident_bf):
                pool.affine_select(out=t[:], in_=t[:], compare_op=ALU.not_equal, fill=1.0, base=0,
                                   pattern=[[-1, P]], channel_multiplier=1).then_inc(made, 1)
            pool.affine_select(out=mask_qk[:], in_=mask_qk[:], compare_op=ALU.is_ge, fill=-1e30, base=0,
                               pattern=[[-1, P]], channel_multiplier=1).then_inc(made, 1)
            pool.affine_select(out=mask_kq[:], in_=mask_kq[:], compare_op=ALU.is_ge, fill=-1e30, base=0,
                               pattern=[[1, P]], channel_multiplier=-1).then_inc(made, 1)
            for u in range(2):
                pool.memset(q_op[u][:].bitcast(F32), 0.0).then_inc(made, 1)
            pool.wait_ge(made, 13)
            for u in range(2):
                pool.memset(k_op[u][A_MAX:A_ROWS, :].bitcast(F32), 1.0).then_inc(made, 1)
            pool.wait_ge(made, 15)
            with pool.Fori(0, NT // 2) as it:
                for u in range(2):
                    i = it * 2 + u
                    pool.wait_ge(ln_step, 4 * i + 4)
                    pool.tensor_tensor(rstd[:, u, :], ve[:, u, :], minus_half[:, 0:1], ALU.pow).then_inc(ln_rstd, 1)
                    pool.wait_ge(abs_taken, i + 1)
                    pool.wait_ge(o_summed, i + 2)
                    pool.tensor_tensor(w_abs[:, QKV:], w_in[u][:, QKV:], w_abs[:, QKV:], ALU.add).then_inc(o_summed, 1)
            for u in range(4):
                pool.wait_ge(staged_out[u], 16 * 8 + 32 * NI // 4)
            pool.memset(k_op[2][A_MAX:A_ROWS, :].bitcast(F32), 1.0).then_inc(made, 1)
            pool.wait_ge(made, 16)

            def values(t, k):
                i = t * 3 + k
                if not (isinstance(i, int) and i < 3):
                    pool.wait_ge(pv_done, 8 * i - 8)
                pool.tensor_copy(v_g[:, k % 3].rearrange("p t e -> p (t e)").unsqueeze(1), v_steps[:, ds(i, 1), :]).then_inc(vg_ready, 1)

            def normalise(t, k):
                i = t * 3 + k
                pool.wait_ge(o_copied, 2 * i + 4)
                pool.wait_ge(den_rec, 4 * i + 4)
                pool.wait_ge(att_lo_ready, i + 1)
                pool.tensor_tensor(att, o_sb, den_sb, ALU.mult).then_inc(att_ready, 1)
                pool.wait_ge(att_hi_ready, i + 1)
                pool.tensor_tensor(attT_lo[:, ds(i, 1), :], att.unsqueeze(1), attT_hi[:, ds(i, 1), :], ALU.subtract).then_inc(att_lo_ready, 1)

            pool.sem_inc(att_lo_ready, 1)
            pool.sem_inc(att_ready, 1)
            pool.wait_ge(v_ready, NT + 2)
            values(0, 0)
            values(0, 1)
            with pool.Fori(0, A_ROUNDS) as t:
                for k in (1, 2, 3):
                    values(t, k + 1)
                    normalise(t, k - 1)
            for i in range(NI - 3, NI):
                if i + 1 < NI:
                    values(0, i + 1)
                normalise(0, i - 1)
            normalise(0, NI - 1)
            pool.wait_ge(att_lo_ready, NI + 1)
            pool.wait_ge(pv_done, 8 + 2 * QT * NI)
            pool.sem_inc(xatt_free, 1)
            pool.memset(v_x, 0.0).then_inc(vx_zero, 1)
            with pool.Fori(0, NT) as i:
                pool.wait_ge(l_step, 5 * i + 5)
                pool.tensor_tensor(rstds[:, ds(i, 1)], ves[:], minus_half[:, 0:1], ALU.pow).then_inc(l_rstd, 1)
                pool.wait_ge(y_step, 10 * i + 10)
                pool.tensor_tensor(rs3[:], ve3[:], minus_half[:, 0:3], ALU.pow).then_inc(y_rstd, 1)
            pool.wait_ge(y_rstd, NT)
            pool.memset(kr[X_MAX:P, :].bitcast(F32), 0.0).then_inc(k_ones, 1)
            pool.wait_ge(k_ones, 1)
            pool.memset(kr[X_MAX:X_MAX + 2, :].bitcast(F32), 1.0).then_inc(k_ones, 1)

            def x_values(qd, b):
                i = qd * 2 + b
                pool.wait_ge(xpv_done, 4 * i + 4)
                pool.tensor_copy(v_q[:, b], v_x[:, b * QT:(b + 1) * QT, ds(qd * NQ * 32, NQ * 32)]).then_inc(xv_ready, 1)

            def x_normalise(qd, b):
                i = qd * 2 + b
                pool.wait_ge(xden_rec, i + 1)
                pool.wait_ge(y_stored, 16 * NQ * i + 16)
                pool.tensor_tensor(att, o_sb, den_sb, ALU.mult).then_inc(xatt_ready, 1)

            pool.wait_ge(k_ones, 2)
            pool.wait_ge(vx_ready, NT + 1)
            pool.wait_ge(qkv_mm, NT)
            pool.sem_inc(y_stored, 16)
            x_values(0, 0)
            x_values(0, 1)
            with pool.Fori(0, X_QUADS - 1) as qd:
                x_normalise(qd, 0)
                x_values(qd + 1, 0)
                x_normalise(qd, 1)
                x_values(qd + 1, 1)
            x_normalise(X_QUADS - 1, 0)
            x_normalise(X_QUADS - 1, 1)

            def write(k, i, h):
                h3 = h.rearrange("p (s r c) -> p s r c", s=HS, r=RH)
                a3 = abar[:, 0:3 * H].rearrange("p (s r c) -> p s r c", s=HS, r=RH)
                pool.wait_ge(W["sp_ready"][k], i + 1)
                pool.tensor_tensor(a3, sp_b[:, 0:H].rearrange("p (s r) -> p s r", s=HS).unsqueeze(3).broadcast_to([P, HS, RH, C - 1]),
                                   sp_b[:, H:].rearrange("p (r c) -> p r c", r=RH).unsqueeze(1).broadcast_to([P, HS, RH, C - 1]),
                                   ALU.mult).then_inc(W["da_ready"][k], 1)
                pool.wait_ge(W["abar_ready"][k], i + 1)
                pool.tensor_tensor(h_a.rearrange("p (s r c) -> p s r c", s=HS, r=RH), h3[:, :, :, 0:C - 1], a3,
                                   ALU.mult).then_inc(W["ha_ready"][k], 1)

            def round_(i, u, first, second, dense):
                if first:
                    write(0, i, h_in)
                    pool.wait_ge(y2_step, 5 * i + 5)
                    pool.tensor_tensor(rs3[:, 0:2], ve3[:, 0:2], minus_half[:, 0:2], ALU.pow).then_inc(y2_rstd, 1)
                if second:
                    write(1, i - 1, h_mid[1 - u])
                    pool.wait_ge(f_step, 4 * i)
                    pool.tensor_tensor(rstd[:, 0, :], ves[:], minus_half[:, 0:1], ALU.pow).then_inc(f_rstd, 1)

            run_rounds(pool, round_)

        @block.scalar
        def _(act):
            with act.Fori(0, NT // 2) as it:
                for u in range(2):
                    i = it * 2 + u
                    act.wait_ge(w_loaded[u], 16 * (it + 1))
                    act.activation(sign_qkv[:, ds(i, 1), :], w_in[u][:, 0:QKV].unsqueeze(1), ACT.Sign).then_inc(signs_done, 1)
                    act.activation(sign_o[:, ds(i, 1), :], w_in[u][:, QKV:].unsqueeze(1), ACT.Sign).then_inc(signs_done, 1)
                    act.wait_ge(xT_done, i + 3)
                    for h in range(2):
                        act.activation(xnT_hi[:, 4 * h:4 * h + 4, ds(i * P, P)],
                                       psum[:, 2 * u + h, :].rearrange("p (c n) -> p c n", c=4), ACT.Copy).then_inc(xT_hi, 1)
            act.wait_ge(c_ready, 5)
            for n in range(4):
                act.wait_ge(qk_mm, n + 1)
                act.activation(stage[n][0], psum[:, n, :], ACT.Identity, scale=c_k[:, n % 2:n % 2 + 1]).then_inc(qk_hi, 1)
            act.wait_ge(trig_done, 1)
            for k in range(2):
                act.activation(trig[:, k], trig_r[:, k], ACT.Sin).then_inc(trig_done, 1)
            act.wait_ge(trig_done, 2)
            act.activation(trig[:, 2], trig[:, 0], ACT.Copy, scale=-1.0).then_inc(trig_done, 1)
            for r in range(R4):
                act.wait_ge(lora_mm, r + 1)
                act.activation(a_eff[:, :, :, r * R8:(r + 1) * R8],
                               psum[:, r, :].rearrange("p (c b r) -> p b c r", c=KC, b=NT), ACT.Copy).then_inc(lora_ready, 1)
            with act.Fori(0, NI // 4) as it:
                for u in range(4):
                    i = it * 4 + u
                    wait_apart(act, (qk_mm, i + 5), (staged_out[u], 32 * it + 128))
                    act.activation(stage[u][0], psum[:, u, :], ACT.Identity, scale=c_q[:, ds(it * 2 + u // 2, 1)]).then_inc(qk_hi, 1)
            act.sem_inc(pv_done, 8)

            def exp(t, k, n):
                i = t * 3 + k
                kt, j = n // 4, n % 4
                if j == 0:
                    act.wait_ge(pv_done, 8 * i + 2 * kt + 2)
                act.wait_ge(st_mm, 16 * i + n + 49)
                act.activation(prob_a[:, kt, j, :], psum[:, 4 + n % 2, :], ACT.Exp, scale=A_SCALE).then_inc(p_ready, 1)

            def copy_out(t, k, n, bank, to):
                i = t * 3 + k
                act.wait_ge(pv_done, 8 * i + 15 + n)
                act.wait_ge(att_ready, i + 1)
                act.activation(to, psum[:, bank, :], ACT.Copy).then_inc(o_copied, 1)

            def att_hi(t, k):
                i = t * 3 + k
                act.wait_ge(att_ready, i + 2)
                act.activation(attT_hi[:, ds(i, 1), :], att.unsqueeze(1), ACT.Copy).then_inc(att_hi_ready, 1)

            def max_hi(t, k):
                i = t * 3 + k
                act.wait_ge(mT_done, i + 1)
                if k:
                    act.wait_ge(m_loaded[(k - 1) % 3], 32 * (t + (k - 1) // 3 + 1))
                act.activation(m_hi[:], psum[0:16, 0, 0:P], ACT.Copy).then_inc(m_hi_ready, 1)

            def step(t, k, first=False, last=False):
                for n in range(16):
                    exp(t, k, n)
                    if n == 3 and not first:
                        copy_out(t, k - 1, 0, 7, den_sb)
                    if n == 5 and not first:
                        copy_out(t, k - 1, 1, 6, o_sb)
                    if n == 11 and not last:
                        max_hi(t, k + 1)
                    if n == 15 and not first:
                        att_hi(t, k - 1)

            max_hi(0, 0)
            step(0, 0, first=True)
            with act.Fori(0, A_ROUNDS) as t:
                for k in (1, 2, 3):
                    step(t, k)
            for i in range(NI - 3, NI):
                step(0, i, last=i == NI - 1)
            copy_out(0, NI - 1, 0, 7, den_sb)
            copy_out(0, NI - 1, 1, 6, o_sb)
            att_hi(0, NI - 1)
            act.wait_ge(vx_zero, 1)
            g0, b0 = COLS["g1"][0], COLS["b1"][0]
            act.sem_inc(qk_stored, 32)
            with act.Fori(0, NT) as i:
                act.wait_ge(hT_mm, i + 1)
                for h in range(2):
                    act.activation(hT[:, 4 * h:4 * h + 4, :], psum[:, 2 + h, :].rearrange("p (c n) -> p c n", c=4), ACT.Copy).then_inc(hT_ready, 1)
                act.wait_ge(ynT_mm, i + 1)
                for n in range(6):
                    act.activation(ynT[:, n, :], psum[:, 6 + n // 4, (n % 4) * P:(n % 4 + 1) * P], ACT.Identity,
                                   scale=cols[:, g0 + n:g0 + n + 1], bias=cols[:, b0 + n:b0 + n + 1]).then_inc(ynT_ready, 1)
                act.wait_ge(qkv_mm, i + 1)
                act.activation(v_x[:, ds(i, 1), :].rearrange("p o (h e) -> p (o h) e", e=32)[:, :, 0:X_HD],
                               psum[:, 3, 0:H].rearrange("p (h e) -> p h e", e=X_HD), ACT.Copy).then_inc(vx_ready, 1)
                act.wait_ge(rT_mm, i + 2)
                act.wait_ge(qk_stored, 32 * i + 32)
                act.activation(hi_st[:], psum[:, 4, :], ACT.Copy).then_inc(r_hi, 1)
            act.sem_inc(xpv_done, 8)

            def x_max_hi(qd, b, first=False):
                i = qd * 2 + b
                act.wait_ge(xmT_done, i + 1)
                if not first:
                    act.wait_ge(xm_loaded[1 - b], 32 * (qd + b))
                act.activation(m_hi[:], psum[0:16, 1, 0:P], ACT.Copy).then_inc(xm_hi, 1)

            def x_step(qd, b, q1, b1, first=False):
                i = qd * 2 + b
                for kt in range(QT):
                    act.wait_ge(xpv_done, 4 * i + kt + 7)
                    for j in range(NQ):
                        n = 4 * kt + j
                        act.wait_ge(xst_mm, 16 * i + n + 33)
                        act.activation(prob[:, kt % 2, j, 0:S - kt * P], psum[:, 4 + n % 2, 0:S - kt * P], ACT.Exp, scale=X_SCALE).then_inc(xp_ready, 1)
                act.wait_ge(xpv_done, 4 * i + 12)
                if not first:
                    act.wait_ge(xatt_ready, i)
                act.activation(o_sb, psum[:, 6, :], ACT.Copy).then_inc(xo_copied, 1)
                act.activation(den_sb, psum[:, 7, :], ACT.Copy).then_inc(xo_copied, 1)
                if q1 is not None:
                    x_max_hi(q1, b1)

            x_max_hi(0, 0, True)
            x_step(0, 0, 0, 1, True)
            x_step(0, 1, 1, 0)
            with act.Fori(1, X_QUADS - 1) as qd:
                x_step(qd, 0, qd, 1)
                x_step(qd, 1, qd + 1, 0)
            x_step(X_QUADS - 1, 0, X_QUADS - 1, 1)
            x_step(X_QUADS - 1, 1, None, None)

            def low_rank(k, i):
                act.wait_ge(W["w_mm"][k], i + 2 - k)
                act.activation(low[k], psum[0:DR, 2 * k + 1, 0:P], ACT.Copy).then_inc(W["low_ready"][k], 1)

            def exps(k, i):
                w = {n: s[k] for n, s in W.items()}
                act.wait_ge(w["az_ready"], i + 1)
                act.activation(e_b, e_b, ACT.Exp, scale=-1.0).then_inc(w["e_ready"], 1)
                act.wait_ge(w["e_ready"], i + 1)
                act.activation(e_b, e_b, ACT.Ln, bias=1.0).then_inc(w["l_ready"], 1)
                act.wait_ge(w["da_ready"], i + 1)
                act.activation(abar[:, 0:3 * H], abar[:, 0:3 * H], ACT.Exp, scale=-1.0).then_inc(w["abar_ready"], 1)

            def turned(to, bank, done):
                for h in range(2):
                    act.activation(to[:, 4 * h:4 * h + 4, :], psum[:, bank + h, :].rearrange("p (c n) -> p c n", c=4), ACT.Copy).then_inc(done, 1)

            g2, b2 = COLS["g2"][0], COLS["b2"][0]

            def round_(i, u, first, second, dense):
                if first:
                    low_rank(0, i)
                if dense:
                    act.wait_ge(fT_mm, i - 1)
                    turned(hT_f, 6, fT_ready)
                if first:
                    exps(0, i)
                if second:
                    low_rank(1, i - 1)
                if dense:
                    act.wait_ge(ax_mm, i - 1)
                    act.activation(ax, psum[:, 5, 0:R2], ACT.Copy).then_inc(ax_ready, 1)
                if first:
                    act.wait_ge(h2T_mm, i + 1)
                    turned(hT, 6, h2T_ready)
                if dense:
                    act.wait_ge(axT_mm, i - 1)
                    act.activation(axT, psum[0:R2, 7, 0:P], ACT.Copy).then_inc(axT_ready, 1)
                if first:
                    act.wait_ge(y2T_mm, i + 1)
                    for n in range(4):
                        act.activation(ynT[:, n, :], psum[:, 7, n * P:(n + 1) * P], ACT.Identity,
                                       scale=cols[:, g2 + n:g2 + n + 1], bias=cols[:, b2 + n:b2 + n + 1]).then_inc(y2T_ready, 1)
                if second:
                    exps(1, i - 1)
                if first:
                    act.wait_ge(gu_mm, i + 1)
                    act.activation(mlpT_f.rearrange("p (h n) -> p h n", h=2), psum[:, 0:2, :], ACT.Tanh, scale=0.5).then_inc(tanh_ready, 1)

            run_rounds(act, round_)

        @block.vector
        def _(dve):
            dve.memset(w_abs[:, 0:QKV], 0.0).then_inc(qkv_summed, 2)
            dve.wait_ge(s_const, 64)
            dve.tensor_copy(pos_f[:], pos_i[:]).then_inc(ang_step, 1)
            dve.wait_ge(ang_step, 1)
            for f in range(HALF):
                dve.tensor_scalar(ang[:, :, f], pos_f[:], float(ROPE_INV[f]), None, ALU.mult).then_inc(ang_step, 1)
            dve.wait_ge(ang_step, 1 + HALF)
            n_step = 1 + HALF

            def link(ins):
                nonlocal n_step
                ins.then_inc(ang_step, 1)
                n_step += 1
                dve.wait_ge(ang_step, n_step)

            for k in range(2):
                n, r = trig_n[:, k], trig_r[:, k]
                link(dve.tensor_scalar(n, ang, float(1 / TWO_PI), 0.25 * k, ALU.mult, ALU.add))
                link(dve.tensor_scalar(n, n, MAGIC, None, ALU.add))
                link(dve.tensor_scalar(n, n, -MAGIC, None, ALU.add))
                link(dve.scalar_tensor_tensor(r, n, -TP1, ang, ALU.mult, ALU.add))
                link(dve.scalar_tensor_tensor(r, n, -TP2, r, ALU.mult, ALU.add))
                link(dve.scalar_tensor_tensor(r, n, -TP3, r, ALU.mult, ALU.add))
                link(dve.tensor_scalar(r, r, float(k * np.pi / 2), 3.1415925, ALU.add, ALU.min))
                link(dve.tensor_scalar(r, r, -3.1415925, None, ALU.max))
            dve.sem_inc(trig_done, 1)

            with dve.Fori(0, NT // 2) as it:
                for u in range(2):
                    i = it * 2 + u
                    dve.wait_ge(x_slot[u], 16 * (it + 1))
                    for h in range(2):
                        dve.bn_stats(st[:, u, h, :], x_in[:, u, h * 512:(h + 1) * 512]).then_inc(ln_step, 1)
                    wait_apart(dve, (ln_step, 4 * i + 2))
                    dve.bn_aggr(mv[:, u, :], st[:, u]).then_inc(ln_step, 1)
                    dve.wait_ge(ln_step, 4 * i + 3)
                    dve.tensor_scalar(ve[:, u, :], mv[:, u, 1:2], LN_EPS, None, ALU.add).then_inc(ln_step, 1)
                    dve.wait_ge(ln_rstd, i + 1)
                    dve.tensor_scalar(x_in[:, u, :], x_in[:, u, :], mv[:, u, 0:1], rstd[:, u, 0:1],
                                      ALU.subtract, ALU.mult).then_inc(xn_ready, 1)
                    dve.wait_ge(signs_done, 2 * i + 2)
                    dve.tensor_scalar(w_in[u].bitcast(I32), w_in[u].bitcast(I32), 0x7FFFFFFF, None, ALU.bitwise_and).then_inc(abs_taken, 1)
                    dve.wait_ge(qkv_summed, i + 2)
                    dve.wait_ge(abs_taken, i + 1)
                    dve.tensor_tensor(w_abs[:, 0:QKV], w_in[u][:, 0:QKV], w_abs[:, 0:QKV], ALU.add).then_inc(qkv_summed, 1)
                    for h in range(2):
                        dve.wait_ge(xT_hi, 2 * i + h + 1)
                        dve.tensor_tensor(xnT_lo[:, 4 * h:4 * h + 4, ds(i * P, P)],
                                          psum[:, 2 * u + h, :].rearrange("p (c n) -> p c n", c=4),
                                          xnT_hi[:, 4 * h:4 * h + 4, ds(i * P, P)], ALU.subtract).then_inc(xT_free, 1)
            dve.wait_ge(means_done, 1)
            for h in range(2):
                dve.scalar_tensor_tensor(c_o[:, h * 512:(h + 1) * 512], psum[:, 4 + h, :], 1e-8,
                                         scale_rows[:, KVD + h * 512:KVD + (h + 1) * 512], ALU.max, ALU.mult).then_inc(c_ready, 1)
            dve.scalar_tensor_tensor(c_v, psum[:, 6, 0:KVD], 1e-8, scale_rows[:, 0:KVD], ALU.max, ALU.mult).then_inc(c_ready, 1)
            dve.scalar_tensor_tensor(c_k[:], psum[:, 7, KC:KC + 2], 1e-8, cols[:, slice(*COLS["k_scale"])], ALU.max, ALU.mult).then_inc(c_ready, 1)
            dve.scalar_tensor_tensor(c_q[:], psum[:, 7, 0:KC], 1e-8, cols[:, slice(*COLS["q_scale"])], ALU.max, ALU.mult).then_inc(c_ready, 1)
            dve.wait_ge(c_ready, 5)
            for n in range(4):
                dve.wait_ge(qk_hi, n + 1)
                dve.scalar_tensor_tensor(stage[n][1], psum[:, n, :], c_k[:, n % 2:n % 2 + 1], stage[n][0].bitcast(F32), ALU.mult, ALU.subtract).then_inc(qk_lo, 1)
            with dve.Fori(0, NT // 2) as it:
                for u in range(2):
                    i = it * 2 + u
                    dve.wait_ge(v_mm, i + 1)
                    dve.scalar_tensor_tensor(v_heads[:, :, ds(i, 1), :].rearrange("p g o e -> p g (o e)"),
                                             psum[:, 4 + u, 0:KVD].rearrange("p (g e) -> p g e", e=A_HD), V_GAIN,
                                             c_v.rearrange("p (g e) -> p g e", e=A_HD), ALU.mult, ALU.mult).then_inc(v_ready, 1)
            dve.wait_ge(trig_done, 4)
            for m in range(2):
                for h in range(2):
                    dve.wait_ge(lora_mm, R4 + 2 * m + h + 1)
                    dve.tensor_copy(b_eff[:, m, h * 512:(h + 1) * 512], psum[:, 4 + 2 * m + h, :]).then_inc(lora_ready, 1)
            with dve.Fori(0, NI // 4) as it:
                for u in range(4):
                    i = it * 4 + u
                    dve.wait_ge(qk_hi, i + 5)
                    dve.scalar_tensor_tensor(stage[u][1], psum[:, u, :], c_q[:, ds(it * 2 + u // 2, 1)], stage[u][0].bitcast(F32),
                                             ALU.mult, ALU.subtract).then_inc(qk_lo, 1)

            def maximum(t, k, n):
                i = t * 3 + k
                dve.wait_ge(s_mm, 16 * i + n + 1)
                dve.tensor_reduce(m_neg[:, k % 3, n:n + 1], psum[:, 2 + n % 2, :], AX_X, ALU.max, negate=True).then_inc(s_max, 1)

            def max_lo(t, k):
                i = t * 3 + k
                dve.wait_ge(m_hi_ready, i + 1)
                dve.tensor_tensor(m_lo[:], psum[0:16, 0, 0:P], m_hi[:].bitcast(F32), ALU.subtract).then_inc(m_lo_ready, 1)

            def invert(t, k, n):
                i = t * 3 + k
                if n == 0:
                    dve.wait_ge(o_copied, 2 * i + 3)
                part = den_sb[:, n * P:(n + 1) * P]
                dve.reciprocal(part, part).then_inc(den_rec, 1)

            def step(t, k, first=False, left=2):
                for n in range(8):
                    if left > 0:
                        maximum(t, k + 1, 8 + n)
                    if n in (4, 6) and not first:
                        invert(t, k - 1, n // 2 - 2)
                for n in range(8):
                    if left > 1:
                        maximum(t, k + 2, n)
                    if n in (0, 2) and not first:
                        invert(t, k - 1, 2 + n // 2)
                    if n == 3 and left > 0:
                        max_lo(t, k + 1)

            for n in range(16):
                maximum(0, 0, n)
            max_lo(0, 0)
            for n in range(8):
                maximum(0, 1, n)
            step(0, 0, first=True)
            with dve.Fori(0, A_ROUNDS) as t:
                for k in (1, 2, 3):
                    step(t, k)
            for i in range(NI - 3, NI):
                step(0, i, left=NI - 1 - i)
            for n in range(4):
                invert(0, NI - 1, n)

            dve.wait_ge(trig_done, 4)
            def residual(i, u, use, h_done):
                for h in range(2):
                    dve.wait_ge(op_mm, 2 * i + h + 1)
                    if h == 0 and h_done is not None:
                        dve.wait_ge(hT_mm, h_done)
                    dve.scalar_tensor_tensor(y0[:, h * 512:(h + 1) * 512], psum[:, h, :], 1.0 / V_GAIN, c_o[:, h * 512:(h + 1) * 512],
                                             ALU.mult, ALU.mult).then_inc(y0_ready, 1)
                dve.wait_ge(y0_ready, 2 * i + 4)
                dve.wait_ge(x_again[u], 16 * use)
                dve.tensor_tensor(x1[:, ds(i, 1), :], y0.unsqueeze(1), x_in[:, u:u + 1, :], ALU.add).then_inc(x1_ready, 1)
                wait_apart(dve, (x1_ready, i + 1))
                for h in range(2):
                    dve.bn_stats(st[:, 0, h, :], x1[:, ds(i, 1), h * 512:(h + 1) * 512]).then_inc(l_step, 1)
                wait_apart(dve, (l_step, 5 * i + 2))
                dve.bn_aggr(mv[:, 0, :], st[:, 0]).then_inc(l_step, 1)
                dve.wait_ge(l_step, 5 * i + 3)
                dve.tensor_copy(mvs[:, ds(2 * i, 2)], mv[:, 0, :]).then_inc(l_step, 1)
                dve.tensor_scalar(ves[:], mv[:, 0, 1:2], LN_EPS, None, ALU.add).then_inc(l_step, 1)
                dve.wait_ge(l_rstd, i + 1)
                dve.tensor_scalar(h_st, x1[:, ds(i, 1), :].rearrange("p o n -> p (o n)"), mvs[:, ds(2 * i, 1)], rstds[:, ds(i, 1)],
                                  ALU.subtract, ALU.mult).then_inc(h_ready, 1)

            def read(i):
                dve.wait_ge(y_mm, i + 1)
                y = [psum[:, 4 + h, 0:4 * 3 * HC].rearrange("p (c o n) -> p c o n", c=4, o=3) for h in range(2)]
                for o in range(3):
                    for h in range(2):
                        dve.bn_stats(st3[:, o, h, :], y[h][:, :, o, :]).then_inc(y_step, 1)
                wait_apart(dve, (y_step, 10 * i + 6))
                for o in range(3):
                    dve.bn_aggr(mv3[:, o, :], st3[:, o]).then_inc(y_step, 1)
                dve.wait_ge(y_step, 10 * i + 9)
                dve.tensor_scalar(ve3[:], mv3[:, :, 1], LN_EPS, None, ALU.add).then_inc(y_step, 1)
                dve.wait_ge(y_rstd, i + 1)
                dve.wait_ge(rT_mm, i + 1)
                for o in range(3):
                    for h in range(2):
                        dve.tensor_scalar(yn[:, o * H + h * P:o * H + (h + 1) * P].rearrange("p (c n) -> p c n", c=4), y[h][:, :, o, :],
                                          mv3[:, o, 0:1], rs3[:, o:o + 1], ALU.subtract, ALU.mult).then_inc(yn_ready, 1)

            def rope(i):
                dve.wait_ge(qkv_mm, i + 1)
                qk = psum[:, 2, :].rearrange("p (h e f) -> p h e f", e=2, f=HALF)
                to = rot.rearrange("p (h e f) -> p h e f", e=2, f=HALF)
                other = rope_a.rearrange("p (h f) -> p h f", f=HALF)

                def angle(k):
                    return trig[:, k, ds(i, 1), :].broadcast_to([P, 2 * X_NH, HALF])

                for e in range(2):
                    dve.tensor_tensor(to[:, :, e, :], qk[:, :, e, :], angle(1), ALU.mult).then_inc(rope_step, 1)
                for e in range(2):
                    dve.tensor_tensor(other, qk[:, :, 1 - e, :], angle(0 if e else 2), ALU.mult).then_inc(rope_step, 1)
                    dve.wait_ge(rope_step, 6 * i + 9 + 2 * e)
                    dve.tensor_tensor(to[:, :, e, :], to[:, :, e, :], other, ALU.add).then_inc(rope_step, 1)
                    dve.wait_ge(rope_step, 6 * i + 10 + 2 * e)

            def split(i):
                dve.wait_ge(r_hi, i + 1)
                dve.tensor_tensor(lo_st[:], psum[:, 4, :], hi_st[:].bitcast(F32), ALU.subtract).then_inc(r_lo, 1)

            dve.sem_inc(rT_mm, 1)
            dve.sem_inc(y0_ready, 2)
            residual(0, 0, 1, None)
            with dve.Fori(0, NT // 2 - 1) as it:
                for u in range(2):
                    i = it * 2 + u
                    read(i)
                    rope(i)
                    split(i)
                    residual(i + 1, 1 - u, it + 1 + u, i + 1)
            read(NT - 2)
            rope(NT - 2)
            split(NT - 2)
            residual(NT - 1, 1, NT // 2, NT - 1)
            read(NT - 1)
            rope(NT - 1)
            split(NT - 1)

            def x_maxima(qd, b):
                i = qd * 2 + b
                for n in range(16):
                    dve.wait_ge(xs_mm, 16 * i + n + 1)
                    dve.tensor_reduce(m_neg[:, b, n:n + 1], psum[:, 2 + n % 2, 0:(n % QT + 1) * P], AX_X, ALU.max, negate=True).then_inc(xs_max, 1)

            def x_max_lo(qd, b):
                i = qd * 2 + b
                dve.wait_ge(xm_hi, i + 1)
                dve.tensor_tensor(m_lo[:], psum[0:16, 1, 0:P], m_hi[:].bitcast(F32), ALU.subtract).then_inc(xm_lo, 1)

            def x_invert(qd, b):
                i = qd * 2 + b
                dve.wait_ge(xo_copied, 2 * i + 4)
                dve.reciprocal(den_sb, den_sb).then_inc(xden_rec, 1)

            def x_step(qd, b, q1, b1, first=False):
                if q1 is not None:
                    x_maxima(q1, b1)
                if not first:
                    x_invert(*((qd, 0) if b else (qd - 1, 1)))
                if q1 is not None:
                    x_max_lo(q1, b1)

            x_maxima(0, 0)
            x_max_lo(0, 0)
            x_step(0, 0, 0, 1, True)
            x_step(0, 1, 1, 0)
            with dve.Fori(1, X_QUADS - 1) as qd:
                x_step(qd, 0, qd, 1)
                x_step(qd, 1, qd + 1, 0)
            x_step(X_QUADS - 1, 0, X_QUADS - 1, 1)
            x_step(X_QUADS - 1, 1, None, None)
            x_invert(X_QUADS - 1, 1)

            def write(k, i, h, to):
                w = {n: s[k] for n, s in W.items()}
                bank = 2 * k
                wab = rows[:, slice(*ROWS[f"wab{k + 1}"])]
                mid = [HS, RH, C - 1]
                h4 = h.rearrange("p (s r c) -> p s r c", s=HS, r=RH)
                to4 = to.rearrange("p (s r c) -> p s r c", s=HS, r=RH)
                o2 = psum[:, bank, 0:H].rearrange("p (s r) -> p s r", s=HS)
                bb3 = bbar[:, 0:3 * H].rearrange("p (s r c) -> p s r c", s=HS, r=RH)
                bs2 = b_skip.rearrange("p (s r) -> p s r", s=HS)
                dve.wait_ge(w["du_mm"], i + 1)
                dve.tensor_tensor(z_b[:, 0:H], psum[:, bank + 1, H:2 * H], rows[:, slice(*ROWS[f"du{k + 1}"])], ALU.add).then_inc(w["z_ready"], 1)
                dve.tensor_tensor(z_b[:, H:], psum[:, bank, H:N_Z], wab[:, 0:N_A], ALU.add).then_inc(w["z_ready"], 1)
                dve.tensor_tensor(ab_b, psum[:, bank, N_Z:H + N_AB], wab[:, N_A:], ALU.add).then_inc(w["z_ready"], 1)
                dve.wait_ge(w["z_ready"], 3 * i + 3)
                dve.scalar_tensor_tensor(e_b, z_b, -1.0, z_b, ALU.mult, ALU.max).then_inc(w["az_ready"], 1)
                dve.wait_ge(w["l_ready"], i + 1)
                dve.scalar_tensor_tensor(sp_b[:], z_b, 0.0, e_b, ALU.max, ALU.add).then_inc(w["sp_ready"], 1)
                dve.wait_ge(w["sp_ready"], i + 1)
                dve.tensor_scalar(rc_b, sp_b[:, H:], SSM_EPS, None, ALU.add).then_inc(w["r_step"], 1)
                dve.wait_ge(w["r_step"], 3 * i + 1)
                dve.reciprocal(rc_b, rc_b).then_inc(w["r_step"], 1)
                dve.wait_ge(w["r_step"], 3 * i + 2)
                dve.scalar_tensor_tensor(r_b, ab_b[:, 0:N_A], -1.0, rc_b, ALU.mult, ALU.mult).then_inc(w["r_step"], 1)
                dve.tensor_tensor(bs2, sp_b[:, 0:H].rearrange("p (s r) -> p s r", s=HS),
                                  ab_b[:, N_A:].unsqueeze(1).broadcast_to([P, HS, RH]), ALU.mult).then_inc(w["b_step"], 1)
                dve.wait_ge(w["b_step"], 4 * i + 1)
                dve.tensor_tensor(bs2, bs2, o2, ALU.mult).then_inc(w["b_step"], 1)
                dve.wait_ge(w["b_step"], 4 * i + 2)
                dve.tensor_tensor(to4[:, :, :, C - 1], h4[:, :, :, C - 1], bs2, ALU.add).then_inc(w["hn_ready"], 1)
                dve.wait_ge(w["abar_ready"], i + 1)
                dve.wait_ge(w["r_step"], 3 * i + 3)
                dve.scalar_tensor_tensor(bbar[:, 0:3 * H].rearrange("p (s n) -> p s n", s=HS), abar[:, 0:3 * H].rearrange("p (s n) -> p s n", s=HS),
                                         -1.0, r_b.unsqueeze(1).broadcast_to([P, HS, N_A]), ALU.add, ALU.mult).then_inc(w["b_step"], 1)
                dve.wait_ge(w["b_step"], 4 * i + 3)
                dve.tensor_tensor(bb3, bb3, o2.unsqueeze(3).broadcast_to([P] + mid), ALU.mult).then_inc(w["b_step"], 1)
                dve.wait_ge(w["b_step"], 4 * i + 4)
                dve.wait_ge(w["ha_ready"], i + 1)
                dve.tensor_tensor(to4[:, :, :, 0:C - 1], h_a.rearrange("p (s r c) -> p s r c", s=HS, r=RH), bb3, ALU.add).then_inc(w["hn_ready"], 1)

            def to_mid(i, u):
                x1_t = x1[:, ds(i, 1), :].rearrange("p o n -> p (o n)")
                dve.tensor_scalar(h_in, x1_t, mvs[:, ds(2 * i, 1)], rstds[:, ds(i, 1)], ALU.subtract, ALU.mult).then_inc(h2_ready, 1)
                dve.wait_ge(h2_ready, i + 1)
                write(0, i, h_in, h_mid[u])

            def read_2(i):
                dve.wait_ge(y2_mm, i + 1)
                y = psum[:, 6, :].rearrange("p (c o n) -> p c o n", c=KC, o=2)
                for o in range(2):
                    dve.bn_stats(st3[:, o, 0, :], y[:, :, o, :]).then_inc(y2_step, 1)
                wait_apart(dve, (y2_step, 5 * i + 2))
                for o in range(2):
                    dve.bn_aggr(mv3[:, o, :], st3[:, o, 0, :]).then_inc(y2_step, 1)
                dve.wait_ge(y2_step, 5 * i + 4)
                dve.tensor_scalar(ve3[:, 0:2], mv3[:, 0:2, 1], LN_EPS, None, ALU.add).then_inc(y2_step, 1)
                dve.wait_ge(y2_rstd, i + 1)
                for o in range(2):
                    dve.tensor_scalar(yn[:, o * H:(o + 1) * H].rearrange("p (c n) -> p c n", c=KC), y[:, :, o, :],
                                      mv3[:, o, 0:1], rs3[:, o:o + 1], ALU.subtract, ALU.mult).then_inc(y2n_ready, 1)

            def gated(i):
                dve.wait_ge(tanh_ready, i + 1)
                t2 = mlpT_f.rearrange("p (h n) -> p h n", h=2)
                dve.scalar_tensor_tensor(t2, t2, 1.0, psum[:, 0:2, :], ALU.add, ALU.mult).then_inc(g_ready, 1)
                dve.wait_ge(g_ready, i + 1)
                dve.scalar_tensor_tensor(t2, t2, 0.5, psum[:, 6:8, :], ALU.mult, ALU.mult).then_inc(mlp_ready, 1)

            def to_dense(i):
                x1_t = x1[:, ds(i, 1), :].rearrange("p o n -> p (o n)")
                dve.wait_ge(W["hn_ready"][1], 2 * i + 4)
                dve.tensor_tensor(x1_t, x1_t, h_out, ALU.add).then_inc(x2_ready, 1)
                wait_apart(dve, (x2_ready, i + 1))
                for h in range(2):
                    dve.bn_stats(st[:, 0, h, :], x1[:, ds(i, 1), h * 512:(h + 1) * 512]).then_inc(f_step, 1)
                wait_apart(dve, (f_step, 4 * i + 2))
                dve.bn_aggr(mv[:, 0, :], st[:, 0]).then_inc(f_step, 1)
                dve.wait_ge(f_step, 4 * i + 3)
                dve.tensor_scalar(ves[:], mv[:, 0, 1:2], LN_EPS, None, ALU.add).then_inc(f_step, 1)
                dve.wait_ge(f_rstd, i + 1)
                dve.tensor_scalar(h_out, x1_t, mv[:, 0, 0:1], rstd[:, 0, 0:1], ALU.subtract, ALU.mult).then_inc(xf_ready, 1)

            def finish(i):
                dve.wait_ge(f_mm, i + 2)
                dve.wait_ge(out_stored, 16 * i + 16)
                o3 = out_t.rearrange("p (h n) -> p h n", h=2)
                dve.tensor_tensor(o3, psum[:, 4:6, :], rows[:, slice(*ROWS["bias"])].rearrange("p (h n) -> p h n", h=2), ALU.add).then_inc(o_step, 1)
                dve.wait_ge(o_step, i + 2)
                dve.tensor_tensor(out_t.unsqueeze(1), out_t.unsqueeze(1), x1[:, ds(i, 1), :], ALU.add).then_inc(out_ready, 1)

            def round_(i, u, first, second, dense):
                if first:
                    to_mid(i, u)
                    read_2(i)
                if second:
                    if dense:
                        dve.wait_ge(fT_mm, i - 1)
                    write(1, i - 1, h_mid[1 - u], h_out)
                if first:
                    gated(i)
                if second:
                    to_dense(i - 1)
                if dense:
                    finish(i - 2)

            dve.sem_inc(out_stored, 16)
            run_rounds(dve, round_)

        @block.tensor
        def _(pe):
            pe.sem_inc(xT_free, 4)
            pe.wait_ge(made, 11)
            with pe.Fori(0, NT // 2) as it:
                for u in range(2):
                    i = it * 2 + u
                    pe.wait_ge(xn_ready, i + 1)
                    pe.wait_ge(xT_free, 2 * i + 2)
                    for c in range(KC):
                        mm = pe.transpose(psum[:, 2 * u + c // 4, (c % 4) * P:(c % 4 + 1) * P], x_in[:, u, c * P:(c + 1) * P], ident[:])
                        if c == KC - 1:
                            mm.then_inc(xT_done, 1)
            pe.wait_ge(qkv_summed, NT + 2)
            pe.wait_ge(o_summed, NT + 2)
            for h in range(2):
                pe.matmul(psum[:, 4 + h, :], mean_w, w_abs[:, QKV + h * 512:QKV + (h + 1) * 512], start=True, stop=True)
            pe.matmul(psum[:, 6, 0:KVD], mean_w, w_abs[:, D + KVD:QKV], start=True, stop=True)
            for c in range(KC + 2):
                mm = pe.matmul(psum[:, 7, c:c + 1], w_abs[:, c * P:(c + 1) * P], mean_w[:, 0:1], start=True, stop=True)
            mm.then_inc(means_done, 1)
            pe.wait_ge(signs_done, 2 * NT)
            pe.wait_ge(xT_free, 2 * NT + 4)

            def project(bank, width, weights, tokens, swap=False):
                for c in range(KC):
                    for part in range(2):
                        x = (xnT_hi, xnT_lo)[part]
                        w = weights(c)
                        mm = pe.matmul(psum[:, bank, 0:width], *((x[:, c, tokens], w) if swap else (w, x[:, c, tokens])),
                                       start=(c == 0 and part == 0), stop=(c == KC - 1 and part == 1))
                return mm

            for n in range(4):
                b, m = n // 2, n % 2
                project(n, S, lambda c: sign_qkv[:, c, D + m * P:D + (m + 1) * P], slice(b * S, (b + 1) * S)).then_inc(qk_mm, 1)
            pe.wait_ge(c_ready, 5)
            pe.sem_inc(v_ready, 2)
            with pe.Fori(0, NT // 2) as it:
                for u in range(2):
                    i = it * 2 + u
                    pe.wait_ge(v_ready, i + 1)
                    project(4 + u, KVD, lambda c: sign_qkv[:, c, D + KVD:QKV], ds(i * P, P), swap=True).then_inc(v_mm, 1)
            pe.wait_ge(qk_lo, 4)
            pe.wait_ge(v_ready, NT + 2)
            pe.wait_ge(lora_loaded, 16 * (2 * R4 + 2))
            for r in range(R4):
                for c in range(KC):
                    mm = pe.matmul(psum[:, r, c * NT * R8:(c + 1) * NT * R8], lora_in[:, r, c * P:(c + 1) * P], gate_a, start=True, stop=True)
                mm.then_inc(lora_mm, 1)
            for m in range(2):
                for h in range(2):
                    for k in range(R4):
                        mm = pe.matmul(psum[:, 4 + 2 * m + h, :], gate_b[:, k, m * P:(m + 1) * P], lora_in[:, R4 + k, h * 512:(h + 1) * 512],
                                       start=(k == 0), stop=(k == R4 - 1))
                    mm.then_inc(lora_mm, 1)
            pe.wait_ge(lora_ready, R4 + 4)
            with pe.Fori(0, NI // 4) as it:
                for u in range(4):
                    i = it * 4 + u
                    pe.wait_ge(qk_lo, i + 1)
                    g, b = it * 2 + u // 2, u % 2
                    project(u, S, lambda c: sign_qkv[:, c, ds(g * P, P)], slice(b * S, (b + 1) * S)).then_inc(qk_mm, 1)
            pe.wait_ge(qk_lo, NI + 4)
            pe.sem_inc(s_max, 2)
            pe.sem_inc(p_ready, 2)
            pe.sem_inc(o_copied, 2)

            def score(t, k, n):
                i, u = t * 3 + k, k % 3
                if n == 0:
                    pe.wait_ge(qk_loaded[u], 96 * (t + k // 3 + 1))
                j, qt = n // QT, n % QT
                pe.wait_ge(s_max, 16 * i + n + 1)
                pe.matmul(psum[:, 2 + n % 2, :], qa_op[u][0:A_MAX, j, qt * P:(qt + 1) * P], k_op[u][0:A_MAX, :],
                          start=True, stop=True).then_inc(s_mm, 1)

            def turn_max(t, k):
                i = t * 3 + k
                pe.wait_ge(s_max, 16 * i + 18)
                if k:
                    pe.wait_ge(m_lo_ready, i)
                pe.transpose(psum[0:16, 0, 0:P], m_neg[:, k % 3, :], ident[:]).then_inc(mT_done, 1)

            def shifted(t, k, n):
                i, u = t * 3 + k, k % 3
                kt, j = n // 4, n % 4
                if n == 0:
                    pe.wait_ge(m_loaded[u], 32 * (t + k // 3 + 1))
                pe.wait_ge(p_ready, 16 * i + n + 1)
                pe.matmul(psum[:, 4 + n % 2, :], k_op[u][0:A_ROWS, kt * P:(kt + 1) * P], qa_op[u][0:A_ROWS, j, :],
                          start=True, stop=True).then_inc(st_mm, 1)

            def sums(t, k, kt, n):
                i = t * 3 + k
                bank = 7 - n
                pe.wait_ge(p_ready, 16 * i + 4 * kt + 6)
                if kt == 0:
                    pe.wait_ge(vg_ready, i + 1)
                    pe.wait_ge(o_copied, 2 * i + 1 + n)
                for j in range(A_REP):
                    mm = pe.matmul(psum[j * 32:(j + 1) * 32, bank, :], v_g[:, k % 3, kt, :] if n else ones32[:], prob_a[:, kt, j, :],
                                   start=(kt == 0), stop=(kt == QT - 1))
                mm.then_inc(pv_done, 1)

            def step(t, k, first=False, left=2):
                for n in range(16):
                    if n < 8 and left > 0:
                        score(t, k + 1, n + 8)
                    if n >= 8 and left > 1:
                        score(t, k + 2, n - 8)
                    shifted(t, k, n)
                    if n in (1, 3) and not first:
                        sums(t, k - 1, QT - 1, n // 2)
                    if n == 10 and left > 0:
                        turn_max(t, k + 1)
                    if n % 2 == 1 and n > 3:
                        sums(t, k, n // 4 - 1, n % 4 // 2)

            for n in range(16):
                score(0, 0, n)
            turn_max(0, 0)
            for n in range(8):
                score(0, 1, n)
            step(0, 0, first=True)
            with pe.Fori(0, A_ROUNDS) as t:
                for k in (1, 2, 3):
                    step(t, k)
            for i in range(NI - 3, NI):
                step(0, i, left=NI - 1 - i)
            sums(0, NI - 1, QT - 1, 0)
            sums(0, NI - 1, QT - 1, 1)

            pe.wait_ge(att_hi_ready, NI)
            pe.wait_ge(att_lo_ready, NI + 1)
            pe.wait_ge(xw_loaded, 16 * 3)

            def out_proj(i, h):
                pe.wait_ge(y0_ready, 2 * i + 2)
                for g in range(KC):
                    for part in range(2):
                        mm = pe.matmul(psum[:, h, :], (o_in_hi, o_in_lo)[part][:, g, ds(i * P, P)], sign_o[:, g, h * 512:(h + 1) * 512],
                                       start=(g == 0 and part == 0), stop=(g == KC - 1 and part == 1))
                mm.then_inc(op_mm, 1)

            def turn(bank, src, n, done):
                for c in range(n):
                    mm = pe.transpose(psum[:, bank + c // 4, (c % 4) * P:(c % 4 + 1) * P], src[:, c * P:(c + 1) * P], ident[:])
                mm.then_inc(done, 1)

            def x_tile(i, nxt):
                pe.wait_ge(h_ready, i + 1)
                pe.wait_ge(vx_ready, i + 1)
                pe.wait_ge(rope_step, 6 * i + 6)
                turn(2, h_st, KC, hT_mm)
                if nxt:
                    out_proj(i + 1, 0)
                pe.wait_ge(hT_ready, 2 * i + 2)
                pe.wait_ge(r_lo, i + 1)
                for c in range(KC):
                    mm = pe.matmul(psum[:, 4 + c // 4, (c % 4) * 3 * HC:(c % 4 + 1) * 3 * HC], hT[:, c, :], read1[:, c, :], start=True, stop=True)
                mm.then_inc(y_mm, 1)
                if nxt:
                    out_proj(i + 1, 1)
                pe.wait_ge(yn_ready, 6 * i + 6)
                turn(6, yn, 6, ynT_mm)
                pe.wait_ge(ynT_ready, 6 * i + 6)
                for o in range(3):
                    for k in range(2):
                        mm = pe.matmul(psum[:, 2 + o // 2, (o % 2) * H:(o % 2 + 1) * H], ynT[:, 2 * o + k, :], wqkv[:, 2 * o + k, :],
                                       start=(k == 0), stop=(k == 1))
                mm.then_inc(qkv_mm, 1)
                pe.wait_ge(rope_step, 6 * i + 12)
                turn(4, rot, 4, rT_mm)

            pe.sem_inc(vx_ready, 1)
            pe.sem_inc(rope_step, 6)
            pe.sem_inc(r_lo, 1)
            out_proj(0, 0)
            out_proj(0, 1)
            with pe.Fori(0, NT - 1) as i:
                x_tile(i, True)
            x_tile(NT - 1, False)

            pe.sem_inc(xs_max, 2)
            pe.sem_inc(xp_ready, 2)
            pe.sem_inc(xo_copied, 2)
            pe.wait_ge(r_lo, NT + 1)

            def x_scores(qd, b):
                i = qd * 2 + b
                pe.wait_ge(xq_loaded[b], 128 * (qd + 1))
                for j in range(NQ):
                    for qt in range(QT):
                        n = j * QT + qt
                        bank = psum[:, 2 + n % 2, :]
                        pe.wait_ge(xs_max, 16 * i + n + 1)
                        pe.matmul(bank[:, 0:(qt + 1) * P], q_op[b][0:X_MAX, j, qt * P:(qt + 1) * P], kx_op[b][0:X_MAX, j, 0:(qt + 1) * P],
                                  start=True, stop=True)
                        pe.matmul(bank[:, qt * P:(qt + 1) * P], ident_bf[:], mask_qk[:], start=False, stop=True, skip_group_check=True).then_inc(xs_mm, 1)

            def x_turn_max(qd, b, first=False):
                i = qd * 2 + b
                pe.wait_ge(xs_max, 16 * i + 18)
                if not first:
                    pe.wait_ge(xm_lo, i)
                pe.transpose(psum[0:16, 1, 0:P], m_neg[:, b, :], ident[:]).then_inc(xmT_done, 1)

            def x_shifted(qd, b, kt):
                i = qd * 2 + b
                for j in range(NQ):
                    n = 4 * kt + j
                    bank = psum[:, 4 + n % 2, :]
                    pe.wait_ge(xp_ready, 16 * i + n + 1)
                    pe.matmul(bank[:, 0:S - kt * P], kx_op[b][:, j, kt * P:(kt + 1) * P], q_op[b][:, j, kt * P:], start=True, stop=True)
                    pe.matmul(bank[:, 0:P], ident_bf[:], mask_kq[:], start=False, stop=True, skip_group_check=True).then_inc(xst_mm, 1)

            def x_values(qd, b, kt):
                i = qd * 2 + b
                pe.wait_ge(xp_ready, 16 * i + 4 * kt + 6)
                for bank in (6, 7):
                    for j in range(NQ):
                        w = v_q[:, b, kt, j * 32:(j + 1) * 32] if bank == 6 else ones32[:]
                        mm = pe.matmul(psum[j * 32:(j + 1) * 32, bank, kt * P:], w, prob[:, kt % 2, j, 0:S - kt * P],
                                       start=(kt == 0), stop=(kt == QT - 1), skip_group_check=True)
                mm.then_inc(xpv_done, 1)

            def x_step(qd, b, q1, b1):
                i = qd * 2 + b
                if q1 is not None:
                    x_scores(q1, b1)
                pe.wait_ge(xm_loaded[b], 32 * (qd + 1))
                x_shifted(qd, b, 0)
                x_shifted(qd, b, 1)
                pe.wait_ge(xv_ready, i + 1)
                pe.wait_ge(xo_copied, 2 * i + 2)
                for kt in range(QT):
                    x_values(qd, b, kt)
                    if kt + 2 < QT:
                        x_shifted(qd, b, kt + 2)
                if q1 is not None:
                    x_turn_max(q1, b1)

            x_scores(0, 0)
            x_turn_max(0, 0, True)
            x_step(0, 0, 0, 1)
            x_step(0, 1, 1, 0)
            with pe.Fori(1, X_QUADS - 1) as qd:
                x_step(qd, 0, qd, 1)
                x_step(qd, 1, qd + 1, 0)
            x_step(X_QUADS - 1, 0, X_QUADS - 1, 1)
            x_step(X_QUADS - 1, 1, None, None)

            def products(k, i, lhs, w, chunks):
                for c in range(chunks):
                    pe.matmul(psum[:, 2 * k, 0:H + N_AB], lhs[:, c, :], w[:, c, 0:H + N_AB], start=(c == 0), stop=(c == chunks - 1))
                for c in range(chunks):
                    mm = pe.matmul(psum[0:DR, 2 * k + 1, 0:P], w[:, c, H + N_AB:], lhs[:, c, :], start=(c == 0), stop=(c == chunks - 1))
                mm.then_inc(W["w_mm"][k], 1)

            def deltas(k, i):
                pe.wait_ge(W["low_ready"][k], i + 1)
                pe.matmul(psum[:, 2 * k + 1, H:2 * H], low[k], du[k], start=True, stop=True).then_inc(W["du_mm"][k], 1)

            def dense_products(h, chunks):
                for c in chunks:
                    pe.matmul(psum[:, 4 + h, :], hT_f[:, c, :], kern[:, c, h * 512:(h + 1) * 512], start=(c == 0), stop=False)

            def round_(i, u, first, second, dense):
                if first or second:
                    pe.wait_ge(mlp_ready, i + 1)
                if first:
                    pe.wait_ge(yT_loaded, 16 * i + 16)
                    products(0, i, yT, write1, 2)
                if dense:
                    pe.wait_ge(xf_ready, i - 1)
                    turn(6, h_out, KC, fT_mm)
                if first:
                    deltas(0, i)
                if second:
                    pe.wait_ge(W["hn_ready"][1], 2 * i)
                    products(1, i - 1, mlpT, write2, KC)
                if dense:
                    pe.wait_ge(fT_ready, 2 * i - 2)
                    pe.wait_ge(lo_loaded, 32 * i - 32)
                    pe.wait_ge(o_step, i - 1)
                    for c in range(KC):
                        mm = pe.matmul(psum[:, 5, 0:R2], hT_f[:, c, :], lora_at[:, c, :], start=(c == 0), stop=(c == KC - 1))
                    mm.then_inc(ax_mm, 1)
                if second:
                    deltas(1, i - 1)
                if dense:
                    dense_products(0, range(KC))
                if first:
                    pe.wait_ge(W["hn_ready"][0], 2 * i + 2)
                    turn(6, h_mid[u], KC, h2T_mm)
                    pe.wait_ge(h2T_ready, 2 * i + 2)
                    for c in range(KC):
                        mm = pe.matmul(psum[:, 6, c * 2 * HC:(c + 1) * 2 * HC], hT[:, c, :], read2[:, c, :], start=True, stop=True)
                    mm.then_inc(y2_mm, 1)
                if dense:
                    wait_apart(pe, (ax_ready, i - 1))
                    pe.transpose(psum[0:R2, 7, 0:P], ax, ident[:]).then_inc(axT_mm, 1)
                    dense_products(1, range(KC // 2))
                    pe.wait_ge(axT_ready, i - 1)
                if first:
                    pe.wait_ge(y2n_ready, 2 * i + 2)
                    turn(7, yn, 4, y2T_mm)
                    pe.wait_ge(y2T_ready, 4 * i + 4)
                    for n, bank in ((0, 0), (1, 6)):
                        for f in range(KC):
                            for k in range(2):
                                mm = pe.matmul(psum[:, bank + f // 4, (f % 4) * P:(f % 4 + 1) * P], ctx_w[:, n, k, f * P:(f + 1) * P], ynT[:, 2 * n + k, :],
                                               start=(k == 0), stop=(k == 1))
                    mm.then_inc(gu_mm, 1)
                if dense:
                    dense_products(1, range(KC // 2, KC))
                    for h in range(2):
                        mm = pe.matmul(psum[:, 4 + h, :], axT, lora_bt[0:R2, h * 512:(h + 1) * 512], start=False, stop=True)
                    mm.then_inc(f_mm, 1)

            pe.wait_ge(xo_copied, 2 * XI + 2)
            pe.wait_ge(w2_loaded, 16 * 5)
            pe.wait_ge(kern_loaded, 48)
            pe.sem_inc(mlp_ready, 1)
            pe.sem_inc(W["hn_ready"][1], 2)
            pe.sem_inc(o_step, 1)
            run_rounds(pe, round_)


def kernel(**inputs):
    import concourse.bacc as bacc
    from concourse.bass_utils import run_bass_kernel_spmd

    nc = bacc.Bacc("TRN2", target_bir_lowering=False, num_devices=1)
    arrays = {"in_" + n: v for n, v in lay_out(inputs).items()}
    dram = {n[3:]: nc.dram_tensor(n, a.shape, mybir.dt.from_np(a.dtype), kind="ExternalInput").ap() for n, a in arrays.items()}
    out = nc.dram_tensor("out", (T, D), F32, kind="ExternalOutput").ap()
    build_program(nc, dram, out)
    r = run_bass_kernel_spmd(nc, [arrays], core_ids=[0])
    return r.results[0]["out"].reshape(B, S, D)


def lay_out(inputs):
    a = {n: np.asarray(v) for n, v in inputs.items()}
    x = "L0_xattn_"
    cat = np.concatenate
    columns = lambda v: v.reshape(-1, P).T
    lay = {}
    lay["x"] = a["x"].reshape(T, D)
    lay["pos"] = a["pos_BxS"].astype(np.int32).reshape(NT, P).T
    lay["wT"] = cat([a[f"L0_attn_{n}_weight"].T for n in "qkvo"], axis=1)
    lay["cols"] = cat([columns(a["L0_attn_q_scale"]), columns(a["L0_attn_k_scale"]),
                       columns(a[x + "attn_read_g"]), columns(a[x + "attn_read_b"]),
                       columns(a[x + "mlp_read_g"]), columns(a[x + "mlp_read_b"])], axis=1)
    lay["rows"] = np.broadcast_to(cat([a[x + "attn_wab_b"], a[x + "mlp_wab_b"],
                                       a[x + "attn_du_b"], a[x + "mlp_du_b"], a["L0_ffn_bias"]])[None], (P, N_ROWS))
    lay["scale_rows"] = np.broadcast_to(cat([a["L0_attn_v_scale"], a["L0_attn_o_scale"]])[None], (P, N_SCALES))
    for name, w in (("read1", a[x + "attn_read_w"]), ("read2", a[x + "mlp_read_w"])):
        n_out = w.shape[1]
        block = np.zeros((KC, HC, C, n_out, HC), np.float32)
        for h in range(HC):
            block[:, h, :, :, h] = w.reshape(KC, HC, n_out, C)[:, h].transpose(0, 2, 1)
        lay[name] = block.reshape(KC, P, n_out * HC).transpose(1, 0, 2)
    lay["wqkv"] = a[x + "qkv_w"].transpose(0, 2, 1).reshape(3, 2, P, H).transpose(2, 0, 1, 3)
    for n, name in ((1, "attn"), (2, "mlp")):
        wod, wab = a[x + name + "_wod_w"], a[x + name + "_wab_w"]
        wT = cat([wod[:H], wab, wod[H:]]).T
        lay[f"write{n}"] = wT.reshape(-1, P, N_W).transpose(1, 0, 2)
        lay[f"du{n}"] = a[x + name + "_du_w"].T
    lay["ctx"] = a["ctx_1024"].transpose(0, 2, 1).reshape(2, 2, P, M).transpose(2, 0, 1, 3)
    lay["kern"] = a["L0_ffn_kernel"].reshape(KC, P, D).transpose(1, 0, 2)
    lay["lora_a"] = a["L0_ffn_lora_A"].reshape(N_LORA, R4, R8, D).transpose(1, 0, 2, 3).reshape(R4, P, D)
    lay["lora_as"] = a["L0_ffn_lora_A_shared"].T.reshape(KC, P, RANK).transpose(1, 0, 2)
    lay["lora_b"] = a["L0_ffn_lora_B"].transpose(0, 2, 1).reshape(R4, P, D)
    lay["lora_bs"] = a["L0_ffn_lora_B_shared"].T
    gate = a["L0_ffn_gate"]
    gate_a = np.zeros((N_LORA, R8, NT, R8), np.float32)
    for r in range(R8):
        gate_a[:, r, :, r] = gate.T
    lay["gate_a"] = gate_a.reshape(P, NT * R8)
    gate_b = np.zeros((N_LORA, RANK, NT, RANK), np.float32)
    for r in range(RANK):
        gate_b[:, r, :, r] = gate.T
    lay["gate_b"] = gate_b.reshape(R4, P, NT * RANK).transpose(1, 0, 2)
    return {n: np.ascontiguousarray(v) for n, v in lay.items()}
```

```python
from contextlib import ExitStack

import numpy as np

import concourse.bass as bass
from concourse import mybir

F32 = mybir.dt.float32
F32R = mybir.dt.float32r
F16 = mybir.dt.float16
BF16 = mybir.dt.bfloat16
I32 = mybir.dt.int32
ALU = mybir.AluOpType
ACT = mybir.ActivationFunctionType
AX_X = mybir.AxisListType.X
ds = bass.ds

P = 128
B, S, D = 2, 512, 1024
T = B * S
NT = T // P
KC = D // P
QT = S // P
LN_EPS = 1e-5

A_HD, A_KV = 32, 8
A_REP = D // A_HD // A_KV
KVD = A_KV * A_HD
QKV = D + 2 * KVD
A_SCALE = float(1.0 / np.sqrt(A_HD))
A_MAX = 3 * A_HD
A_ROWS = A_MAX + 2
NI = A_KV * B
Q_BANKS = (0, 4, 5, 7)
Q_EARLY = NI // 2
OP_HT, OP_YN = 8, 15
LEAD = 10
A_ROUNDS = (NI - 4) // 3
V_GAIN = 4.0

H, C, RH = 256, 4, 16
HS, DR, M = H // RH, 8, 1024
X_NH = 16
X_HD = H // X_NH
HALF = X_HD // 2
HC = P // C
NQ = 4
X_QUADS = X_NH // NQ
XI = X_QUADS * B
X_MAX = 4 * X_HD
X_SCALE = float(1.0 / np.sqrt(X_HD))
N_A = (C - 1) * RH
N_AB = 2 * N_A + RH
N_Z = H + N_A
N_W = H + N_AB + DR
SSM_EPS = 1e-5

N_LORA, RANK = 16, 32
R8 = P // N_LORA
R4 = RANK // R8
R2 = 2 * RANK

MAGIC = 1.5 * 2.0 ** 23
TWO_PI = 2 * np.pi
TP1 = 6.28125
TP2 = float(np.float32(np.float16(TWO_PI - TP1)))
TP3 = float(TWO_PI - TP1 - TP2)
ROPE_INV = (np.float32(1) / np.power(np.float32(10000), np.arange(HALF, dtype=np.float32) / np.float32(HALF))).astype(np.float32)

COLS = {}
_at = 0
for _n, _w in (("q_scale", KC), ("k_scale", KVD // P), ("g1", 6), ("b1", 6), ("g2", 4), ("b2", 4)):
    COLS[_n] = (_at, _at + _w)
    _at += _w
N_COLS = _at
ROWS = {}
_at = 0
for _n, _w in (("wab1", N_AB), ("wab2", N_AB), ("du1", H), ("du2", H), ("bias", D)):
    ROWS[_n] = (_at, _at + _w)
    _at += _w
N_ROWS = _at
N_SCALES = KVD + D


def build_program(nc, d, out):
    ctx = ExitStack()
    with ctx:
        def sb(name, shape, dt=F32):
            return ctx.enter_context(nc.sbuf_tensor(name, shape, dt))

        def sem(name):
            return ctx.enter_context(nc.semaphore(name))

        def scratch(name, shape):
            return nc.dram_tensor(name, shape, F32).ap()

        psum = ctx.enter_context(nc.psum_tensor("psum", [P, 8, 512], F32))

        cols = sb("cols", [P, N_COLS])
        rows = sb("rows", [P, N_ROWS])
        ident = sb("ident", [P, P])
        ident_bf = sb("ident_bf", [P, P], BF16)
        mask_qk = sb("mask_qk", [P, P], BF16)
        mask_kq = sb("mask_kq", [P, P], BF16)
        ones32 = sb("ones32", [P, A_HD])
        minus_half = sb("minus_half", [P, 4])
        c_q = sb("c_q", [P, KC])
        c_k = sb("c_k", [P, KVD // P])
        c_o = sb("c_o", [P, D])
        pos_i = sb("pos_i", [P, NT], I32)
        pos_f = sb("pos_f", [P, NT])
        trig = sb("trig", [P, 3, NT, HALF])

        region_x = sb("region_x", [P, KC * T])
        region_a = sb("region_a", [P, KC * T])
        region_w = sb("region_w", [P, QKV + D + QKV + D + KC * QKV // 2])
        region_p = sb("region_p", [P, 2 * 4 * 512])
        xnT_hi = region_x[:, 0:KC * T // 2].bitcast(F16).rearrange("p (c t) -> p c t", c=KC)
        xnT_lo = region_x[:, KC * T // 2:].bitcast(F16).rearrange("p (c t) -> p c t", c=KC)
        x1 = region_x[:, :].rearrange("p (t n) -> p t n", t=NT)
        attT_hi, attT_lo = (region_a[:, n * KC * T // 2:(n + 1) * KC * T // 2].bitcast(F16).rearrange("p (i s) -> p i s", s=S) for n in range(2))
        o_in_hi, o_in_lo = (x.rearrange("p (c b) s -> p c (b s)", b=B) for x in (attT_hi, attT_lo))
        kern = region_a[:, :].rearrange("p (c n) -> p c n", c=KC)
        w_in = [region_w[:, 0:QKV + D], region_a[:, 0:QKV + D]]
        _o = QKV + D
        w_abs = region_w[:, _o:_o + QKV + D]
        _o += QKV + D
        sign_qkv = region_w[:, _o:].bitcast(F16).rearrange("p (c n) -> p c n", c=KC)
        prob_a = region_x[:, :].rearrange("p (b j n) -> p b j n", b=4, j=4)
        x_in = region_p[:, 0:2 * D].rearrange("p (u n) -> p u n", u=2)
        _o = 2 * D
        scale_rows = region_p[:, _o:_o + N_SCALES]
        _o += N_SCALES
        mean_w = region_p[:, _o:_o + P]
        _o += P
        c_v = region_p[:, _o:_o + KVD]
        _o += KVD
        ang = region_p[:, _o:_o + NT * HALF].rearrange("p (t f) -> p t f", f=HALF)
        _o += NT * HALF
        trig_n, trig_r = (region_p[:, _o + n * 2 * NT * HALF:_o + (n + 1) * 2 * NT * HALF].rearrange("p (k t f) -> p k t f", k=2, f=HALF)
                          for n in range(2))

        q_op = [sb(f"q_op{u}", [P, A_REP, S], F32R) for u in range(2)]
        kr = sb("kr", [P, 2 * NQ * S], F32R)
        k_op = [kr[:, u * S:(u + 1) * S] for u in range(3)]
        qa_op = [q_op[0], q_op[1], kr[:, 4 * S:].rearrange("p (j n) -> p j n", j=A_REP)]
        hi_st = sb("hi_st", [P, S], F32R)
        lo_st = sb("lo_st", [P, S], F32R)
        stage = [(hi_st[:], lo_st[:])] + [(kr[:, (2 + 2 * n) * S:(3 + 2 * n) * S], kr[:, (3 + 2 * n) * S:(4 + 2 * n) * S]) for n in range(3)]
        m_hi = sb("m_hi", [16, P], F32R)
        m_lo = sb("m_lo", [16, P], F32R)

        st = sb("st", [P, 2, 2, 6])
        mv = sb("mv", [P, 2, 2])
        ve = sb("ve", [P, 2, 1])
        rstd = sb("rstd", [P, 2, 1])

        v_all = sb("v_all", [P, NT, KVD])
        v_heads = v_all[:].rearrange("p a b -> p (a b)").rearrange("p (g t e) -> p g t e", g=A_KV, e=A_HD)
        v_steps = v_all[:].rearrange("p a b -> p (a b)").rearrange("p (i n) -> p i n", n=QT * A_HD)
        v_g = sb("v_g", [P, 3, QT, A_HD])
        m_neg = sb("m_neg", [P, 3, 16])
        o_sb, den_sb, att = (region_w[:, n * S:(n + 1) * S] for n in range(3))

        v_x = region_w[:, 3 * S:3 * S + NT * 2 * H].rearrange("p (t n) -> p t n", t=NT)
        _o = 3 * S + NT * 2 * H
        ctx_parts = region_w[:, _o:_o + 4 * M].rearrange("p (w n) -> p w n", w=4)
        ctx_w = region_w[:, _o:_o + 4 * M].rearrange("p (w k n) -> p w k n", w=2, k=2)
        _o += 4 * M
        wqkv = region_w[:, _o:_o + 6 * H].rearrange("p (s n) -> p s n", s=6)
        lora_bt = region_w[:, _o:_o + D]
        lora_at = region_w[:, _o + D:_o + D + KC * R2].rearrange("p (c r) -> p c r", c=KC)
        y0 = region_p[:, 2 * D:3 * D]
        h_st = region_p[:, 3 * D:4 * D]
        yn = sb("yn", [P, 3 * H])
        hT = v_all[:].rearrange("p t n -> p (t n)")[:, 0:D].rearrange("p (c n) -> p c n", c=KC)
        v_q = [x.rearrange("p (k n) -> p k n", k=QT) for x in (v_all[:].rearrange("p t n -> p (t n)")[:, 0:QT * P],
                                                               v_all[:].rearrange("p t n -> p (t n)")[:, QT * P:2 * QT * P], yn[:, 0:QT * P])]
        pair_sum = region_p[:, :].rearrange("p (b j n) -> p b j n", b=2, j=A_REP)
        prob_x = [region_p[:, 0:NQ * S], region_p[:, NQ * S:NQ * (2 * S - P)], v_all[:].rearrange("p t n -> p (t n)")[:, D:D + NQ * 2 * P],
                  region_p[:, NQ * (2 * S - P):]]
        prob_x = [prob_x[k].rearrange("p (j n) -> p j n", j=NQ) for k in range(QT)]
        v_rest = v_all[:].rearrange("p t n -> p (t n)")[:, D:2 * D]
        read1 = v_rest[:, 0:KC * 3 * HC].rearrange("p (c n) -> p c n", c=KC)
        read2 = v_rest[:, 0:KC * 2 * HC].rearrange("p (c n) -> p c n", c=KC)
        du = [v_rest[0:DR, KC * 2 * HC + n * H:KC * 2 * HC + (n + 1) * H] for n in range(2)]
        ynT = sb("ynT", [P, 6, P])
        den_inv, den_sel, spread_32 = ynT[:, 0, :], ynT[:, 1, :].rearrange("p (k e) -> p k e", k=QT), ynT[:, 2:, :]
        den_hi, den_parts, spread = hi_st[:, 0:P], hi_st[:, P:2 * P], lo_st[:].rearrange("p (k n) -> p k n", k=QT)
        rot = yn[:, 0:2 * H]
        rope_a = yn[:, 2 * H:3 * H]
        mvs = sb("mvs", [P, 2 * NT])
        den_mask = mvs[:, 0:1]
        ves = sb("ves", [P, 1])
        rstds = sb("rstds", [P, NT])
        st3 = sb("st3", [P, 3, 2, 6])
        mv3 = sb("mv3", [P, 3, 2])
        ve3 = sb("ve3", [P, 3])
        rs3 = sb("rs3", [P, 3])
        _w = [region_p[:, n * D:(n + 1) * D] for n in range(4)] + [region_w[:, 3 * S + n * D:3 * S + (n + 1) * D] for n in range(4)]
        h_in, h_mid_0, h_mid_1, h_out, mlpT_f, out_t, abar, bbar = _w
        h_mid = [h_mid_0, h_mid_1]
        hT_f = c_o[:].rearrange("p (c n) -> p c n", c=KC)
        mlpT = mlpT_f.rearrange("p (f n) -> p f n", f=KC)
        h_a = region_w[:, 0:3 * H]
        z_b, e_b = region_w[:, 3 * H:3 * H + N_Z], region_w[:, 3 * H + N_Z:3 * H + 2 * N_Z]
        b_skip = abar[:, 3 * H:4 * H]
        sp_b = sb("sp_b", [P, N_Z])
        ab_b, r_b, rc_b = bbar[:, 3 * H:3 * H + 64], bbar[:, 3 * H + 64:3 * H + 64 + N_A], bbar[:, 3 * H + 128:3 * H + 128 + N_A]
        yT = v_g[:].rearrange("p b t e -> p (b t e)")[:, 0:2 * P].rearrange("p (k n) -> p k n", k=2)
        with nc.sbuf_tensor("sign_o_all", [P, KC, D], F16) as sign_o:
            pass
        with nc.sbuf_tensor("third_op", [P, 2 * NQ * S], F32R) as third_op:
            pass
        region_s = sb("region_s", [P, KC * D // 2])
        by_head = [x.rearrange("p (j n) -> p j n", j=NQ) for x in (kr[:, 0:NQ * S], kr[:, NQ * S:], third_op[:, 0:NQ * S], third_op[:, NQ * S:])]
        kx_op, qx_op = by_head[0:3], [q_op[0], q_op[1], by_head[3]]
        write1 = region_s[:, 0:2 * N_W].rearrange("p (k n) -> p k n", k=2)
        write2 = region_s[:, 2 * N_W:10 * N_W].rearrange("p (k n) -> p k n", k=KC)
        low = [region_s[0:DR, 10 * N_W + n * P:10 * N_W + (n + 1) * P] for n in range(2)]
        ax = bbar[:, 3 * H + 192:3 * H + 192 + R2]
        axT = region_w[0:R2, 3 * H + 2 * N_Z:3 * H + 2 * N_Z + P]
        lora_in = region_a[:, :].rearrange("p (s n) -> p s n", s=2 * R4)
        gate_b = region_w[:, 0:R4 * NT * RANK].rearrange("p (k n) -> p k n", k=R4)
        gate_a = region_w[:, R4 * NT * RANK:R4 * NT * RANK + NT * R8]
        a_eff = region_p[:, 0:KC * NT * RANK].rearrange("p (b c r) -> p b c r", b=NT, c=KC)
        b_eff = region_p[:, 2 * D:4 * D].rearrange("p (m n) -> p m n", m=2)

        def wait_apart(eng, *waits):
            waits = [(semaphore, eng.to_reg(value)) for semaphore, value in waits]
            eng.wait_ge(s_const, 64)
            for semaphore, value in waits:
                eng.wait_ge(semaphore, value)

        def early_scores(i, half):
            n = 4 * (i - Q_EARLY) + 2 * half
            return range(n, min(n + 2, 16 + LEAD))

        def run_steps(eng, step):
            step(0, 0, first=True)
            with eng.Fori(0, (XI - 2) // 3) as t:
                for k in (1, 2, 3):
                    step(t, k)
            step(0, XI - 1, last=True)

        def run_rounds(eng, round_):
            round_(0, 0, True, False, False, False)
            round_(1, 1, True, True, False, False)
            round_(2, 0, True, True, True, False)
            with eng.Fori(0, (NT - 4) // 2) as it:
                for u in (1, 0):
                    round_(it * 2 + 4 - u, u, True, True, True, True)
            round_(NT - 1, 1, True, True, True, True)
            round_(NT, 0, False, True, True, True)
            round_(NT + 1, 1, False, False, True, True)

        a_scr = scratch("a_scr", [NT, P, KC * RANK])
        b_scr = scratch("b_scr", [NT * RANK, D])
        k_scr = scratch("k_scr", [2, A_KV, B, A_HD, S])
        q_scr = scratch("q_scr", [2, A_KV, B, A_REP * A_HD, S])
        qk_scr = scratch("qk_scr", [2, 2, H, T])
        y_scr = scratch("y_scr", [H, T])

        s_const = sem("const_loaded")
        block = ctx.enter_context(nc.Block())

        x_slot = [sem(f"x_slot{u}_loaded") for u in range(2)]
        w_loaded = [sem(f"w_loaded{u}") for u in range(2)]
        signs_done, abs_taken, qkv_summed, o_summed = sem("signs_done"), sem("abs_taken"), sem("qkv_summed"), sem("o_summed")
        made = sem("constants_made")
        ln_step, ln_rstd = sem("ln_step"), sem("ln_rstd")
        xn_ready = sem("xn_ready")
        xT_done, xT_hi, xT_free = sem("xT_done"), sem("xT_hi"), sem("xT_free")
        means_done, c_ready = sem("weight_means_done"), sem("scales_ready")
        qk_mm, qk_hi, qk_lo = sem("qk_mm"), sem("qk_hi"), sem("qk_lo")
        staged_out = [sem(f"staged_out{u}") for u in range(4)]
        v_mm, v_ready = sem("v_mm"), sem("v_ready")
        ang_step, trig_done = sem("ang_step"), sem("trig_done")
        qk_loaded = [sem(f"qk_loaded{u}") for u in range(3)]
        m_loaded = [sem(f"m_loaded{u}") for u in range(3)]
        s_mm, s_max = sem("s_mm"), sem("s_max")
        mT_done, m_hi_ready, m_lo_ready = sem("mT_done"), sem("m_hi_ready"), sem("m_lo_ready")
        st_mm, p_ready, pv_done = sem("st_mm"), sem("p_ready"), sem("pv_done")
        vg_ready = sem("vg_ready")
        pair_ready, den_done, den_spread = sem("pair_ready"), sem("den_done"), sem("den_spread")
        o_copied, den_rec, att_ready, att_hi_ready, att_lo_ready = sem("o_copied"), sem("den_rec"), sem("att_ready"), sem("att_hi_ready"), sem("att_lo_ready")
        lora_loaded, lora_mm, lora_ready, lora_stored = sem("lora_loaded"), sem("lora_mm"), sem("lora_ready"), sem("lora_stored")
        xw_loaded = sem("xw_loaded")
        op_mm, y0_ready, x1_ready = sem("op_mm"), sem("y0_ready"), sem("x1_ready")
        l_step, l_rstd, h_ready = sem("l_step"), sem("l_rstd"), sem("h_ready")
        hT_mm, hT_ready, y_mm = sem("hT_mm"), sem("hT_ready"), sem("y_mm")
        y_step, y_rstd, yn_ready = sem("y_step"), sem("y_rstd"), sem("yn_ready")
        ynT_mm, ynT_ready, qkv_mm = sem("ynT_mm"), sem("ynT_ready"), sem("qkv_mm")
        rope_step, vx_ready, rT_mm, r_hi, r_lo, qk_stored = (sem(n) for n in (
            "rope_step", "vx_ready", "rT_mm", "r_hi", "r_lo", "qk_stored"))
        xq_loaded = [sem(f"xq_loaded{u}") for u in range(3)]
        xm_loaded = [sem(f"xm_loaded{u}") for u in range(3)]
        xs_mm, xs_max, xmT_done, xm_hi, xm_lo = sem("xs_mm"), sem("xs_max"), sem("xmT_done"), sem("xm_hi"), sem("xm_lo")
        xst_mm, xp_ready, xpv_done, xv_ready = sem("xst_mm"), sem("xp_ready"), sem("xpv_done"), sem("xv_ready")
        xo_copied, xden_rec, xatt_ready, y_stored = sem("xo_copied"), sem("xden_rec"), sem("xatt_ready"), sem("y_stored")
        w2_loaded, kern_loaded, yT_loaded, lo_loaded = sem("w2_loaded"), sem("kern_loaded"), sem("yT_loaded"), sem("lo_loaded")
        h2_ready = sem("h2_ready")
        W = {n: [sem(f"{n}_{k}") for k in (1, 2)] for n in (
            "w_mm", "low_ready", "du_mm", "z_ready", "az_ready", "e_ready", "l_ready", "sp_ready", "r_step",
            "da_ready", "abar_ready", "ha_ready", "b_step", "hn_ready")}
        h2T_mm, h2T_ready, y2_mm = sem("h2T_mm"), sem("h2T_ready"), sem("y2_mm")
        y2_step, y2_rstd, y2n_ready = sem("y2_step"), sem("y2_rstd"), sem("y2n_ready")
        y2T_mm, y2T_ready, gu_mm, tanh_ready, g_ready, mlp_ready = (sem(n) for n in (
            "y2T_mm", "y2T_ready", "gu_mm", "tanh_ready", "g_ready", "mlp_ready"))
        x2_ready, f_step, f_rstd, xf_ready = (sem(n) for n in ("x2_ready", "f_step", "f_rstd", "xf_ready"))
        fT_mm, fT_ready, ax_mm, ax_ready, axT_mm, axT_ready, f_mm, o_step, out_ready, out_stored = (sem(n) for n in (
            "fT_mm", "fT_ready", "ax_mm", "ax_ready", "axT_mm", "axT_ready", "f_mm", "o_step", "out_ready", "out_stored"))

        @block.sync
        def _(sp):
            sp.dma_start(cols[:], d["cols"]).then_inc(s_const, 16)
            sp.dma_start(rows[:], d["rows"]).then_inc(s_const, 16)
            sp.dma_start(scale_rows, d["scale_rows"]).then_inc(s_const, 16)
            sp.dma_start(pos_i[:], d["pos"]).then_inc(s_const, 16)
            sp.sem_inc(xT_done, 2)
            with sp.Fori(0, NT // 2) as it:
                for u in range(2):
                    i = it * 2 + u
                    sp.wait_ge(xT_done, i + 1)
                    sp.dma_start(x_in[:, u, :], d["x"][ds(i * P, P), :]).then_inc(x_slot[u], 16)
                    sp.wait_ge(qkv_summed, i + 1)
                    sp.wait_ge(o_summed, i + 1)
                    sp.dma_start(w_in[u], d["wT"][ds(i * P, P), :]).then_inc(w_loaded[u], 16)
            sp.wait_ge(qkv_summed, NT + 2)
            sp.wait_ge(o_summed, NT + 2)
            sp.wait_ge(xT_done, NT + 2)
            for r in range(R4):
                sp.dma_start(lora_in[:, r, :], d["lora_a"][r]).then_inc(lora_loaded, 16)
                sp.dma_start(lora_in[:, R4 + r, :], d["lora_b"][r]).then_inc(lora_loaded, 16)
            sp.dma_start(gate_a, d["gate_a"]).then_inc(lora_loaded, 16)
            sp.dma_start(gate_b, d["gate_b"]).then_inc(lora_loaded, 16)
            for n in range(4):
                b, m = n // 2, n % 2
                sp.wait_ge(qk_hi, n + 1)
                sp.wait_ge(qk_lo, n + 1)
                for part in range(2):
                    for h in range(4):
                        sp.dma_start(k_scr[part, 4 * m + h, b], stage[n][part][h * A_HD:(h + 1) * A_HD, :].bitcast(F32)).then_inc(staged_out[n], 16)
            sp.wait_ge(lora_ready, R4 + 4)
            for b in range(NT):
                sp.dma_start(a_scr[b], a_eff[:, b].rearrange("p c r -> p (c r)")).then_inc(lora_stored, 16)
            for m in range(2):
                sp.dma_start(b_scr[m * P:(m + 1) * P, :], b_eff[:, m, :]).then_inc(lora_stored, 16)
            q_rows = q_scr.rearrange("a g b n s -> a (g b) n s")

            def store_q(i, u):
                sp.wait_ge(qk_hi, i + 5)
                sp.wait_ge(qk_lo, i + 5)
                for part in range(2):
                    sp.dma_start(q_rows[part, ds(i, 1)].rearrange("o n s -> (o n) s"), stage[u][part].bitcast(F32)).then_inc(staged_out[u], 16)

            k_rows = k_scr.rearrange("a g b n s -> a (g b) n s")

            def load_qk(t, k):
                i, u = t * 3 + k, k % 3
                sp.wait_ge(st_mm, 16 * i + 16)
                for part in range(3):
                    sp.dma_start(k_op[u][part * A_HD:(part + 1) * A_HD, :].bitcast(F32),
                                 k_rows[part % 2, ds(i, 1)].rearrange("o n s -> (o n) s")).then_inc(qk_loaded[u], 16)
                    sp.dma_start(qa_op[u][part * A_HD:(part + 1) * A_HD].bitcast(F32),
                                 q_rows[part // 2, ds(i, 1)].rearrange("o (j e) s -> (o e) j s", j=A_REP)).then_inc(qk_loaded[u], 16)

            def load_max(t, k):
                i, u = t * 3 + k, k % 3
                sp.wait_ge(m_hi_ready, i + 1)
                sp.wait_ge(m_lo_ready, i + 1)
                for r, src in ((A_MAX, m_hi), (A_MAX + 1, m_lo)):
                    sp.dma_start(qa_op[u][r:r + 1].rearrange("o j n -> o (j n)").bitcast(F32), src[:].bitcast(F32)).then_inc(m_loaded[u], 16)

            sp.sem_inc(st_mm, 48)
            for i in range(4):
                store_q(i, i)
            sp.wait_ge(made, 15)
            for u in range(4):
                sp.wait_ge(staged_out[u], 16 * 8 + (32 if u < 2 else 0))
            for k in range(2):
                load_qk(0, k)
            with sp.Fori(1, Q_EARLY // 4) as it:
                for u in range(4):
                    store_q(it * 4 + u, u)
            for i in range(Q_EARLY, NI):
                store_q(i, i % 4)
                if i == Q_EARLY + 5:
                    load_max(0, 0)


            def load_x(i, u):
                sp.dma_start(x_in[:, u, :], d["x"][ds(i * P, P), :] if not isinstance(i, int) else d["x"][i * P:(i + 1) * P, :]).then_inc(x_slot[u], 16)

            for u in range(4):
                sp.wait_ge(staged_out[u], 16 * 8 + 32 * NI // 4)
            load_qk(0, 2)
            load_max(0, 1)
            load_qk(0, 3)
            load_max(0, 2)
            with sp.Fori(0, A_ROUNDS) as t:
                for k in (2, 3, 4):
                    load_qk(t, k + 2)
                    load_max(t, k + 1)
                    if k == 3:
                        sp.dma_start(ctx_parts[:, ds(t, 1), :], d["ctx"].rearrange("p w k n -> p (w k) n")[:, ds(t, 1), :]).then_inc(xw_loaded, 16)
            sp.dma_start(wqkv, d["wqkv"].rearrange("p o k n -> p (o k) n")).then_inc(xw_loaded, 16)
            load_max(0, NI - 1)
            sp.wait_ge(vg_ready, NI)
            sp.dma_start(read1, d["read1"]).then_inc(xw_loaded, 16)
            sp.wait_ge(den_done, 2 * NI + 2)
            load_x(0, 0)
            load_x(1, 1)
            load_max(0, NI - 1)


            def store_qk(i):
                sp.wait_ge(r_hi, i + 1)
                sp.wait_ge(r_lo, i + 2)
                for part in range(2):
                    sp.dma_start(qk_scr[part].rearrange("q (m p) t -> p (q m) t", p=P)[:, :, ds(i * P, P)],
                                 (hi_st, lo_st)[part][:].rearrange("p (s t) -> p s t", s=4).bitcast(F32)).then_inc(qk_stored, 16)

            with sp.Fori(0, NT // 2 - 1) as it:
                for u in range(2):
                    i = it * 2 + u
                    sp.wait_ge(x1_ready, i + 1)
                    load_x(i + 2, u)
                    store_qk(i)
            store_qk(NT - 2)
            store_qk(NT - 1)
            sp.wait_ge(qk_stored, 2 * 16 * NT + 32)
            sp.wait_ge(made, 31)
            sp.wait_ge(op_mm, 2 * NT)
            sp.sem_inc(xst_mm, 48)
            sp.sem_inc(W["w_mm"][0], 1)

            def load_quad(i):
                u, qd, b = i % 3, i // 2, i % 2
                sp.wait_ge(xst_mm, 16 * i + 16)
                for side, dst, parts in ((0, qx_op[u], (0, 0, 1, 1)), (1, kx_op[u], (0, 1, 0, 1))):
                    for r, part in enumerate(parts):
                        sp.dma_start(dst[r * X_HD:(r + 1) * X_HD].bitcast(F32),
                                     qk_scr[part, side, qd * NQ * X_HD:(qd + 1) * NQ * X_HD, b * S:(b + 1) * S].rearrange("(j d) n -> d j n", j=NQ)
                                     ).then_inc(xq_loaded[u], 16)

            def load_max(i):
                u = i % 3
                sp.wait_ge(xm_hi, i + 1)
                sp.wait_ge(xm_lo, i + 1)
                for r, src in ((X_MAX, m_hi), (X_MAX + 1, m_lo)):
                    sp.dma_start(qx_op[u][r:r + 1].rearrange("o j n -> o (j n)").bitcast(F32), src[:].bitcast(F32)).then_inc(xm_loaded[u], 16)

            def store_y(i):
                qd, b = i // 2, i % 2
                sp.wait_ge(xatt_ready, i + 2)
                for j in range(NQ):
                    h = (qd * NQ + j) * X_HD
                    sp.dma_start(y_scr[h:h + X_HD, b * S:(b + 1) * S], att[j * 32:j * 32 + X_HD, :]).then_inc(y_stored, 16)

            def load_late(n):
                sp.dma_start(kern[:, n, :], d["kern"][:, n, :]).then_inc(kern_loaded, 16)

            def load_y(i):
                sp.wait_ge(W["w_mm"][0], i + 1)
                sp.dma_start(yT, y_scr.rearrange("(k p) t -> p k t", p=P)[:, :, ds(i * P, P)]).then_inc(yT_loaded, 16)

            for i in range(3):
                load_quad(i)
            load_max(0)
            load_max(1)
            sp.wait_ge(qkv_mm, NT)
            sp.dma_start(lora_at[:, :, RANK:], d["lora_as"]).then_inc(kern_loaded, 16)
            sp.dma_start(lora_bt[RANK:R2, :], d["lora_bs"]).then_inc(kern_loaded, 16)
            for i in range(1, XI):
                if i + 2 < XI:
                    load_quad(i + 2)
                if i + 1 < XI:
                    load_max(i + 1)
                store_y(i - 1)
                load_late(i - 1)
            load_late(KC - 1)
            sp.wait_ge(xst_mm, 16 * (XI - 2) + 48)
            sp.dma_start(write1, d["write1"]).then_inc(w2_loaded, 16)
            sp.dma_start(write2, d["write2"]).then_inc(w2_loaded, 16)
            sp.wait_ge(y_stored, 16 * NQ * (XI - 1) + 16)
            load_y(0)
            sp.wait_ge(xpv_done, 8 * XI + 8)
            sp.dma_start(read2, d["read2"]).then_inc(w2_loaded, 16)
            for n in range(2):
                sp.dma_start(du[n], d[f"du{n + 1}"]).then_inc(w2_loaded, 16)
            store_y(XI - 1)
            sp.wait_ge(y_stored, 16 * NQ * XI + 16)
            sp.wait_ge(lora_stored, 16 * (NT + 2))
            def load_adapters(i):
                sp.wait_ge(f_mm, i + 1)
                sp.dma_start(lora_at[:, :, 0:RANK], a_scr[ds(i, 1)].rearrange("o p (c r) -> (o p) c r", c=KC)).then_inc(lo_loaded, 16)
                sp.dma_start(lora_bt[0:RANK, :], b_scr[ds(i * RANK, RANK), :]).then_inc(lo_loaded, 16)

            def store_out(i):
                sp.wait_ge(out_ready, i + 1)
                sp.dma_start(out[ds(i * P, P), :], out_t).then_inc(out_stored, 16)

            sp.sem_inc(f_mm, 1)
            load_y(1)
            for i in (1, 2):
                load_y(i + 1)
                load_adapters(i - 1)
            with sp.Fori(3, NT - 1) as i:
                load_y(i + 1)
                store_out(i - 3)
                load_adapters(i - 1)
            for i in (NT - 1, NT):
                store_out(i - 3)
                load_adapters(i - 1)
            for i in (NT - 2, NT - 1):
                store_out(i)
            sp.wait_ge(out_stored, 16 * NT + 16)

        @block.gpsimd
        def _(pool):
            pool.memset(w_abs[:, QKV:], 0.0).then_inc(o_summed, 2)
            pool.memset(ident[:], 0.0).then_inc(made, 1)
            pool.memset(ident_bf[:], 0.0).then_inc(made, 1)
            pool.memset(mask_qk[:], 0.0).then_inc(made, 1)
            pool.memset(mask_kq[:], 0.0).then_inc(made, 1)
            pool.memset(mean_w, 1.0 / D).then_inc(made, 1)
            pool.memset(ones32[:], 1.0).then_inc(made, 1)
            pool.memset(minus_half[:], -0.5).then_inc(made, 1)
            pool.wait_ge(made, 4)
            for t in (ident, ident_bf):
                pool.affine_select(out=t[:], in_=t[:], compare_op=ALU.not_equal, fill=1.0, base=0,
                                   pattern=[[-1, P]], channel_multiplier=1).then_inc(made, 1)
            pool.affine_select(out=mask_qk[:], in_=mask_qk[:], compare_op=ALU.is_ge, fill=-1e30, base=0,
                               pattern=[[-1, P]], channel_multiplier=1).then_inc(made, 1)
            pool.affine_select(out=mask_kq[:], in_=mask_kq[:], compare_op=ALU.is_ge, fill=-1e30, base=0,
                               pattern=[[1, P]], channel_multiplier=-1).then_inc(made, 1)
            for u in range(2):
                pool.memset(q_op[u][:].bitcast(F32), 0.0).then_inc(made, 1)
            pool.wait_ge(made, 13)
            for u in range(2):
                pool.memset(k_op[u][A_MAX:A_ROWS, :].bitcast(F32), 1.0).then_inc(made, 1)
            pool.wait_ge(made, 15)
            with pool.Fori(0, NT // 2) as it:
                for u in range(2):
                    i = it * 2 + u
                    pool.wait_ge(ln_step, 4 * i + 4)
                    pool.tensor_tensor(rstd[:, u, :], ve[:, u, :], minus_half[:, 0:1], ALU.pow).then_inc(ln_rstd, 1)
                    pool.wait_ge(abs_taken, i + 1)
                    pool.wait_ge(o_summed, i + 2)
                    pool.tensor_tensor(w_abs[:, QKV:], w_in[u][:, QKV:], w_abs[:, QKV:], ALU.add).then_inc(o_summed, 1)
            for u in range(4):
                pool.wait_ge(staged_out[u], 16 * 8 + 32 * NI // 4)
            pool.memset(k_op[2][A_MAX:A_ROWS, :].bitcast(F32), 1.0).then_inc(made, 1)
            pool.wait_ge(made, 16)

            def values(t, k):
                i = t * 3 + k
                if not (isinstance(i, int) and i < 3):
                    pool.wait_ge(pv_done, 4 * i - 4)
                pool.tensor_copy(v_g[:, k % 3].rearrange("p t e -> p (t e)").unsqueeze(1), v_steps[:, ds(i, 1), :]).then_inc(vg_ready, 1)

            def pair(t, k, n):
                i = t * 3 + k
                pool.wait_ge(p_ready, 16 * i + 8 * n + 11)
                pool.wait_ge(den_done, 2 * i + n + 1)
                pool.tensor_tensor(pair_sum[:, n], prob_a[:, 2 * n], prob_a[:, 2 * n + 1], ALU.add).then_inc(pair_ready, 1)

            def split(t, k):
                i = t * 3 + k
                pool.wait_ge(att_hi_ready, i + 1)
                pool.tensor_tensor(attT_lo[:, ds(i, 1), :], att.unsqueeze(1), attT_hi[:, ds(i, 1), :], ALU.subtract).then_inc(att_lo_ready, 1)

            def step(t, k, done=3, last=False):
                if not last:
                    values(t, k + 1)
                if done > 0:
                    pair(t, k - 1, 1)
                if done > 1:
                    split(t, k - 2)
                pair(t, k, 0)

            pool.wait_ge(qk_lo, NI + 4)
            pool.memset(v_x, 0.0).then_inc(made, 1)
            pool.memset(den_sel, 0.0).then_inc(made, 1)
            pool.wait_ge(made, 18)
            for n in range(QT):
                pool.memset(den_sel[:, n, n * A_HD // QT:(n + 1) * A_HD // QT], 1.0).then_inc(made, 1)
                pool.tensor_tensor(spread_32[:, n, :].rearrange("p (j e) -> p j e", j=A_REP),
                                   *(ident[:, n * A_HD // QT + m:P:A_HD].unsqueeze(2).broadcast_to([P, A_REP, A_HD]) for m in range(2)),
                                   ALU.add).then_inc(made, 1)
            pool.sem_inc(att_lo_ready, 1)
            pool.sem_inc(att_ready, 1)
            pool.sem_inc(den_done, 2)
            pool.wait_ge(lora_stored, 16 * (NT + 2))
            pool.wait_ge(v_ready, NT + 2)
            values(0, 0)
            step(0, 0, done=0)
            step(0, 1, done=1)
            with pool.Fori(0, A_ROUNDS) as t:
                for k in (2, 3, 4):
                    step(t, k)
            step(0, NI - 2)
            step(0, NI - 1, last=True)
            pair(0, NI - 1, 1)
            split(0, NI - 2)
            split(0, NI - 1)
            pool.wait_ge(att_lo_ready, NI + 1)
            pool.wait_ge(pv_done, 4 + QT * NI)
            with pool.Fori(0, NT) as i:
                pool.wait_ge(l_step, 5 * i + 5)
                pool.tensor_tensor(rstds[:, ds(i, 1)], ves[:], minus_half[:, 0:1], ALU.pow).then_inc(l_rstd, 1)
                pool.wait_ge(y_step, 10 * i + 10)
                pool.tensor_tensor(rs3[:], ve3[:], minus_half[:, 0:3], ALU.pow).then_inc(y_rstd, 1)
            pool.wait_ge(y_rstd, NT)
            pool.wait_ge(op_mm, 2 * NT)
            for x in (kr, third_op):
                pool.memset(x[X_MAX:P, :].bitcast(F32), 0.0).then_inc(made, 1)
            pool.wait_ge(made, 29)
            for x in (kr[:], third_op[:, 0:NQ * S]):
                pool.memset(x[X_MAX:X_MAX + 2, :].bitcast(F32), 1.0).then_inc(made, 1)

            def x_values(t, k):
                i = t * 3 + k
                if not (isinstance(i, int) and i < 3):
                    pool.wait_ge(xpv_done, 8 * i - 8)
                pool.tensor_copy(v_q[k % 3], v_x[:, ds(i % 2 * QT, QT), ds(i // 2 * NQ * 32, NQ * 32)]).then_inc(xv_ready, 1)

            def x_normalise(t, k):
                i = t * 3 + k
                pool.wait_ge(xo_copied, 2 * i + 4)
                pool.wait_ge(xden_rec, 4 * i + 4)
                pool.wait_ge(y_stored, 16 * NQ * i + 16)
                pool.tensor_tensor(att, o_sb, den_sb, ALU.mult).then_inc(xatt_ready, 1)

            def x_step(t, k, first=False, last=False):
                if not last:
                    x_values(t, k + 1)
                if not first:
                    x_normalise(t, k - 1)

            pool.wait_ge(made, 31)
            pool.wait_ge(vx_ready, NT + 1)
            pool.wait_ge(qkv_mm, NT)
            pool.wait_ge(rT_mm, NT + 1)
            pool.sem_inc(y_stored, 16)
            pool.sem_inc(xatt_ready, 1)
            x_values(0, 0)
            run_steps(pool, x_step)
            x_normalise(0, XI - 1)

            def write(k, i, h):
                h3 = h.rearrange("p (s r c) -> p s r c", s=HS, r=RH)
                a3 = abar[:, 0:3 * H].rearrange("p (s r c) -> p s r c", s=HS, r=RH)
                pool.wait_ge(W["sp_ready"][k], i + 1)
                pool.tensor_tensor(a3, sp_b[:, 0:H].rearrange("p (s r) -> p s r", s=HS).unsqueeze(3).broadcast_to([P, HS, RH, C - 1]),
                                   sp_b[:, H:].rearrange("p (r c) -> p r c", r=RH).unsqueeze(1).broadcast_to([P, HS, RH, C - 1]),
                                   ALU.mult).then_inc(W["da_ready"][k], 1)
                pool.wait_ge(W["abar_ready"][k], i + 1)
                pool.tensor_tensor(h_a.rearrange("p (s r c) -> p s r c", s=HS, r=RH), h3[:, :, :, 0:C - 1], a3,
                                   ALU.mult).then_inc(W["ha_ready"][k], 1)

            def round_(i, u, first, second, dense, done):
                if first:
                    write(0, i, h_in)
                    pool.wait_ge(y2_step, 5 * i + 5)
                    pool.tensor_tensor(rs3[:, 0:2], ve3[:, 0:2], minus_half[:, 0:2], ALU.pow).then_inc(y2_rstd, 1)
                if second:
                    write(1, i - 1, h_mid[1 - u])
                    pool.wait_ge(f_step, 4 * i)
                    pool.tensor_tensor(rstd[:, 0, :], ves[:], minus_half[:, 0:1], ALU.pow).then_inc(f_rstd, 1)

            run_rounds(pool, round_)

        @block.scalar
        def _(act):
            with act.Fori(0, NT // 2) as it:
                for u in range(2):
                    i = it * 2 + u
                    act.wait_ge(w_loaded[u], 16 * (it + 1))
                    act.activation(sign_qkv[:, ds(i, 1), :], w_in[u][:, 0:QKV].unsqueeze(1), ACT.Sign).then_inc(signs_done, 1)
                    act.activation(sign_o[:, ds(i, 1), :], w_in[u][:, QKV:].unsqueeze(1), ACT.Sign).then_inc(signs_done, 1)
                    act.wait_ge(signs_done, 2 * i + 2)
                    act.activation(w_in[u], w_in[u], ACT.Abs).then_inc(abs_taken, 1)
                    act.wait_ge(xT_done, i + 3)
                    for h in range(2):
                        act.activation(xnT_hi[:, 4 * h:4 * h + 4, ds(i * P, P)],
                                       psum[:, 2 * u + h, :].rearrange("p (c n) -> p c n", c=4), ACT.Copy).then_inc(xT_hi, 1)
            act.wait_ge(c_ready, 5)
            for n in range(4):
                act.wait_ge(qk_mm, n + 1)
                act.activation(stage[n][0], psum[:, n, :], ACT.Identity, scale=c_k[:, n % 2:n % 2 + 1]).then_inc(qk_hi, 1)
            act.wait_ge(trig_done, 1)
            for k in range(2):
                act.activation(trig[:, k], trig_r[:, k], ACT.Sin).then_inc(trig_done, 1)
            act.wait_ge(trig_done, 2)
            act.activation(trig[:, 2], trig[:, 0], ACT.Copy, scale=-1.0).then_inc(trig_done, 1)
            for r in range(R4):
                act.wait_ge(lora_mm, r + 1)
                act.activation(a_eff[:, :, :, r * R8:(r + 1) * R8],
                               psum[:, r, :].rearrange("p (c b r) -> p b c r", c=KC, b=NT), ACT.Copy).then_inc(lora_ready, 1)
            with act.Fori(0, Q_EARLY // 4) as it:
                for u in range(4):
                    i = it * 4 + u
                    wait_apart(act, (qk_mm, i + 5), (staged_out[u], 32 * it + 128))
                    act.activation(stage[u][0], psum[:, Q_BANKS[u], :], ACT.Identity, scale=c_q[:, ds(it * 2 + u // 2, 1)]).then_inc(qk_hi, 1)

            def max_hi(t, k):
                i = t * 3 + k
                act.wait_ge(mT_done, i + 1)
                if k:
                    act.wait_ge(m_loaded[(k - 1) % 3], 32 * (t + (k - 1) // 3 + 1))
                act.activation(m_hi[:], psum[0:16, 6, 0:P], ACT.Copy).then_inc(m_hi_ready, 1)

            for i in range(Q_EARLY, NI):
                act.wait_ge(qk_mm, i + 5)
                act.wait_ge(staged_out[i % 4], 32 * (i // 4) + 128)
                act.activation(stage[i % 4][0], psum[:, Q_BANKS[i % 4], :], ACT.Identity, scale=c_q[:, i // 2:i // 2 + 1]).then_inc(qk_hi, 1)
                if i == Q_EARLY + 4:
                    max_hi(0, 0)
            act.sem_inc(pv_done, 4)
            act.sem_inc(pair_ready, 2)

            def exp(t, k, n):
                i = t * 3 + k
                kt, j = n // 4, n % 4
                if j == 0:
                    act.wait_ge(pv_done, 4 * i + kt + 1)
                    act.wait_ge(pair_ready, 2 * i + kt // 2 + 1)
                act.wait_ge(st_mm, 16 * i + n + 49)
                act.activation(prob_a[:, kt, j, :], psum[:, (0, 4, 5)[(16 * k + n) % 3], :], ACT.Exp, scale=A_SCALE).then_inc(p_ready, 1)

            def copy_values(t, k):
                i = t * 3 + k
                act.wait_ge(pv_done, 4 * i + 8)
                act.wait_ge(att_ready, i + 1)
                act.activation(o_sb, psum[:, 6, :], ACT.Copy).then_inc(o_copied, 1)

            def att_hi(t, k):
                i = t * 3 + k
                act.wait_ge(att_ready, i + 2)
                act.activation(attT_hi[:, ds(i, 1), :], att.unsqueeze(1), ACT.Copy).then_inc(att_hi_ready, 1)

            def step(t, k, done=3, last=False):
                for n in range(16):
                    exp(t, k, n)
                    if n == 5 and done > 1:
                        att_hi(t, k - 2)
                    if n == 7 and done > 0:
                        copy_values(t, k - 1)
                    if n == 9 and not last:
                        max_hi(t, k + 1)

            step(0, 0, done=0)
            act.wait_ge(made, 26)
            act.wait_ge(staged_out[0], 16 * 8 + 32 * NI // 4)
            act.activation(lo_st[:], spread_32.rearrange("p k n -> p (k n)"), ACT.Copy).then_inc(made, 1)
            step(0, 1, done=1)
            with act.Fori(0, A_ROUNDS) as t:
                for k in (2, 3, 4):
                    step(t, k)
            step(0, NI - 2)
            step(0, NI - 1, last=True)
            att_hi(0, NI - 2)
            copy_values(0, NI - 1)
            att_hi(0, NI - 1)
            act.wait_ge(made, 17)
            g0, b0 = COLS["g1"][0], COLS["b1"][0]
            act.sem_inc(qk_stored, 32)
            def rotated_hi(i):
                act.wait_ge(rT_mm, i + 2)
                act.wait_ge(qk_stored, 32 * i + 32)
                act.activation(hi_st[:], psum[:, 6, :], ACT.Copy).then_inc(r_hi, 1)

            def x_round(i, first=False):
                act.wait_ge(hT_mm, i + 1)
                for h in range(2):
                    act.activation(hT[:, 4 * h:4 * h + 4, :], psum[:, 2 + h, :].rearrange("p (c n) -> p c n", c=4), ACT.Copy).then_inc(hT_ready, 1)
                if not first:
                    rotated_hi(i - 1)
                act.wait_ge(ynT_mm, i + 1)
                for n in range(6):
                    act.activation(ynT[:, n, :], psum[:, 6 + n // 4, (n % 4) * P:(n % 4 + 1) * P], ACT.Identity,
                                   scale=cols[:, g0 + n:g0 + n + 1], bias=cols[:, b0 + n:b0 + n + 1]).then_inc(ynT_ready, 1)
                act.wait_ge(qkv_mm, i + 1)
                act.activation(v_x[:, ds(i, 1), :].rearrange("p o (h e) -> p (o h) e", e=32)[:, :, 0:X_HD],
                               psum[:, 5, 0:H].rearrange("p (h e) -> p h e", e=X_HD), ACT.Copy).then_inc(vx_ready, 1)

            x_round(0, first=True)
            with act.Fori(1, NT) as i:
                x_round(i)
            rotated_hi(NT - 1)
            act.sem_inc(xpv_done, 8)

            def x_max_hi(t, k):
                i = t * 3 + k
                act.wait_ge(xmT_done, i + 1)
                if k:
                    act.wait_ge(xm_loaded[(k - 1) % 3], 32 * (t + (k - 1) // 3 + 1))
                act.activation(m_hi[:], psum[0:16, 1, 0:P], ACT.Copy).then_inc(xm_hi, 1)

            def x_copy_out(t, k, n, bank, to):
                i = t * 3 + k
                act.wait_ge(xpv_done, 8 * i + 15 + n)
                act.wait_ge(xatt_ready, i + 1)
                act.activation(to, psum[:, bank, :], ACT.Copy).then_inc(xo_copied, 1)

            def x_step(t, k, first=False, last=False):
                i = t * 3 + k
                for n in range(16):
                    kt, j = n // 4, n % 4
                    if j == 0:
                        act.wait_ge(xpv_done, 8 * i + 2 * kt + 2)
                    act.wait_ge(xst_mm, 16 * i + n + 49)
                    act.activation(prob_x[kt][:, j, :], psum[:, 4 + n % 2, 0:S - kt * P], ACT.Exp, scale=X_SCALE).then_inc(xp_ready, 1)
                    if n == 3 and not first:
                        x_copy_out(t, k - 1, 0, 7, den_sb)
                    if n == 5 and not first:
                        x_copy_out(t, k - 1, 1, 6, o_sb)
                    if n == 9 and not last:
                        x_max_hi(t, k + 1)

            x_max_hi(0, 0)
            run_steps(act, x_step)
            x_copy_out(0, XI - 1, 0, 7, den_sb)
            x_copy_out(0, XI - 1, 1, 6, o_sb)

            def low_rank(k, i):
                act.wait_ge(W["w_mm"][k], i + 2 - k)
                act.activation(low[k], psum[0:DR, 2 * k + 1, 0:P], ACT.Copy).then_inc(W["low_ready"][k], 1)

            def log_part(k, i):
                w = {n: s[k] for n, s in W.items()}
                act.wait_ge(w["az_ready"], i + 1)
                act.activation(e_b, e_b, ACT.Exp, scale=-1.0).then_inc(w["e_ready"], 1)
                act.wait_ge(w["e_ready"], i + 1)
                act.activation(e_b, e_b, ACT.Ln, bias=1.0).then_inc(w["l_ready"], 1)

            def decays(k, i):
                act.wait_ge(W["da_ready"][k], i + 1)
                act.activation(abar[:, 0:3 * H], abar[:, 0:3 * H], ACT.Exp, scale=-1.0).then_inc(W["abar_ready"][k], 1)

            def turned(to, bank, done):
                for h in range(2):
                    act.activation(to[:, 4 * h:4 * h + 4, :], psum[:, bank + h, :].rearrange("p (c n) -> p c n", c=4), ACT.Copy).then_inc(done, 1)

            g2, b2 = COLS["g2"][0], COLS["b2"][0]

            def round_(i, u, first, second, dense, done):
                if first:
                    low_rank(0, i)
                if first:
                    log_part(0, i)
                if dense:
                    act.wait_ge(fT_mm, i - 1)
                    turned(hT_f, 6, fT_ready)
                if second:
                    low_rank(1, i - 1)
                if first:
                    decays(0, i)
                if dense:
                    act.wait_ge(ax_mm, i - 1)
                    act.activation(ax, psum[:, 5, 0:R2], ACT.Copy).then_inc(ax_ready, 1)
                if first:
                    act.wait_ge(h2T_mm, i + 1)
                    turned(hT, 6, h2T_ready)
                if dense:
                    act.wait_ge(axT_mm, i - 1)
                    act.activation(axT, psum[0:R2, 5, P:2 * P], ACT.Copy).then_inc(axT_ready, 1)
                if first:
                    act.wait_ge(y2T_mm, i + 1)
                    for n in range(4):
                        act.activation(ynT[:, n, :], psum[:, 7, n * P:(n + 1) * P], ACT.Identity,
                                       scale=cols[:, g2 + n:g2 + n + 1], bias=cols[:, b2 + n:b2 + n + 1]).then_inc(y2T_ready, 1)
                if second:
                    log_part(1, i - 1)
                    decays(1, i - 1)
                if first:
                    act.wait_ge(gu_mm, i + 1)
                    act.activation(mlpT_f.rearrange("p (h n) -> p h n", h=2), psum[:, 0:2, :], ACT.Tanh, scale=0.5).then_inc(tanh_ready, 1)

            run_rounds(act, round_)

        @block.vector
        def _(dve):
            dve.memset(w_abs[:, 0:QKV], 0.0).then_inc(qkv_summed, 2)
            dve.wait_ge(s_const, 64)
            dve.tensor_copy(pos_f[:], pos_i[:]).then_inc(ang_step, 1)
            dve.wait_ge(ang_step, 1)
            for f in range(HALF):
                dve.tensor_scalar(ang[:, :, f], pos_f[:], float(ROPE_INV[f]), None, ALU.mult).then_inc(ang_step, 1)
            dve.wait_ge(ang_step, 1 + HALF)
            n_step = 1 + HALF

            def link(ins):
                nonlocal n_step
                ins.then_inc(ang_step, 1)
                n_step += 1
                dve.wait_ge(ang_step, n_step)

            for k in range(2):
                n, r = trig_n[:, k], trig_r[:, k]
                link(dve.tensor_scalar(n, ang, float(1 / TWO_PI), 0.25 * k, ALU.mult, ALU.add))
                link(dve.tensor_scalar(n, n, MAGIC, None, ALU.add))
                link(dve.tensor_scalar(n, n, -MAGIC, None, ALU.add))
                link(dve.scalar_tensor_tensor(r, n, -TP1, ang, ALU.mult, ALU.add))
                link(dve.scalar_tensor_tensor(r, n, -TP2, r, ALU.mult, ALU.add))
                link(dve.scalar_tensor_tensor(r, n, -TP3, r, ALU.mult, ALU.add))
                link(dve.tensor_scalar(r, r, float(k * np.pi / 2), 3.1415925, ALU.add, ALU.min))
                link(dve.tensor_scalar(r, r, -3.1415925, None, ALU.max))
            dve.sem_inc(trig_done, 1)

            with dve.Fori(0, NT // 2) as it:
                for u in range(2):
                    i = it * 2 + u
                    dve.wait_ge(x_slot[u], 16 * (it + 1))
                    for h in range(2):
                        dve.bn_stats(st[:, u, h, :], x_in[:, u, h * 512:(h + 1) * 512]).then_inc(ln_step, 1)
                    wait_apart(dve, (ln_step, 4 * i + 2))
                    dve.bn_aggr(mv[:, u, :], st[:, u]).then_inc(ln_step, 1)
                    dve.wait_ge(ln_step, 4 * i + 3)
                    dve.tensor_scalar(ve[:, u, :], mv[:, u, 1:2], LN_EPS, None, ALU.add).then_inc(ln_step, 1)
                    dve.wait_ge(ln_rstd, i + 1)
                    dve.tensor_scalar(x_in[:, u, :], x_in[:, u, :], mv[:, u, 0:1], rstd[:, u, 0:1],
                                      ALU.subtract, ALU.mult).then_inc(xn_ready, 1)
                    dve.wait_ge(qkv_summed, i + 2)
                    dve.wait_ge(abs_taken, i + 1)
                    dve.tensor_tensor(w_abs[:, 0:QKV], w_in[u][:, 0:QKV], w_abs[:, 0:QKV], ALU.add).then_inc(qkv_summed, 1)
                    for h in range(2):
                        dve.wait_ge(xT_hi, 2 * i + h + 1)
                        dve.tensor_tensor(xnT_lo[:, 4 * h:4 * h + 4, ds(i * P, P)],
                                          psum[:, 2 * u + h, :].rearrange("p (c n) -> p c n", c=4),
                                          xnT_hi[:, 4 * h:4 * h + 4, ds(i * P, P)], ALU.subtract).then_inc(xT_free, 1)
            dve.wait_ge(means_done, 1)
            for h in range(2):
                dve.scalar_tensor_tensor(c_o[:, h * 512:(h + 1) * 512], psum[:, 4 + h, :], 1e-8,
                                         scale_rows[:, KVD + h * 512:KVD + (h + 1) * 512], ALU.max, ALU.mult).then_inc(c_ready, 1)
            dve.scalar_tensor_tensor(c_v, psum[:, 6, 0:KVD], 1e-8, scale_rows[:, 0:KVD], ALU.max, ALU.mult).then_inc(c_ready, 1)
            dve.scalar_tensor_tensor(c_k[:], psum[:, 7, KC:KC + 2], 1e-8, cols[:, slice(*COLS["k_scale"])], ALU.max, ALU.mult).then_inc(c_ready, 1)
            dve.scalar_tensor_tensor(c_q[:], psum[:, 7, 0:KC], 1e-8, cols[:, slice(*COLS["q_scale"])], ALU.max, ALU.mult).then_inc(c_ready, 1)
            dve.wait_ge(c_ready, 5)
            for n in range(4):
                dve.wait_ge(qk_hi, n + 1)
                dve.scalar_tensor_tensor(stage[n][1], psum[:, n, :], c_k[:, n % 2:n % 2 + 1], stage[n][0].bitcast(F32), ALU.mult, ALU.subtract).then_inc(qk_lo, 1)
            with dve.Fori(0, NT // 2) as it:
                for u in range(2):
                    i = it * 2 + u
                    dve.wait_ge(v_mm, i + 1)
                    dve.scalar_tensor_tensor(v_heads[:, :, ds(i, 1), :].rearrange("p g o e -> p g (o e)"),
                                             psum[:, 4 + u, 0:KVD].rearrange("p (g e) -> p g e", e=A_HD), V_GAIN,
                                             c_v.rearrange("p (g e) -> p g e", e=A_HD), ALU.mult, ALU.mult).then_inc(v_ready, 1)
            dve.wait_ge(trig_done, 4)
            for m in range(2):
                for h in range(2):
                    dve.wait_ge(lora_mm, R4 + 2 * m + h + 1)
                    dve.tensor_copy(b_eff[:, m, h * 512:(h + 1) * 512], psum[:, 4 + 2 * m + h, :]).then_inc(lora_ready, 1)
            with dve.Fori(0, Q_EARLY // 4) as it:
                for u in range(4):
                    i = it * 4 + u
                    dve.wait_ge(qk_hi, i + 5)
                    dve.scalar_tensor_tensor(stage[u][1], psum[:, Q_BANKS[u], :], c_q[:, ds(it * 2 + u // 2, 1)], stage[u][0].bitcast(F32),
                                             ALU.mult, ALU.subtract).then_inc(qk_lo, 1)

            def maximum(t, k, n):
                i = t * 3 + k
                dve.wait_ge(s_mm, 16 * i + n + 1)
                dve.tensor_reduce(m_neg[:, k % 3, n:n + 1], psum[:, 1 + (16 * k + n) % 3, :], AX_X, ALU.max, negate=True).then_inc(s_max, 1)

            def max_lo(t, k):
                i = t * 3 + k
                dve.wait_ge(m_hi_ready, i + 1)
                dve.tensor_tensor(m_lo[:], psum[0:16, 6, 0:P], m_hi[:].bitcast(F32), ALU.subtract).then_inc(m_lo_ready, 1)

            dve.wait_ge(made, 11)
            dve.tensor_reduce(den_mask, ident[:, 1:P:A_HD // QT], AX_X, ALU.add, negate=True)
            for i in range(Q_EARLY, NI):
                u = i % 4
                for n in early_scores(i, 0):
                    maximum(0, n // 16, n % 16)
                dve.wait_ge(qk_hi, i + 5)
                dve.scalar_tensor_tensor(stage[u][1], psum[:, Q_BANKS[u], :], c_q[:, i // 2:i // 2 + 1], stage[u][0].bitcast(F32),
                                         ALU.mult, ALU.subtract).then_inc(qk_lo, 1)
                for n in early_scores(i, 1):
                    maximum(0, n // 16, n % 16)
                if i == Q_EARLY + 4:
                    max_lo(0, 0)

            def invert(t, k):
                i = t * 3 + k
                dve.wait_ge(den_done, 2 * i + 4)
                dve.reciprocal(den_inv, psum[:, 7, 0:P]).then_inc(den_rec, 1)

            def round_inverse(t, k):
                dve.wait_ge(den_rec, 3 * (t * 3 + k) + 1)
                dve.tensor_copy(den_hi, den_inv).then_inc(den_rec, 1)

            def inverse_parts(t, k):
                dve.wait_ge(den_rec, 3 * (t * 3 + k) + 2)
                dve.scalar_tensor_tensor(den_parts, den_hi.bitcast(F32), den_mask, den_inv, ALU.mult, ALU.add).then_inc(den_rec, 1)

            def normalise(t, k):
                i = t * 3 + k
                dve.wait_ge(o_copied, i + 2)
                dve.wait_ge(den_spread, i + 1)
                dve.wait_ge(att_lo_ready, i + 1)
                dve.tensor_tensor(att, o_sb, psum[:, 7, :], ALU.mult).then_inc(att_ready, 1)

            def step(t, k, done=3, left=2):
                for n in range(16):
                    if n < 16 - LEAD and left > 0:
                        maximum(t, k + 1, n + LEAD)
                    if n >= 16 - LEAD and left > 1:
                        maximum(t, k + 2, n + LEAD - 16)
                    if n == 10 and left > 0:
                        max_lo(t, k + 1)
                    if n == 3 and done > 1:
                        normalise(t, k - 2)
                    if n == 11 and done > 0:
                        invert(t, k - 1)
                    if n == 12 and done > 0:
                        round_inverse(t, k - 1)
                    if n == 13 and done > 0:
                        inverse_parts(t, k - 1)

            step(0, 0, done=0)
            step(0, 1, done=1)
            with dve.Fori(0, A_ROUNDS) as t:
                for k in (2, 3, 4):
                    step(t, k)
            for i in (NI - 2, NI - 1):
                step(0, i, left=NI - 1 - i)
            normalise(0, NI - 2)
            invert(0, NI - 1)
            round_inverse(0, NI - 1)
            inverse_parts(0, NI - 1)
            normalise(0, NI - 1)

            dve.wait_ge(trig_done, 4)
            def residual(i, u, use, h_done):
                for h in range(2):
                    dve.wait_ge(op_mm, 2 * i + h + 1)
                    if h == 0 and h_done is not None:
                        dve.wait_ge(hT_mm, h_done)
                    dve.scalar_tensor_tensor(y0[:, h * 512:(h + 1) * 512], psum[:, h, :], 1.0 / V_GAIN, c_o[:, h * 512:(h + 1) * 512],
                                             ALU.mult, ALU.mult).then_inc(y0_ready, 1)
                dve.wait_ge(y0_ready, 2 * i + 4)
                dve.wait_ge(x_slot[u], 16 * (NT // 2) + 16 * use)
                dve.tensor_tensor(x1[:, ds(i, 1), :], y0.unsqueeze(1), x_in[:, u:u + 1, :], ALU.add).then_inc(x1_ready, 1)
                wait_apart(dve, (x1_ready, i + 1))
                for h in range(2):
                    dve.bn_stats(st[:, 0, h, :], x1[:, ds(i, 1), h * 512:(h + 1) * 512]).then_inc(l_step, 1)
                wait_apart(dve, (l_step, 5 * i + 2))
                dve.bn_aggr(mv[:, 0, :], st[:, 0]).then_inc(l_step, 1)
                dve.wait_ge(l_step, 5 * i + 3)
                dve.tensor_copy(mvs[:, ds(2 * i, 2)], mv[:, 0, :]).then_inc(l_step, 1)
                dve.tensor_scalar(ves[:], mv[:, 0, 1:2], LN_EPS, None, ALU.add).then_inc(l_step, 1)
                dve.wait_ge(l_rstd, i + 1)
                dve.tensor_scalar(h_st, x1[:, ds(i, 1), :].rearrange("p o n -> p (o n)"), mvs[:, ds(2 * i, 1)], rstds[:, ds(i, 1)],
                                  ALU.subtract, ALU.mult).then_inc(h_ready, 1)

            def read(i):
                dve.wait_ge(y_mm, i + 1)
                y = [psum[:, 4 + h, 0:4 * 3 * HC].rearrange("p (c o n) -> p c o n", c=4, o=3) for h in range(2)]
                for o in range(3):
                    for h in range(2):
                        dve.bn_stats(st3[:, o, h, :], y[h][:, :, o, :]).then_inc(y_step, 1)
                wait_apart(dve, (y_step, 10 * i + 6))
                for o in range(3):
                    dve.bn_aggr(mv3[:, o, :], st3[:, o]).then_inc(y_step, 1)
                dve.wait_ge(y_step, 10 * i + 9)
                dve.tensor_scalar(ve3[:], mv3[:, :, 1], LN_EPS, None, ALU.add).then_inc(y_step, 1)
                dve.wait_ge(y_rstd, i + 1)
                dve.wait_ge(rT_mm, i + 1)
                for o in range(3):
                    for h in range(2):
                        dve.tensor_scalar(yn[:, o * H + h * P:o * H + (h + 1) * P].rearrange("p (c n) -> p c n", c=4), y[h][:, :, o, :],
                                          mv3[:, o, 0:1], rs3[:, o:o + 1], ALU.subtract, ALU.mult).then_inc(yn_ready, 1)

            def rope(i):
                dve.wait_ge(qkv_mm, i + 1)
                qk = psum[:, 4, :].rearrange("p (h e f) -> p h e f", e=2, f=HALF)
                to = rot.rearrange("p (h e f) -> p h e f", e=2, f=HALF)
                other = rope_a.rearrange("p (h f) -> p h f", f=HALF)

                def angle(k):
                    return trig[:, k, ds(i, 1), :].broadcast_to([P, 2 * X_NH, HALF])

                for e in range(2):
                    dve.tensor_tensor(to[:, :, e, :], qk[:, :, e, :], angle(1), ALU.mult).then_inc(rope_step, 1)
                for e in range(2):
                    dve.tensor_tensor(other, qk[:, :, 1 - e, :], angle(0 if e else 2), ALU.mult).then_inc(rope_step, 1)
                    dve.wait_ge(rope_step, 6 * i + 9 + 2 * e)
                    dve.tensor_tensor(to[:, :, e, :], to[:, :, e, :], other, ALU.add).then_inc(rope_step, 1)
                    dve.wait_ge(rope_step, 6 * i + 10 + 2 * e)

            def split(i):
                dve.wait_ge(r_hi, i + 1)
                dve.tensor_tensor(lo_st[:], psum[:, 6, :], hi_st[:].bitcast(F32), ALU.subtract).then_inc(r_lo, 1)

            dve.sem_inc(rT_mm, 1)
            dve.sem_inc(y0_ready, 2)
            residual(0, 0, 1, None)
            read(0)
            residual(1, 1, 1, 1)
            rope(0)
            with dve.Fori(0, NT // 2 - 1) as it:
                for u in range(2):
                    i = it * 2 + 1 + u
                    read(i)
                    split(i - 1)
                    residual(i + 1, u, it + 2, i + 1)
                    rope(i)
            read(NT - 1)
            split(NT - 2)
            rope(NT - 1)
            split(NT - 1)

            def x_maximum(t, k, n):
                i = t * 3 + k
                dve.wait_ge(xs_mm, 16 * i + n + 1)
                dve.tensor_reduce(m_neg[:, k % 3, n:n + 1], psum[:, (0, 2, 3)[(16 * k + n) % 3], 0:(n % QT + 1) * P], AX_X, ALU.max, negate=True).then_inc(xs_max, 1)

            def x_max_lo(t, k):
                i = t * 3 + k
                dve.wait_ge(xm_hi, i + 1)
                dve.tensor_tensor(m_lo[:], psum[0:16, 1, 0:P], m_hi[:].bitcast(F32), ALU.subtract).then_inc(xm_lo, 1)

            def x_invert(t, k, n):
                i = t * 3 + k
                if n == 0:
                    dve.wait_ge(xo_copied, 2 * i + 3)
                part = den_sb[:, n * P:(n + 1) * P]
                dve.reciprocal(part, part).then_inc(xden_rec, 1)

            def x_step(t, k, first=False, last=False):
                for n in range(16):
                    if not last:
                        x_maximum(t, k + 1, n)
                if not last:
                    x_max_lo(t, k + 1)
                if not first:
                    for n in range(4):
                        x_invert(t, k - 1, n)

            for n in range(16):
                x_maximum(0, 0, n)
            x_max_lo(0, 0)
            run_steps(dve, x_step)
            for n in range(4):
                x_invert(0, XI - 1, n)

            def write(k, i, h, to, meanwhile=None):
                w = {n: s[k] for n, s in W.items()}
                bank = 2 * k
                wab = rows[:, slice(*ROWS[f"wab{k + 1}"])]
                mid = [HS, RH, C - 1]
                h4 = h.rearrange("p (s r c) -> p s r c", s=HS, r=RH)
                to4 = to.rearrange("p (s r c) -> p s r c", s=HS, r=RH)
                o2 = psum[:, bank, 0:H].rearrange("p (s r) -> p s r", s=HS)
                bb3 = bbar[:, 0:3 * H].rearrange("p (s r c) -> p s r c", s=HS, r=RH)
                bs2 = b_skip.rearrange("p (s r) -> p s r", s=HS)
                dve.wait_ge(w["du_mm"], i + 1)
                dve.tensor_tensor(z_b[:, 0:H], psum[:, bank + 1, H:2 * H], rows[:, slice(*ROWS[f"du{k + 1}"])], ALU.add).then_inc(w["z_ready"], 1)
                dve.tensor_tensor(z_b[:, H:], psum[:, bank, H:N_Z], wab[:, 0:N_A], ALU.add).then_inc(w["z_ready"], 1)
                dve.tensor_tensor(ab_b, psum[:, bank, N_Z:H + N_AB], wab[:, N_A:], ALU.add).then_inc(w["z_ready"], 1)
                dve.wait_ge(w["z_ready"], 3 * i + 3)
                dve.scalar_tensor_tensor(e_b, z_b, -1.0, z_b, ALU.mult, ALU.max).then_inc(w["az_ready"], 1)
                if meanwhile is not None:
                    finish(meanwhile)
                dve.wait_ge(w["l_ready"], i + 1)
                dve.scalar_tensor_tensor(sp_b[:], z_b, 0.0, e_b, ALU.max, ALU.add).then_inc(w["sp_ready"], 1)
                dve.wait_ge(w["sp_ready"], i + 1)
                dve.tensor_scalar(rc_b, sp_b[:, H:], SSM_EPS, None, ALU.add).then_inc(w["r_step"], 1)
                dve.wait_ge(w["r_step"], 3 * i + 1)
                dve.reciprocal(rc_b, rc_b).then_inc(w["r_step"], 1)
                dve.wait_ge(w["r_step"], 3 * i + 2)
                dve.scalar_tensor_tensor(r_b, ab_b[:, 0:N_A], -1.0, rc_b, ALU.mult, ALU.mult).then_inc(w["r_step"], 1)
                dve.tensor_tensor(bs2, sp_b[:, 0:H].rearrange("p (s r) -> p s r", s=HS),
                                  ab_b[:, N_A:].unsqueeze(1).broadcast_to([P, HS, RH]), ALU.mult).then_inc(w["b_step"], 1)
                dve.wait_ge(w["b_step"], 4 * i + 1)
                dve.tensor_tensor(bs2, bs2, o2, ALU.mult).then_inc(w["b_step"], 1)
                dve.wait_ge(w["b_step"], 4 * i + 2)
                dve.tensor_tensor(to4[:, :, :, C - 1], h4[:, :, :, C - 1], bs2, ALU.add).then_inc(w["hn_ready"], 1)
                dve.wait_ge(w["abar_ready"], i + 1)
                dve.wait_ge(w["r_step"], 3 * i + 3)
                dve.scalar_tensor_tensor(bbar[:, 0:3 * H].rearrange("p (s n) -> p s n", s=HS), abar[:, 0:3 * H].rearrange("p (s n) -> p s n", s=HS),
                                         -1.0, r_b.unsqueeze(1).broadcast_to([P, HS, N_A]), ALU.add, ALU.mult).then_inc(w["b_step"], 1)
                dve.wait_ge(w["b_step"], 4 * i + 3)
                dve.tensor_tensor(bb3, bb3, o2.unsqueeze(3).broadcast_to([P] + mid), ALU.mult).then_inc(w["b_step"], 1)
                dve.wait_ge(w["b_step"], 4 * i + 4)
                dve.wait_ge(w["ha_ready"], i + 1)
                dve.tensor_tensor(to4[:, :, :, 0:C - 1], h_a.rearrange("p (s r c) -> p s r c", s=HS, r=RH), bb3, ALU.add).then_inc(w["hn_ready"], 1)

            def to_mid(i, u, done):
                x1_t = x1[:, ds(i, 1), :].rearrange("p o n -> p (o n)")
                dve.tensor_scalar(h_in, x1_t, mvs[:, ds(2 * i, 1)], rstds[:, ds(i, 1)], ALU.subtract, ALU.mult).then_inc(h2_ready, 1)
                dve.wait_ge(h2_ready, i + 1)
                write(0, i, h_in, h_mid[u], i - 3 if done else None)

            def read_2(i):
                dve.wait_ge(y2_mm, i + 1)
                y = psum[:, 6, :].rearrange("p (c o n) -> p c o n", c=KC, o=2)
                for o in range(2):
                    dve.bn_stats(st3[:, o, 0, :], y[:, :, o, :]).then_inc(y2_step, 1)
                wait_apart(dve, (y2_step, 5 * i + 2))
                for o in range(2):
                    dve.bn_aggr(mv3[:, o, :], st3[:, o, 0, :]).then_inc(y2_step, 1)
                dve.wait_ge(y2_step, 5 * i + 4)
                dve.tensor_scalar(ve3[:, 0:2], mv3[:, 0:2, 1], LN_EPS, None, ALU.add).then_inc(y2_step, 1)
                dve.wait_ge(y2_rstd, i + 1)
                for o in range(2):
                    dve.tensor_scalar(yn[:, o * H:(o + 1) * H].rearrange("p (c n) -> p c n", c=KC), y[:, :, o, :],
                                      mv3[:, o, 0:1], rs3[:, o:o + 1], ALU.subtract, ALU.mult).then_inc(y2n_ready, 1)

            def gated(i):
                dve.wait_ge(tanh_ready, i + 1)
                t2 = mlpT_f.rearrange("p (h n) -> p h n", h=2)
                dve.scalar_tensor_tensor(t2, t2, 1.0, psum[:, 0:2, :], ALU.add, ALU.mult).then_inc(g_ready, 1)
                dve.wait_ge(g_ready, i + 1)
                dve.scalar_tensor_tensor(t2, t2, 0.5, psum[:, 6:8, :], ALU.mult, ALU.mult).then_inc(mlp_ready, 1)

            def to_dense(i):
                x1_t = x1[:, ds(i, 1), :].rearrange("p o n -> p (o n)")
                dve.wait_ge(W["hn_ready"][1], 2 * i + 4)
                dve.tensor_tensor(x1_t, x1_t, h_out, ALU.add).then_inc(x2_ready, 1)
                wait_apart(dve, (x2_ready, i + 1))
                for h in range(2):
                    dve.bn_stats(st[:, 0, h, :], x1[:, ds(i, 1), h * 512:(h + 1) * 512]).then_inc(f_step, 1)
                wait_apart(dve, (f_step, 4 * i + 2))
                dve.bn_aggr(mv[:, 0, :], st[:, 0]).then_inc(f_step, 1)
                dve.wait_ge(f_step, 4 * i + 3)
                dve.tensor_scalar(ves[:], mv[:, 0, 1:2], LN_EPS, None, ALU.add).then_inc(f_step, 1)
                dve.wait_ge(f_rstd, i + 1)
                dve.tensor_scalar(h_out, x1_t, mv[:, 0, 0:1], rstd[:, 0, 0:1], ALU.subtract, ALU.mult).then_inc(xf_ready, 1)

            def finish(i):
                dve.wait_ge(f_mm, i + 2)
                dve.wait_ge(out_stored, 16 * i + 16)
                o3 = out_t.rearrange("p (h n) -> p h n", h=2)
                dve.tensor_tensor(o3, psum[:, 4:6, :], rows[:, slice(*ROWS["bias"])].rearrange("p (h n) -> p h n", h=2), ALU.add).then_inc(o_step, 1)
                dve.wait_ge(o_step, i + 2)
                dve.tensor_tensor(out_t.unsqueeze(1), out_t.unsqueeze(1), x1[:, ds(i, 1), :], ALU.add).then_inc(out_ready, 1)

            def round_(i, u, first, second, dense, done):
                if done and not first:
                    finish(i - 3)
                if first:
                    to_mid(i, u, done)
                    read_2(i)
                if second:
                    if dense:
                        dve.wait_ge(fT_mm, i - 1)
                    write(1, i - 1, h_mid[1 - u], h_out)
                if first:
                    gated(i)
                if second:
                    to_dense(i - 1)

            dve.wait_ge(y_stored, 16 * NQ * XI + 16)
            dve.sem_inc(out_stored, 16)
            run_rounds(dve, round_)
            finish(NT - 1)

        @block.tensor
        def _(pe):
            pe.sem_inc(xT_free, 4)
            pe.wait_ge(made, 11)
            with pe.Fori(0, NT // 2) as it:
                for u in range(2):
                    i = it * 2 + u
                    pe.wait_ge(xn_ready, i + 1)
                    pe.wait_ge(xT_free, 2 * i + 2)
                    for c in range(KC):
                        mm = pe.transpose(psum[:, 2 * u + c // 4, (c % 4) * P:(c % 4 + 1) * P], x_in[:, u, c * P:(c + 1) * P], ident[:])
                        if c == KC - 1:
                            mm.then_inc(xT_done, 1)
            pe.wait_ge(qkv_summed, NT + 2)
            pe.wait_ge(o_summed, NT + 2)
            for h in range(2):
                pe.matmul(psum[:, 4 + h, :], mean_w, w_abs[:, QKV + h * 512:QKV + (h + 1) * 512], start=True, stop=True)
            pe.matmul(psum[:, 6, 0:KVD], mean_w, w_abs[:, D + KVD:QKV], start=True, stop=True)
            for c in range(KC + 2):
                mm = pe.matmul(psum[:, 7, c:c + 1], w_abs[:, c * P:(c + 1) * P], mean_w[:, 0:1], start=True, stop=True)
            mm.then_inc(means_done, 1)
            pe.wait_ge(signs_done, 2 * NT)
            pe.wait_ge(xT_free, 2 * NT + 4)

            def project(bank, width, weights, tokens, swap=False, chunks=range(KC)):
                for c in chunks:
                    for part in range(2):
                        x = (xnT_hi, xnT_lo)[part]
                        w = weights(c)
                        mm = pe.matmul(psum[:, bank, 0:width], *((x[:, c, tokens], w) if swap else (w, x[:, c, tokens])),
                                       start=(c == 0 and part == 0), stop=(c == KC - 1 and part == 1))
                return mm

            for n in range(4):
                b, m = n // 2, n % 2
                project(n, S, lambda c: sign_qkv[:, c, D + m * P:D + (m + 1) * P], slice(b * S, (b + 1) * S)).then_inc(qk_mm, 1)
            pe.wait_ge(c_ready, 5)
            pe.sem_inc(v_ready, 2)
            with pe.Fori(0, NT // 2) as it:
                for u in range(2):
                    i = it * 2 + u
                    pe.wait_ge(v_ready, i + 1)
                    project(4 + u, KVD, lambda c: sign_qkv[:, c, D + KVD:QKV], ds(i * P, P), swap=True).then_inc(v_mm, 1)
            pe.wait_ge(qk_lo, 4)
            pe.wait_ge(v_ready, NT + 2)
            pe.wait_ge(lora_loaded, 16 * (2 * R4 + 2))
            for r in range(R4):
                for c in range(KC):
                    mm = pe.matmul(psum[:, r, c * NT * R8:(c + 1) * NT * R8], lora_in[:, r, c * P:(c + 1) * P], gate_a, start=True, stop=True)
                mm.then_inc(lora_mm, 1)
            for m in range(2):
                for h in range(2):
                    for k in range(R4):
                        mm = pe.matmul(psum[:, 4 + 2 * m + h, :], gate_b[:, k, m * P:(m + 1) * P], lora_in[:, R4 + k, h * 512:(h + 1) * 512],
                                       start=(k == 0), stop=(k == R4 - 1))
                    mm.then_inc(lora_mm, 1)
            def project_q(i, u, g, chunks=range(KC)):
                if chunks[0] == 0:
                    pe.wait_ge(qk_lo, i + 1)
                return project(Q_BANKS[u], S, lambda c: sign_qkv[:, c, ds(g * P, P)], slice(u % 2 * S, (u % 2 + 1) * S), chunks=chunks)

            pe.wait_ge(lora_ready, R4 + 4)
            pe.sem_inc(s_max, 3)
            with pe.Fori(0, Q_EARLY // 4) as it:
                for u in range(4):
                    project_q(it * 4 + u, u, it * 2 + u // 2).then_inc(qk_mm, 1)

            def score(t, k, n):
                i, u = t * 3 + k, k % 3
                if n == 0:
                    pe.wait_ge(qk_loaded[u], 96 * (t + k // 3 + 1))
                j, qt = n // QT, n % QT
                pe.wait_ge(s_max, 16 * i + n + 1)
                pe.matmul(psum[:, 1 + (16 * k + n) % 3, :], qa_op[u][0:A_MAX, j, qt * P:(qt + 1) * P], k_op[u][0:A_MAX, :],
                          start=True, stop=True).then_inc(s_mm, 1)

            def turn_max(t, k):
                i = t * 3 + k
                pe.wait_ge(s_max, 16 * i + 19)
                if k:
                    pe.wait_ge(m_lo_ready, i)
                    pe.wait_ge(o_copied, i)
                pe.transpose(psum[0:16, 6, 0:P], m_neg[:, k % 3, :], ident[:]).then_inc(mT_done, 1)

            for i in range(Q_EARLY, NI):
                project_q(i, i % 4, i // 2, range(KC // 2))
                for n in early_scores(i, 0):
                    score(0, n // 16, n % 16)
                project_q(i, i % 4, i // 2, range(KC // 2, KC)).then_inc(qk_mm, 1)
                if i == Q_EARLY + 4:
                    turn_max(0, 0)
                for n in early_scores(i, 1):
                    score(0, n // 16, n % 16)
            pe.wait_ge(qk_lo, NI + 3)
            pe.sem_inc(p_ready, 3)
            pe.sem_inc(o_copied, 1)

            def shifted(t, k, n):
                i, u = t * 3 + k, k % 3
                kt, j = n // 4, n % 4
                if n == 0:
                    pe.wait_ge(m_loaded[u], 32 * (t + k // 3 + 1))
                pe.wait_ge(p_ready, 16 * i + n + 1)
                pe.matmul(psum[:, (0, 4, 5)[(16 * k + n) % 3], :], k_op[u][0:A_ROWS, kt * P:(kt + 1) * P], qa_op[u][0:A_ROWS, j, :],
                          start=True, stop=True).then_inc(st_mm, 1)

            def values(t, k, kt, last=False):
                i = t * 3 + k
                pe.wait_ge(p_ready, 16 * i + 4 * kt + 7)
                if kt == 0:
                    pe.wait_ge(vg_ready, i + 1)
                    pe.wait_ge(o_copied, i + 1)
                    if not last:
                        pe.wait_ge(m_lo_ready, i + 2)
                for j in range(A_REP):
                    mm = pe.matmul(psum[j * 32:(j + 1) * 32, 6, :], v_g[:, k % 3, kt, :], prob_a[:, kt, j, :], start=(kt == 0), stop=(kt == QT - 1))
                mm.then_inc(pv_done, 1)

            def denominators(t, k, n):
                i = t * 3 + k
                pe.wait_ge(pair_ready, 2 * i + n + 3)
                if n == 0:
                    pe.wait_ge(att_ready, i + 1)
                for q in range(QT):
                    for j in range(A_REP):
                        mm = pe.matmul(psum[j * 32:(j + 1) * 32, 7, 0:P], den_sel[:, q, :], pair_sum[:, n, j, q * P:(q + 1) * P],
                                       start=(n == 0 and q == 0), stop=(n == 1 and q == QT - 1))
                mm.then_inc(den_done, 1)

            def spread_inverse(t, k):
                i = t * 3 + k
                pe.wait_ge(den_rec, 3 * i + 3)
                for q in range(QT):
                    mm = pe.matmul(psum[:, 7, q * P:(q + 1) * P], spread[:, q, :], den_parts, start=True, stop=True)
                mm.then_inc(den_spread, 1)

            def step(t, k, done=3, left=2):
                for n in range(16):
                    if n < 16 - LEAD and left > 0:
                        score(t, k + 1, n + LEAD)
                    if n >= 16 - LEAD and left > 1:
                        score(t, k + 2, n + LEAD - 16)
                    shifted(t, k, n)
                    if n == 1 and done > 1:
                        spread_inverse(t, k - 2)
                    if n in (2, 4, 6) and done > 0:
                        values(t, k - 1, n // 2)
                    if n in (7, 10) and done > 0:
                        denominators(t, k - 1, n // 10)
                    if n == 8 and left > 0:
                        turn_max(t, k + 1)
                    if n == 14:
                        values(t, k, 0, last=left == 0)

            step(0, 0, done=0)
            pe.wait_ge(qk_lo, NI + 4)
            pe.wait_ge(made, 26)
            step(0, 1, done=1)
            pe.wait_ge(made, 27)
            with pe.Fori(0, A_ROUNDS) as t:
                for k in (2, 3, 4):
                    step(t, k)
            for i in (NI - 2, NI - 1):
                step(0, i, left=NI - 1 - i)
            spread_inverse(0, NI - 2)
            for n in range(3):
                values(0, NI - 1, 1 + n)
            for n in range(2):
                denominators(0, NI - 1, n)
            spread_inverse(0, NI - 1)

            pe.wait_ge(att_hi_ready, NI)
            pe.wait_ge(att_lo_ready, NI + 1)

            def out_proj(i, h, begin=0, end=2 * KC):
                if begin == 0:
                    pe.wait_ge(y0_ready, 2 * i + 1 + h)
                for n in range(begin, end):
                    mm = pe.matmul(psum[:, h, :], (o_in_hi, o_in_lo)[n % 2][:, n // 2, ds(i * P, P)], sign_o[:, n // 2, h * 512:(h + 1) * 512],
                                   start=(n == 0), stop=(n == 2 * KC - 1))
                if end == 2 * KC:
                    mm.then_inc(op_mm, 1)

            def turn(bank, src, n, done):
                for c in range(n):
                    mm = pe.transpose(psum[:, bank + c // 4, (c % 4) * P:(c % 4 + 1) * P], src[:, c * P:(c + 1) * P], ident[:])
                mm.then_inc(done, 1)

            pe.wait_ge(xw_loaded, 16 * 6)

            def turn_rotated(i):
                pe.wait_ge(rope_step, 6 * i + 12)
                turn(6, rot, 4, rT_mm)

            def x_round(i, first=False, last=False):
                pe.wait_ge(h_ready, i + 1)
                turn(2, h_st, KC, hT_mm)
                if not last:
                    out_proj(i + 1, 0, 0, OP_HT)
                pe.wait_ge(hT_ready, 2 * i + 2)
                pe.wait_ge(vx_ready, i + 1)
                pe.wait_ge(rope_step, 6 * i + 6)
                for c in range(KC):
                    mm = pe.matmul(psum[:, 4 + c // 4, (c % 4) * 3 * HC:(c % 4 + 1) * 3 * HC], hT[:, c, :], read1[:, c, :], start=True, stop=True)
                mm.then_inc(y_mm, 1)
                if not first:
                    turn_rotated(i - 1)
                if not last:
                    out_proj(i + 1, 0, OP_HT)
                    out_proj(i + 1, 1, 0, OP_YN)
                pe.wait_ge(yn_ready, 6 * i + 6)
                pe.wait_ge(r_lo, i + 1)
                turn(6, yn, 6, ynT_mm)
                if not last:
                    out_proj(i + 1, 1, OP_YN)
                pe.wait_ge(ynT_ready, 6 * i + 6)
                for o in range(3):
                    for k in range(2):
                        mm = pe.matmul(psum[:, 4 + o // 2, (o % 2) * H:(o % 2 + 1) * H], ynT[:, 2 * o + k, :], wqkv[:, 2 * o + k, :],
                                       start=(k == 0), stop=(k == 1))
                mm.then_inc(qkv_mm, 1)

            pe.sem_inc(vx_ready, 1)
            pe.sem_inc(rope_step, 6)
            pe.sem_inc(r_lo, 1)
            out_proj(0, 0)
            out_proj(0, 1)
            x_round(0, first=True)
            with pe.Fori(1, NT - 1) as i:
                x_round(i)
            x_round(NT - 1, last=True)
            turn_rotated(NT - 1)

            pe.sem_inc(xs_max, 3)
            pe.sem_inc(xp_ready, 2)
            pe.sem_inc(xo_copied, 2)
            pe.wait_ge(r_lo, NT + 1)

            def x_score(t, k, n):
                i, u = t * 3 + k, k % 3
                if n == 0:
                    pe.wait_ge(xq_loaded[u], 128 * (t + k // 3 + 1))
                j, qt = n // QT, n % QT
                bank = psum[:, (0, 2, 3)[(16 * k + n) % 3], :]
                pe.wait_ge(xs_max, 16 * i + n + 1)
                pe.matmul(bank[:, 0:(qt + 1) * P], qx_op[u][0:X_MAX, j, qt * P:(qt + 1) * P], kx_op[u][0:X_MAX, j, 0:(qt + 1) * P],
                          start=True, stop=True)
                pe.matmul(bank[:, qt * P:(qt + 1) * P], ident_bf[:], mask_qk[:], start=False, stop=True, skip_group_check=True).then_inc(xs_mm, 1)

            def x_turn_max(t, k):
                i = t * 3 + k
                pe.wait_ge(xs_max, 16 * i + 19)
                if k:
                    pe.wait_ge(xm_lo, i)
                pe.transpose(psum[0:16, 1, 0:P], m_neg[:, k % 3, :], ident[:]).then_inc(xmT_done, 1)

            def x_shifted(t, k, n):
                i, u = t * 3 + k, k % 3
                kt, j = n // 4, n % 4
                if n == 0:
                    pe.wait_ge(xm_loaded[u], 32 * (t + k // 3 + 1))
                bank = psum[:, 4 + n % 2, :]
                pe.wait_ge(xp_ready, 16 * i + n + 1)
                pe.matmul(bank[:, 0:S - kt * P], kx_op[u][:, j, kt * P:(kt + 1) * P], qx_op[u][:, j, kt * P:], start=True, stop=True)
                pe.matmul(bank[:, 0:P], ident_bf[:], mask_kq[:], start=False, stop=True, skip_group_check=True).then_inc(xst_mm, 1)

            def x_sums(t, k, kt, n):
                i = t * 3 + k
                pe.wait_ge(xp_ready, 16 * i + 4 * kt + 6)
                if kt == 0:
                    pe.wait_ge(xv_ready, i + 1)
                    pe.wait_ge(xo_copied, 2 * i + 1 + n)
                for j in range(NQ):
                    w = v_q[k % 3][:, kt, j * 32:(j + 1) * 32] if n else ones32[:]
                    mm = pe.matmul(psum[j * 32:(j + 1) * 32, 7 - n, kt * P:], w, prob_x[kt][:, j, :],
                                   start=(kt == 0), stop=(kt == QT - 1), skip_group_check=True)
                mm.then_inc(xpv_done, 1)

            def x_step(t, k, first=False, last=False):
                for n in range(16):
                    if n < 8 and not last:
                        x_score(t, k + 1, 2 * n)
                        x_score(t, k + 1, 2 * n + 1)
                    x_shifted(t, k, n)
                    if n in (1, 3) and not first:
                        x_sums(t, k - 1, QT - 1, n // 2)
                    if n % 2 == 1 and n > 3:
                        x_sums(t, k, n // 4 - 1, n % 4 // 2)
                    if n == 8 and not last:
                        x_turn_max(t, k + 1)

            for n in range(16):
                x_score(0, 0, n)
            x_turn_max(0, 0)
            run_steps(pe, x_step)
            x_sums(0, XI - 1, QT - 1, 0)
            x_sums(0, XI - 1, QT - 1, 1)

            def products(k, lhs, w, chunks, part):
                for c in part:
                    pe.matmul(psum[:, 2 * k, 0:H + N_AB], lhs[:, c, :], w[:, c, 0:H + N_AB], start=(c == 0), stop=(c == chunks - 1))

            def low_products(k, lhs, w, chunks):
                for c in range(chunks):
                    mm = pe.matmul(psum[0:DR, 2 * k + 1, 0:P], w[:, c, H + N_AB:], lhs[:, c, :], start=(c == 0), stop=(c == chunks - 1))
                mm.then_inc(W["w_mm"][k], 1)

            def deltas(k, i):
                pe.wait_ge(W["low_ready"][k], i + 1)
                pe.matmul(psum[:, 2 * k + 1, H:2 * H], low[k], du[k], start=True, stop=True).then_inc(W["du_mm"][k], 1)

            def dense_products(part):
                for n in part:
                    h, c = n // KC, n % KC
                    pe.matmul(psum[:, 4 + h, :], hT_f[:, c, :], kern[:, c, h * 512:(h + 1) * 512], start=(c == 0), stop=False)

            def round_(i, u, first, second, dense, done):
                if first or second:
                    pe.wait_ge(mlp_ready, i + 1)
                if first:
                    pe.wait_ge(yT_loaded, 16 * i + 16)
                    products(0, yT, write1, 2, range(2))
                    low_products(0, yT, write1, 2)
                if second:
                    pe.wait_ge(W["hn_ready"][1], 2 * i)
                    products(1, mlpT, write2, KC, range(2))
                if first:
                    deltas(0, i)
                if second:
                    products(1, mlpT, write2, KC, range(2, KC))
                if dense:
                    pe.wait_ge(xf_ready, i - 1)
                    turn(6, h_out, KC, fT_mm)
                if second:
                    low_products(1, mlpT, write2, KC)
                if dense:
                    pe.wait_ge(fT_ready, 2 * i - 2)
                    pe.wait_ge(lo_loaded, 32 * i - 32)
                    pe.wait_ge(o_step, i - 1)
                    for c in range(KC):
                        mm = pe.matmul(psum[:, 5, 0:R2], hT_f[:, c, :], lora_at[:, c, :], start=(c == 0), stop=(c == KC - 1))
                    mm.then_inc(ax_mm, 1)
                if second:
                    deltas(1, i - 1)
                if dense:
                    dense_products(range(0, 6))
                if first:
                    pe.wait_ge(W["hn_ready"][0], 2 * i + 2)
                    turn(6, h_mid[u], KC, h2T_mm)
                if dense:
                    wait_apart(pe, (ax_ready, i - 1))
                    pe.transpose(psum[0:R2, 5, P:2 * P], ax, ident[:]).then_inc(axT_mm, 1)
                if dense:
                    dense_products(range(6, 8))
                if first:
                    pe.wait_ge(h2T_ready, 2 * i + 2)
                    for c in range(KC):
                        mm = pe.matmul(psum[:, 6, c * 2 * HC:(c + 1) * 2 * HC], hT[:, c, :], read2[:, c, :], start=True, stop=True)
                    mm.then_inc(y2_mm, 1)
                if dense:
                    pe.wait_ge(axT_ready, i - 1)
                    dense_products(range(8, 12))
                if first:
                    pe.wait_ge(y2n_ready, 2 * i + 2)
                    turn(7, yn, 4, y2T_mm)
                if dense:
                    dense_products(range(12, 13))
                if first:
                    pe.wait_ge(y2T_ready, 4 * i + 4)
                    for n, bank in ((0, 0), (1, 6)):
                        for f in range(KC):
                            for k in range(2):
                                mm = pe.matmul(psum[:, bank + f // 4, (f % 4) * P:(f % 4 + 1) * P], ctx_w[:, n, k, f * P:(f + 1) * P], ynT[:, 2 * n + k, :],
                                               start=(k == 0), stop=(k == 1))
                    mm.then_inc(gu_mm, 1)
                if dense:
                    dense_products(range(13, 16))
                    for h in range(2):
                        mm = pe.matmul(psum[:, 4 + h, :], axT, lora_bt[0:R2, h * 512:(h + 1) * 512], start=False, stop=True)
                    mm.then_inc(f_mm, 1)

            pe.wait_ge(xo_copied, 2 * XI + 2)
            pe.wait_ge(w2_loaded, 16 * 5)
            pe.wait_ge(kern_loaded, 16 * (KC + 2))
            pe.sem_inc(mlp_ready, 1)
            pe.sem_inc(W["hn_ready"][1], 2)
            pe.sem_inc(o_step, 1)
            run_rounds(pe, round_)


def kernel(**inputs):
    import concourse.bacc as bacc
    from concourse.bass_utils import run_bass_kernel_spmd

    nc = bacc.Bacc("TRN2", target_bir_lowering=False, num_devices=1)
    arrays = {"in_" + n: v for n, v in lay_out(inputs).items()}
    dram = {n[3:]: nc.dram_tensor(n, a.shape, mybir.dt.from_np(a.dtype), kind="ExternalInput").ap() for n, a in arrays.items()}
    out = nc.dram_tensor("out", (T, D), F32, kind="ExternalOutput").ap()
    build_program(nc, dram, out)
    r = run_bass_kernel_spmd(nc, [arrays], core_ids=[0])
    return r.results[0]["out"].reshape(B, S, D)


def lay_out(inputs):
    a = {n: np.asarray(v) for n, v in inputs.items()}
    x = "L0_xattn_"
    cat = np.concatenate
    columns = lambda v: v.reshape(-1, P).T
    lay = {}
    lay["x"] = a["x"].reshape(T, D)
    lay["pos"] = a["pos_BxS"].astype(np.int32).reshape(NT, P).T
    lay["wT"] = cat([a[f"L0_attn_{n}_weight"].T for n in "qkvo"], axis=1)
    lay["cols"] = cat([columns(a["L0_attn_q_scale"]), columns(a["L0_attn_k_scale"]),
                       columns(a[x + "attn_read_g"]), columns(a[x + "attn_read_b"]),
                       columns(a[x + "mlp_read_g"]), columns(a[x + "mlp_read_b"])], axis=1)
    lay["rows"] = np.broadcast_to(cat([a[x + "attn_wab_b"], a[x + "mlp_wab_b"],
                                       a[x + "attn_du_b"], a[x + "mlp_du_b"], a["L0_ffn_bias"]])[None], (P, N_ROWS))
    lay["scale_rows"] = np.broadcast_to(cat([a["L0_attn_v_scale"], a["L0_attn_o_scale"]])[None], (P, N_SCALES))
    for name, w in (("read1", a[x + "attn_read_w"]), ("read2", a[x + "mlp_read_w"])):
        n_out = w.shape[1]
        block = np.zeros((KC, HC, C, n_out, HC), np.float32)
        for h in range(HC):
            block[:, h, :, :, h] = w.reshape(KC, HC, n_out, C)[:, h].transpose(0, 2, 1)
        lay[name] = block.reshape(KC, P, n_out * HC).transpose(1, 0, 2)
    lay["wqkv"] = a[x + "qkv_w"].transpose(0, 2, 1).reshape(3, 2, P, H).transpose(2, 0, 1, 3)
    for n, name in ((1, "attn"), (2, "mlp")):
        wod, wab = a[x + name + "_wod_w"], a[x + name + "_wab_w"]
        wT = cat([wod[:H], wab, wod[H:]]).T
        lay[f"write{n}"] = wT.reshape(-1, P, N_W).transpose(1, 0, 2)
        lay[f"du{n}"] = a[x + name + "_du_w"].T
    lay["ctx"] = a["ctx_1024"].transpose(0, 2, 1).reshape(2, 2, P, M).transpose(2, 0, 1, 3)
    lay["kern"] = a["L0_ffn_kernel"].reshape(KC, P, D).transpose(1, 0, 2)
    lay["lora_a"] = a["L0_ffn_lora_A"].reshape(N_LORA, R4, R8, D).transpose(1, 0, 2, 3).reshape(R4, P, D)
    lay["lora_as"] = a["L0_ffn_lora_A_shared"].T.reshape(KC, P, RANK).transpose(1, 0, 2)
    lay["lora_b"] = a["L0_ffn_lora_B"].transpose(0, 2, 1).reshape(R4, P, D)
    lay["lora_bs"] = a["L0_ffn_lora_B_shared"].T
    gate = a["L0_ffn_gate"]
    gate_a = np.zeros((N_LORA, R8, NT, R8), np.float32)
    for r in range(R8):
        gate_a[:, r, :, r] = gate.T
    lay["gate_a"] = gate_a.reshape(P, NT * R8)
    gate_b = np.zeros((N_LORA, RANK, NT, RANK), np.float32)
    for r in range(RANK):
        gate_b[:, r, :, r] = gate.T
    lay["gate_b"] = gate_b.reshape(R4, P, NT * RANK).transpose(1, 0, 2)
    return {n: np.ascontiguousarray(v) for n, v in lay.items()}
```
